# Optimizing a Trainium2 kernel written in Bass

```python
import numpy as np
import jax
import jax.numpy as jnp

def _softmax(x, axis=-1):
    return jax.nn.softmax(x, axis=axis)

def _gelu(x):
    return jax.nn.gelu(x, approximate=True)

def _silu(x):
    return jax.nn.silu(x)

def _sigmoid(x):
    return jax.nn.sigmoid(x)

def _layernorm(x, axis=-1, eps=1e-05):
    m = jnp.mean(x, axis=axis, keepdims=True)
    v = jnp.var(x, axis=axis, keepdims=True)
    return (x - m) / jnp.sqrt(v + eps)

def _scatter_add(tgt, idx, src, axis=0):
    return tgt.at[idx].add(src)

def _segment_sum(src, seg, n):
    return jax.ops.segment_sum(src, seg, n)
kernel_name = 'mk_perceiver_d2_seqx_r8_b15bf7'

def setup_inputs(seed: int=0):
    np.random.seed(seed)
    _w = jnp.asarray

    def _rec_inputs():
        import jax
        import jax.numpy as jnp
        _rk = jax.random.key(seed)
        x = 7.22e-05 + 1 * jax.random.normal(jax.random.fold_in(_rk, 1), (1, 64, 128), jnp.float32)
        _lenS = 64 - jax.random.randint(jax.random.fold_in(_rk, 7), (1,), 0, max(1, 64 // 4) + 1, jnp.int32)
        _lenS2 = 6272 - jax.random.randint(jax.random.fold_in(_rk, 8), (1,), 0, max(1, 6272 // 4) + 1, jnp.int32)
        _ctx_1024P = jax.random.normal(jax.random.fold_in(_rk, 11), (1, 16, 128), jnp.float32)
        _ctx_1024c = jax.random.dirichlet(jax.random.fold_in(_rk, 511), 0.3 * jnp.ones((16,), jnp.float32), (1, 6272))
        _ctx_1024t = jnp.einsum('bsk,bkd->bsd', _ctx_1024c, _ctx_1024P)
        _ctx_1024t = _ctx_1024t * jax.lax.rsqrt(jnp.mean(jnp.square(_ctx_1024t)) + 1e-12) * 0.953939
        ctx_1024 = 4.13588e-05 + 0.999923 * (_ctx_1024t + 0.3 * jax.random.normal(jax.random.fold_in(_rk, 611), (1, 6272, 128), jnp.float32))
        return (x, ctx_1024)
    x, ctx_1024 = _rec_inputs()

    def _L0_xattn_setup():
        import jax, jax.numpy as jnp
        import numpy as np
        D_MODEL = 128
        N_HEADS = 16
        HEAD_DIM = D_MODEL // N_HEADS
        SCALE = HEAD_DIM ** (-0.5)
        key = jax.random.key(seed)
        ks = jax.random.split(key, 11)
        B, L = (4, 256)
        s = 1.0 / np.sqrt(D_MODEL)
        inp = {'queries': jax.random.normal(ks[0], (B, L, D_MODEL), jnp.float32), 'keys': jax.random.normal(ks[1], (B, L, D_MODEL), jnp.float32), 'values': jax.random.normal(ks[2], (B, L, D_MODEL), jnp.float32), 'Wq': jax.random.normal(ks[3], (D_MODEL, D_MODEL), jnp.float32) * s, 'bq': jnp.zeros((D_MODEL,), jnp.float32), 'Wk': jax.random.normal(ks[4], (D_MODEL, D_MODEL), jnp.float32) * s, 'bk': jnp.zeros((D_MODEL,), jnp.float32), 'Wv': jax.random.normal(ks[5], (D_MODEL, D_MODEL), jnp.float32) * s, 'bv': jnp.zeros((D_MODEL,), jnp.float32), 'Wo': jax.random.normal(ks[6], (D_MODEL, D_MODEL), jnp.float32) * s, 'bo': jnp.zeros((D_MODEL,), jnp.float32)}
        return inp
    _L0_xattn_all = _L0_xattn_setup()
    _L0_xattn_in = {k: v for k, v in _L0_xattn_all.items() if k in ('Wq', 'bq', 'Wk', 'bk', 'Wv', 'bv', 'Wo', 'bo')}
    del _L0_xattn_all

    def _L0_attn_setup():
        import jax, jax.numpy as jnp
        import numpy as np
        B, S, E, H, Dh = (2, 256, 128, 16, 64)
        key = jax.random.key(seed)
        ks = jax.random.split(key, 8)
        w = 0.02
        return {'x': jax.random.normal(ks[0], (B, S, E), jnp.float32), 'Wq': jax.random.normal(ks[1], (H, Dh, E), jnp.float32) * w, 'bq': jax.random.normal(ks[2], (H, Dh), jnp.float32) * w, 'Wk': jax.random.normal(ks[3], (H, Dh, E), jnp.float32) * w, 'bk': jax.random.normal(ks[4], (H, Dh), jnp.float32) * w, 'Wv': jax.random.normal(ks[5], (H, Dh, E), jnp.float32) * w, 'bv': jax.random.normal(ks[6], (H, Dh), jnp.float32) * w, 'proj': jax.random.normal(ks[7], (H * Dh, E), jnp.float32) * w}
    _L0_attn_all = _L0_attn_setup()
    _L0_attn_in = {k: v for k, v in _L0_attn_all.items() if k in ('Wq', 'bq', 'Wk', 'bk', 'Wv', 'bv', 'proj')}
    del _L0_attn_all

    def _L0_ffn_setup():
        import jax, jax.numpy as jnp
        import numpy as np
        D = 128
        F = 128
        E = 8
        K = 2
        B, T = (2, 256)

        def _moe_forward(x, router_w, w1, w2, shared_gate_up, shared_down, shared_gate_w):
            b, t, d = x.shape
            xf = x.reshape(-1, d)
            n = xf.shape[0]
            logits = xf @ router_w
            probs = jax.nn.softmax(logits, axis=-1)
            topw, topi = jax.lax.top_k(probs, K)
            combine = jnp.zeros((n, E), dtype=probs.dtype).at[jnp.arange(n)[:, None], topi].add(topw)
            h = jax.nn.silu(jnp.einsum('nd,edf->nef', xf, w1))
            ye = jnp.einsum('nef,efd->ned', h, w2)
            routed = jnp.einsum('ne,ned->nd', combine, ye)
            gu = xf @ shared_gate_up
            gate, up = (gu[:, :F], gu[:, F:])
            shared = jax.nn.silu(gate) * up @ shared_down
            shared = jax.nn.sigmoid(xf @ shared_gate_w) * shared
            return (routed + shared).reshape(b, t, d)
        key = jax.random.key(seed)
        ks = jax.random.split(key, 7)
        std = 0.02
        x = jax.random.normal(ks[0], (B, T, D), dtype=jnp.float32)
        router_w = jax.random.normal(ks[1], (D, E), dtype=jnp.float32) * std
        w1 = jax.random.normal(ks[2], (E, D, F), dtype=jnp.float32) * std
        w2 = jax.random.normal(ks[3], (E, F, D), dtype=jnp.float32) * std
        shared_gate_up = jax.random.normal(ks[4], (D, 2 * F), dtype=jnp.float32) * std
        shared_down = jax.random.normal(ks[5], (F, D), dtype=jnp.float32) * std
        shared_gate_w = jax.random.normal(ks[6], (D, 1), dtype=jnp.float32) * std
        return {'x': x, 'router_w': router_w, 'w1': w1, 'w2': w2, 'shared_gate_up': shared_gate_up, 'shared_down': shared_down, 'shared_gate_w': shared_gate_w}
    _L0_ffn_all = _L0_ffn_setup()
    _L0_ffn_in = {k: v for k, v in _L0_ffn_all.items() if k in ('router_w', 'w1', 'w2', 'shared_gate_up', 'shared_down', 'shared_gate_w')}
    del _L0_ffn_all

    def _L1_xattn_setup():
        import jax, jax.numpy as jnp
        import numpy as np
        E = 128
        KD = 128
        H = 16
        DH = E // H
        EPS = 1e-05

        def layernorm(x, gamma, beta):
            mu = jnp.mean(x, axis=-1, keepdims=True)
            var = jnp.mean(jnp.square(x - mu), axis=-1, keepdims=True)
            return (x - mu) * jax.lax.rsqrt(var + EPS) * gamma + beta
        key = jax.random.key(seed)
        ks = jax.random.split(key, 16)
        B, QN, KN = (4, 128, 256)
        s_q = 1.0 / np.sqrt(E)
        s_k = 1.0 / np.sqrt(KD)
        return {'q': jax.random.normal(ks[0], (B, QN, E), jnp.float32), 'k': jax.random.normal(ks[1], (B, KN, KD), jnp.float32), 'v': jax.random.normal(ks[2], (B, KN, KD), jnp.float32), 'Wq': jax.random.uniform(ks[3], (E, E), jnp.float32, -s_q, s_q), 'bq': jax.random.uniform(ks[4], (E,), jnp.float32, -s_q, s_q), 'Wk': jax.random.uniform(ks[5], (E, KD), jnp.float32, -s_k, s_k), 'bk': jax.random.uniform(ks[6], (E,), jnp.float32, -s_k, s_k), 'Wv': jax.random.uniform(ks[7], (E, KD), jnp.float32, -s_k, s_k), 'bv': jax.random.uniform(ks[8], (E,), jnp.float32, -s_k, s_k), 'Wp': jax.random.uniform(ks[9], (E, E), jnp.float32, -s_q, s_q), 'bp': jax.random.uniform(ks[10], (E,), jnp.float32, -s_q, s_q), 'q_gamma': jnp.ones((DH,), jnp.float32), 'q_beta': jnp.zeros((DH,), jnp.float32), 'k_gamma': jnp.ones((DH,), jnp.float32), 'k_beta': jnp.zeros((DH,), jnp.float32)}
    _L1_xattn_all = _L1_xattn_setup()
    _L1_xattn_in = {k: v for k, v in _L1_xattn_all.items() if k in ('Wq', 'bq', 'Wk', 'bk', 'Wv', 'bv', 'Wp', 'bp', 'q_gamma', 'q_beta', 'k_gamma', 'k_beta')}
    del _L1_xattn_all

    def _L1_attn_setup():
        import jax, jax.numpy as jnp
        import numpy as np
        DIM = 128
        HEADS = 16
        HEAD_DIM = DIM // HEADS

        def apply_rope(x):
            B, S, H, D = x.shape
            half = D // 2
            freqs = 1.0 / 10000.0 ** (jnp.arange(half, dtype=jnp.float32) / half)
            pos = jnp.arange(S, dtype=jnp.float32)
            angles = pos[:, None] * freqs[None, :]
            sin = jnp.sin(angles)[None, :, None, :]
            cos = jnp.cos(angles)[None, :, None, :]
            x1, x2 = (x[..., :half], x[..., half:])
            return jnp.concatenate([x1 * cos - x2 * sin, x1 * sin + x2 * cos], axis=-1)
        key = jax.random.key(seed)
        ks = jax.random.split(key, 5)
        x = jax.random.normal(ks[0], (2, 256, DIM), dtype=jnp.float32)
        s = 1.0 / np.sqrt(DIM)
        qkv_w = jax.random.uniform(ks[1], (3 * DIM, DIM), minval=-s, maxval=s, dtype=jnp.float32)
        qkv_b = jax.random.uniform(ks[2], (3 * DIM,), minval=-s, maxval=s, dtype=jnp.float32)
        proj_w = jax.random.uniform(ks[3], (DIM, DIM), minval=-s, maxval=s, dtype=jnp.float32)
        proj_b = jax.random.uniform(ks[4], (DIM,), minval=-s, maxval=s, dtype=jnp.float32)
        return {'x': x, 'qkv_w': qkv_w, 'qkv_b': qkv_b, 'proj_w': proj_w, 'proj_b': proj_b}
    _L1_attn_all = _L1_attn_setup()
    _L1_attn_in = {k: v for k, v in _L1_attn_all.items() if k in ('qkv_w', 'qkv_b', 'proj_w', 'proj_b')}
    del _L1_attn_all

    def _L1_ffn_setup():
        import jax, jax.numpy as jnp
        import numpy as np
        H = 128
        I = 256
        E = 32
        B, S = (4, 256)

        def _grouped_mm(a, w, group_sizes):
            return jax.lax.ragged_dot(a, w, group_sizes)

        def _swiglu(x, gw, uw, dw):
            return jax.nn.silu(x @ gw) * (x @ uw) @ dw
        key = jax.random.key(seed)
        ks = jax.random.split(key, 8)
        scale = 0.02
        inp = {'hidden_states': jax.random.normal(ks[0], (B, S, H), dtype=jnp.float32), 'gate_w': jax.random.normal(ks[1], (H, E), dtype=jnp.float32) * scale, 'shared_gate_w': jax.random.normal(ks[2], (H, I), dtype=jnp.float32) * scale, 'shared_up_w': jax.random.normal(ks[3], (H, I), dtype=jnp.float32) * scale, 'shared_down_w': jax.random.normal(ks[4], (I, H), dtype=jnp.float32) * scale, 'routed_gate_w': jax.random.normal(ks[5], (E, H, I), dtype=jnp.float32) * scale, 'routed_up_w': jax.random.normal(ks[6], (E, H, I), dtype=jnp.float32) * scale, 'routed_down_w': jax.random.normal(ks[7], (E, I, H), dtype=jnp.float32) * scale}
        return inp
    _L1_ffn_all = _L1_ffn_setup()
    _L1_ffn_in = {k: v for k, v in _L1_ffn_all.items() if k in ('gate_w', 'shared_gate_w', 'shared_up_w', 'shared_down_w', 'routed_gate_w', 'routed_up_w', 'routed_down_w')}
    del _L1_ffn_all
    return {'x': x, 'ctx_1024': ctx_1024, 'L0_xattn_Wq': _L0_xattn_in['Wq'], 'L0_xattn_bq': _L0_xattn_in['bq'], 'L0_xattn_Wk': _L0_xattn_in['Wk'], 'L0_xattn_bk': _L0_xattn_in['bk'], 'L0_xattn_Wv': _L0_xattn_in['Wv'], 'L0_xattn_bv': _L0_xattn_in['bv'], 'L0_xattn_Wo': _L0_xattn_in['Wo'], 'L0_xattn_bo': _L0_xattn_in['bo'], 'L0_attn_Wq': _L0_attn_in['Wq'], 'L0_attn_bq': _L0_attn_in['bq'], 'L0_attn_Wk': _L0_attn_in['Wk'], 'L0_attn_bk': _L0_attn_in['bk'], 'L0_attn_Wv': _L0_attn_in['Wv'], 'L0_attn_bv': _L0_attn_in['bv'], 'L0_attn_proj': _L0_attn_in['proj'], 'L0_ffn_router_w': _L0_ffn_in['router_w'], 'L0_ffn_w1': _L0_ffn_in['w1'], 'L0_ffn_w2': _L0_ffn_in['w2'], 'L0_ffn_shared_gate_up': _L0_ffn_in['shared_gate_up'], 'L0_ffn_shared_down': _L0_ffn_in['shared_down'], 'L0_ffn_shared_gate_w': _L0_ffn_in['shared_gate_w'], 'L1_xattn_Wq': _L1_xattn_in['Wq'], 'L1_xattn_bq': _L1_xattn_in['bq'], 'L1_xattn_Wk': _L1_xattn_in['Wk'], 'L1_xattn_bk': _L1_xattn_in['bk'], 'L1_xattn_Wv': _L1_xattn_in['Wv'], 'L1_xattn_bv': _L1_xattn_in['bv'], 'L1_xattn_Wp': _L1_xattn_in['Wp'], 'L1_xattn_bp': _L1_xattn_in['bp'], 'L1_xattn_q_gamma': _L1_xattn_in['q_gamma'], 'L1_xattn_q_beta': _L1_xattn_in['q_beta'], 'L1_xattn_k_gamma': _L1_xattn_in['k_gamma'], 'L1_xattn_k_beta': _L1_xattn_in['k_beta'], 'L1_attn_qkv_w': _L1_attn_in['qkv_w'], 'L1_attn_qkv_b': _L1_attn_in['qkv_b'], 'L1_attn_proj_w': _L1_attn_in['proj_w'], 'L1_attn_proj_b': _L1_attn_in['proj_b'], 'L1_ffn_gate_w': _L1_ffn_in['gate_w'], 'L1_ffn_shared_gate_w': _L1_ffn_in['shared_gate_w'], 'L1_ffn_shared_up_w': _L1_ffn_in['shared_up_w'], 'L1_ffn_shared_down_w': _L1_ffn_in['shared_down_w'], 'L1_ffn_routed_gate_w': _L1_ffn_in['routed_gate_w'], 'L1_ffn_routed_up_w': _L1_ffn_in['routed_up_w'], 'L1_ffn_routed_down_w': _L1_ffn_in['routed_down_w']}

def reference(x, ctx_1024, L0_xattn_Wq, L0_xattn_bq, L0_xattn_Wk, L0_xattn_bk, L0_xattn_Wv, L0_xattn_bv, L0_xattn_Wo, L0_xattn_bo, L0_attn_Wq, L0_attn_bq, L0_attn_Wk, L0_attn_bk, L0_attn_Wv, L0_attn_bv, L0_attn_proj, L0_ffn_router_w, L0_ffn_w1, L0_ffn_w2, L0_ffn_shared_gate_up, L0_ffn_shared_down, L0_ffn_shared_gate_w, L1_xattn_Wq, L1_xattn_bq, L1_xattn_Wk, L1_xattn_bk, L1_xattn_Wv, L1_xattn_bv, L1_xattn_Wp, L1_xattn_bp, L1_xattn_q_gamma, L1_xattn_q_beta, L1_xattn_k_gamma, L1_xattn_k_beta, L1_attn_qkv_w, L1_attn_qkv_b, L1_attn_proj_w, L1_attn_proj_b, L1_ffn_gate_w, L1_ffn_shared_gate_w, L1_ffn_shared_up_w, L1_ffn_shared_down_w, L1_ffn_routed_gate_w, L1_ffn_routed_up_w, L1_ffn_routed_down_w):
    import jax
    import jax.numpy as jnp

    def _L0_xattn_ref(queries, keys, values, Wq, bq, Wk, bk, Wv, bv, Wo, bo):
        import jax, jax.numpy as jnp
        import numpy as np
        D_MODEL = 128
        N_HEADS = 16
        HEAD_DIM = D_MODEL // N_HEADS
        SCALE = HEAD_DIM ** (-0.5)
        B, L, _ = queries.shape
        S = keys.shape[1]
        q = (queries @ Wq + bq).reshape(B, L, N_HEADS, HEAD_DIM).transpose(0, 2, 1, 3)
        k = (keys @ Wk + bk).reshape(B, S, N_HEADS, HEAD_DIM).transpose(0, 2, 1, 3)
        v = (values @ Wv + bv).reshape(B, S, N_HEADS, HEAD_DIM).transpose(0, 2, 1, 3)
        scores = jnp.einsum('bhld,bhsd->bhls', q, k) * SCALE
        weights = jax.nn.softmax(scores, axis=-1)
        out = jnp.einsum('bhls,bhsd->bhld', weights, v)
        out = out.transpose(0, 2, 1, 3).reshape(B, L, D_MODEL)
        out = out @ Wo + bo
        return out

    def _L0_attn_ref(x, Wq, bq, Wk, bk, Wv, bv, proj):
        import jax, jax.numpy as jnp
        import numpy as np
        B, S, E, H, Dh = (2, 256, 128, 16, 64)
        b, s, e = x.shape
        h, dh, _ = Wq.shape
        scale = jnp.sqrt(jnp.asarray(dh, x.dtype))
        q = jnp.einsum('bse,hde->bhsd', x, Wq) + bq[None, :, None, :]
        k = jnp.einsum('bse,hde->bhsd', x, Wk) + bk[None, :, None, :]
        v = jnp.einsum('bse,hde->bhsd', x, Wv) + bv[None, :, None, :]
        causal = jnp.triu(jnp.ones((s, s), bool), 1)
        scores = jnp.einsum('bhsd,bhtd->bhst', q, k) / scale
        scores = jnp.where(causal[None, None], -jnp.inf, scores)
        att = jax.nn.softmax(scores, axis=-1) / scale
        z = jnp.einsum('bhst,bhtd->bhsd', att, v)
        z = z.reshape(b, s, h * dh)
        return z @ proj

    def _L0_ffn_ref(x, router_w, w1, w2, shared_gate_up, shared_down, shared_gate_w):
        import jax, jax.numpy as jnp
        import numpy as np
        D = 128
        F = 128
        E = 8
        K = 2
        B, T = (2, 256)

        def _moe_forward(x, router_w, w1, w2, shared_gate_up, shared_down, shared_gate_w):
            b, t, d = x.shape
            xf = x.reshape(-1, d)
            n = xf.shape[0]
            logits = xf @ router_w
            probs = jax.nn.softmax(logits, axis=-1)
            topw, topi = jax.lax.top_k(probs, K)
            combine = jnp.zeros((n, E), dtype=probs.dtype).at[jnp.arange(n)[:, None], topi].add(topw)
            h = jax.nn.silu(jnp.einsum('nd,edf->nef', xf, w1))
            ye = jnp.einsum('nef,efd->ned', h, w2)
            routed = jnp.einsum('ne,ned->nd', combine, ye)
            gu = xf @ shared_gate_up
            gate, up = (gu[:, :F], gu[:, F:])
            shared = jax.nn.silu(gate) * up @ shared_down
            shared = jax.nn.sigmoid(xf @ shared_gate_w) * shared
            return (routed + shared).reshape(b, t, d)
        return _moe_forward(x, router_w, w1, w2, shared_gate_up, shared_down, shared_gate_w)

    def _L1_xattn_ref(q, k, v, Wq, bq, Wk, bk, Wv, bv, Wp, bp, q_gamma, q_beta, k_gamma, k_beta):
        import jax, jax.numpy as jnp
        import numpy as np
        E = 128
        KD = 128
        H = 16
        DH = E // H
        EPS = 1e-05

        def layernorm(x, gamma, beta):
            mu = jnp.mean(x, axis=-1, keepdims=True)
            var = jnp.mean(jnp.square(x - mu), axis=-1, keepdims=True)
            return (x - mu) * jax.lax.rsqrt(var + EPS) * gamma + beta
        B, QN, _ = q.shape
        KN = k.shape[1]
        scale = DH ** (-0.5)
        qh = (q @ Wq.T + bq).reshape(B, QN, H, DH).transpose(0, 2, 1, 3)
        kh = (k @ Wk.T + bk).reshape(B, KN, H, DH).transpose(0, 2, 1, 3)
        vh = (v @ Wv.T + bv).reshape(B, KN, H, DH).transpose(0, 2, 1, 3)
        qh = layernorm(qh, q_gamma, q_beta) * scale
        kh = layernorm(kh, k_gamma, k_beta)
        attn = jax.nn.softmax(jnp.einsum('bhqd,bhkd->bhqk', qh, kh), axis=-1)
        x = jnp.einsum('bhqk,bhkd->bhqd', attn, vh)
        x = x.transpose(0, 2, 1, 3).reshape(B, QN, E)
        return x @ Wp.T + bp

    def _L1_attn_ref(x, qkv_w, qkv_b, proj_w, proj_b):
        import jax, jax.numpy as jnp
        import numpy as np
        DIM = 128
        HEADS = 16
        HEAD_DIM = DIM // HEADS

        def apply_rope(x):
            B, S, H, D = x.shape
            half = D // 2
            freqs = 1.0 / 10000.0 ** (jnp.arange(half, dtype=jnp.float32) / half)
            pos = jnp.arange(S, dtype=jnp.float32)
            angles = pos[:, None] * freqs[None, :]
            sin = jnp.sin(angles)[None, :, None, :]
            cos = jnp.cos(angles)[None, :, None, :]
            x1, x2 = (x[..., :half], x[..., half:])
            return jnp.concatenate([x1 * cos - x2 * sin, x1 * sin + x2 * cos], axis=-1)
        B, S, D = x.shape
        qkv = x @ qkv_w.T + qkv_b
        q, k, v = jnp.split(qkv, 3, axis=-1)
        q = q.reshape(B, S, HEADS, HEAD_DIM)
        k = k.reshape(B, S, HEADS, HEAD_DIM)
        v = v.reshape(B, S, HEADS, HEAD_DIM)
        q = apply_rope(q)
        k = apply_rope(k)
        scale = 1.0 / np.sqrt(HEAD_DIM)
        attn = jnp.einsum('bqhd,bkhd->bhqk', q, k) * scale
        mask = jnp.triu(jnp.ones((S, S), dtype=bool), k=1)
        attn = jnp.where(mask[None, None], -1000000000.0, attn)
        attn = jax.nn.softmax(attn, axis=-1)
        out = jnp.einsum('bhqk,bkhd->bqhd', attn, v).reshape(B, S, D)
        return out @ proj_w.T + proj_b

    def _L1_ffn_ref(hidden_states, gate_w, shared_gate_w, shared_up_w, shared_down_w, routed_gate_w, routed_up_w, routed_down_w):
        import jax, jax.numpy as jnp
        import numpy as np
        H = 128
        I = 256
        E = 32
        B, S = (4, 256)

        def _grouped_mm(a, w, group_sizes):
            return jax.lax.ragged_dot(a, w, group_sizes)

        def _swiglu(x, gw, uw, dw):
            return jax.nn.silu(x @ gw) * (x @ uw) @ dw
        b, s, h = hidden_states.shape
        x = hidden_states.reshape(-1, h)
        shared_out = _swiglu(x, shared_gate_w, shared_up_w, shared_down_w)
        logits = x @ gate_w
        topk_ids = jnp.argmax(logits, axis=-1)
        topk_val = jnp.max(logits, axis=-1)
        scores = jax.nn.sigmoid(topk_val)[:, None]
        xs = x * scores
        tokens_per_expert = jnp.zeros((E,), jnp.int32).at[topk_ids].add(1)
        order = jnp.argsort(topk_ids)
        sorted_x = xs[order]
        g = _grouped_mm(sorted_x, routed_gate_w, tokens_per_expert)
        u = _grouped_mm(sorted_x, routed_up_w, tokens_per_expert)
        d = _grouped_mm(jax.nn.silu(g) * u, routed_down_w, tokens_per_expert)
        inv = jnp.argsort(order)
        routed_out = d[inv]
        return (shared_out + routed_out).reshape(b, s, h)
    x = x + _L0_xattn_ref(_layernorm(x, axis=-1), ctx_1024, ctx_1024, L0_xattn_Wq, L0_xattn_bq, L0_xattn_Wk, L0_xattn_bk, L0_xattn_Wv, L0_xattn_bv, L0_xattn_Wo, L0_xattn_bo)
    x = x + _L0_attn_ref(_layernorm(x, axis=-1), L0_attn_Wq, L0_attn_bq, L0_attn_Wk, L0_attn_bk, L0_attn_Wv, L0_attn_bv, L0_attn_proj)
    x = x + _L0_ffn_ref(_layernorm(x, axis=-1), L0_ffn_router_w, L0_ffn_w1, L0_ffn_w2, L0_ffn_shared_gate_up, L0_ffn_shared_down, L0_ffn_shared_gate_w)
    x = x + _L1_xattn_ref(_layernorm(x, axis=-1), ctx_1024, ctx_1024, L1_xattn_Wq, L1_xattn_bq, L1_xattn_Wk, L1_xattn_bk, L1_xattn_Wv, L1_xattn_bv, L1_xattn_Wp, L1_xattn_bp, L1_xattn_q_gamma, L1_xattn_q_beta, L1_xattn_k_gamma, L1_xattn_k_beta)
    x = x + _L1_attn_ref(_layernorm(x, axis=-1), L1_attn_qkv_w, L1_attn_qkv_b, L1_attn_proj_w, L1_attn_proj_b)
    x = x + _L1_ffn_ref(_layernorm(x, axis=-1), L1_ffn_gate_w, L1_ffn_shared_gate_w, L1_ffn_shared_up_w, L1_ffn_shared_down_w, L1_ffn_routed_gate_w, L1_ffn_routed_up_w, L1_ffn_routed_down_w)
    return x

_drawn_inputs = setup_inputs


def setup_inputs(seed=0):
    import zlib

    import numpy as np

    out = dict(_drawn_inputs(seed))
    spreads = {'L0_xattn_bq': (0.0, 0.343),
     'L0_xattn_bk': (0.0, 0.8),
     'L0_xattn_bv': (0.0, 0.1),
     'L0_xattn_bo': (0.0, 0.1),
     'L1_xattn_q_gamma': (1.0, 0.6),
     'L1_xattn_q_beta': (0.0, 0.8),
     'L1_xattn_k_gamma': (1.0, 0.6),
     'L1_xattn_k_beta': (0.0, 0.8)}
    factors = {'L0_attn_Wq': 8.0,
     'L0_attn_bq': 8.0,
     'L0_attn_Wk': 8.0,
     'L0_attn_bk': 8.0,
     'L0_attn_Wv': 7.251,
     'L0_attn_bv': 8.0,
     'L0_attn_proj': 7.287,
     'L0_ffn_router_w': 8.0,
     'L0_ffn_w1': 8.0,
     'L0_ffn_w2': 8.0,
     'L0_ffn_shared_gate_up': 8.0,
     'L0_ffn_shared_down': 8.0,
     'L0_ffn_shared_gate_w': 8.0,
     'L1_xattn_bq': 7.629,
     'L1_xattn_bk': 8.0,
     'L1_ffn_gate_w': 8.0,
     'L1_ffn_shared_gate_w': 7.646,
     'L1_ffn_shared_up_w': 7.488,
     'L1_ffn_shared_down_w': 7.815,
     'L1_ffn_routed_gate_w': 8.0,
     'L1_ffn_routed_up_w': 8.0,
     'L1_ffn_routed_down_w': 8.0}
    for name, (base, spread) in spreads.items():
        noise = np.random.default_rng([zlib.crc32(name.encode()), seed]).standard_normal(out[name].shape)
        drawn = base * np.exp(spread * noise) if base else spread * noise
        out[name] = jnp.asarray(drawn.astype(out[name].dtype))
    for name, factor in factors.items():
        out[name] = (out[name] * factor).astype(out[name].dtype)
    return out
```

```python
from contextlib import ExitStack

import numpy as np

import concourse.bass as bass
from concourse import mybir

F32 = mybir.dt.float32
F32R = mybir.dt.float32r
U32 = mybir.dt.uint32
ALU = mybir.AluOpType
ACT = mybir.ActivationFunctionType
AX = mybir.AxisListType.X

P = 128
T = 64
D = 128
S = 6272
H = 16
DH = D // H
NG = 4
HG = H // NG
GC = HG * DH
GQ = HG * T
NT = S // P
BT = 4
NB = -(-NT // BT)
CW = BT * P
AUG = DH + 1
SH = 16
SD = 64
NP_ = SH // 2
E0, E1 = 8, 32
F0, F1 = 128, 256
EW = 3 * F1
EPS = 1e-5
XSCALE = DH ** -0.5
QROWS = 3 * GC
KROWS = QROWS + 2
KC = [(0, 3), (3, 6), (6, 9), (9, NB)]
CTX_PIECES = [0, 512, 1536, 3072, 4608, S]
MAXN = 2 * NB
MAX_LAST = NB - 3


def width(c):
    return min(CW, S - c * CW)


def tiles(i):
    return min(BT, NT - i * BT)


def max_schedule(i):
    n = MAX_LAST + 1
    return range(-(-MAXN * min(i, n) // n), -(-MAXN * min(i + 1, n) // n))


EARLY = [("wk0", P, D), ("wv0", P, D), ("bk0", P, 1), ("wq0x3", P, NG * QROWS), ("bq0x3", QROWS, NG), ("wo0", P, D)]
LATE = [("wqa", P, SH * SD), ("wka", P, SH * SD), ("wva", P, SH * SD), ("proja", P, NP_ * D),
        ("bqa", P, NP_), ("bka", P, NP_), ("bva", P, SH),
        ("w1", P, (E0 + 2) * F0), ("w2", P, E0 * D), ("sdown0", P, D), ("router0", P, E0 + 1)]
CONST = [("ident", P, P), ("avg", P, P), ("sel", P, 2 * AUG), ("fold", P, T), ("hmask", QROWS, HG),
         ("headmask", P, H), ("causal", P, T), ("iota", P, E1), ("cos", T, DH), ("sin", T, DH),
         ("qgb", QROWS, 2), ("kgb", P, 2)]
ROWS = [("x", T, D), ("bv0", T, D), ("bo0", T, D), ("bv1", T, D), ("bp1", T, D), ("bproj1", T, D), ("bqkv1", T, 3 * D)]
SMALL1 = [("wv1", P, D), ("wp1", P, D), ("wproj1", P, D), ("gate1", P, E1)]
RAW1 = [("wk1", P, D), ("wq1", P, D), ("cen", P, P), ("cen3", P, NG * QROWS), ("bk1", P, 1), ("bq1x3", QROWS, NG)]
TAIL1 = [("wqkv1", P, 3 * D), ("sgu1", P, 2 * F1), ("sdown1", P, 2 * D)]
PACKS = {"early": EARLY, "late": LATE, "const": CONST, "rows": ROWS, "small1": SMALL1, "raw1": RAW1, "tail1": TAIL1}


def words(pack):
    return sum(w for _, _, w in PACKS[pack])


NEAR = (3 * S - words("tail1")) // EW
assert (E1 - NEAR) * EW <= words("early") + words("late")


def perceiver(nc, ctxT, packs, experts, out):
    with ExitStack() as ctx:
        def sb(name, shape, dt=F32):
            return ctx.enter_context(nc.sbuf_tensor(name, shape, dt))

        def sem(name):
            return ctx.enter_context(nc.semaphore(name))

        ps = ctx.enter_context(nc.psum_tensor("ps", [P, 8, 512], F32))

        arena = sb("arena", [P, 3 * S])
        ctx_sb, khi, klo = arena[:, 0:S], arena[:, S:2 * S], arena[:, 2 * S:3 * S]
        kst = sb("kst", [P, 2, S], F32R)
        qst = sb("qst", [P, NG, GQ], F32R)
        vaug = sb("vaug", [P, NT, H, AUG])
        prob = sb("prob", [P, 2, BT * GQ])
        w0 = sb("w0", [P, words("early") + words("late")])
        consts = sb("consts", [P, words("const")])
        rows = sb("rows", [T, words("rows")])
        small1 = sb("small1", [P, words("small1")])
        wk1c = sb("wk1c", [P, D])
        wq1c = sb("wq1c", [P, NG * QROWS])
        bk1c = sb("bk1c", [P, 1])
        bq1c = sb("bq1c", [P, NG])
        scratch = sb("scratch", [P, 1024])
        y = sb("y", [T, D])
        yT = sb("yT", [P, T])
        attT = sb("attT", [P, T])
        avsb = sb("avsb", [P, GQ])
        eps_col = sb("eps_col", [P, 1])
        mx = sb("mx", [P, 2, NB])
        mneg = sb("mneg", [P, 2])
        mhl = sb("mhl", [P, 2, 2])
        st6 = sb("st6", [T, 6])
        mv = sb("mv", [T, 2])
        lnv = sb("lnv", [T, 1])
        rstd = sb("rstd", [T, 1])
        stat = sb("stat", [P, 4 * 16])
        idx8 = sb("idx8", [T, 8], U32)

        view = {}
        base = {"early": (w0, 0), "late": (w0, words("early")), "const": (consts, 0), "rows": (rows, 0),
                "small1": (small1, 0), "raw1": (prob.rearrange("p a b -> p (a b)"), 0),
                "tail1": (arena, NEAR * EW)}
        for pack, items in PACKS.items():
            t, at = base[pack]
            for name, r, w in items:
                view[name] = t[0:r, at:at + w]
                at += w
        ident = view["ident"]
        x = view["x"]
        flat = prob.rearrange("p a b -> p (a b)")

        q_a, q_b = scratch[:, 0:256], scratch[:, 256:512]
        sa_q, sa_k, sa_s = flat[:, 0:1024], flat[:, 1024:1536], flat[:, 1536:2048]
        sa_pT, sa_v = flat[:, 0:1024], scratch[:, 0:1024]
        s1_qkv, s1_r = scratch[0:T, 0:3 * D], scratch[0:T, 3 * D:7 * D]
        f0_sig, f0_h = flat[:, 0:(E0 + 1) * T], flat[:, (E0 + 1) * T:2 * (E0 + 1) * T]
        vflat = vaug.rearrange("p t h a -> p (t h a)")
        f1_mask, f1_x, f1_h1 = (vflat[:, k * E1 * T:(k + 1) * E1 * T].rearrange("p (e q) -> p e q", e=E1) for k in range(3))
        f1_he = (f1_x, f1_h1)
        f1_gu, f1_sig, f1_h, f1_hT = flat[:, 0:512], flat[:, 512:768], flat[:, 768:1024], flat[:, 1024:1280]
        y2 = flat[:, 1280:1408]
        f1_bc = flat[0:T, 1408:1664].rearrange("p (k c) -> p k c", k=2)

        def expert(e):
            return arena[:, e * EW:(e + 1) * EW] if e < NEAR else w0[:, (e - NEAR) * EW:(e - NEAR + 1) * EW]

        in_pack = {n: sem("in_" + n) for n in PACKS}
        in_ctx = [sem(f"in_ctx{i}") for i in range(len(CTX_PIECES) - 1)]
        in_stack = [[sem(f"in_stack{s}{k}") for k in range(len(KC))] for s in range(2)]
        in_exp = [sem(f"in_exp{i}") for i in range(3)]
        zeroed = sem("zeroed")
        v_ones = sem("v_ones")
        ones_set = sem("ones_set")
        k_proj = sem("k_proj")
        k_full = sem("k_full")
        k_split = sem("k_split")
        k_sq = sem("k_sq")
        k_var = sem("k_var")
        k_rstd = sem("k_rstd")
        k_aff = sem("k_aff")
        v_proj = sem("v_proj")
        v_set = sem("v_set")
        q_ready = sem("q_ready")
        max_made = sem("max_made")
        max_read = sem("max_read")
        shift_cols = sem("shift_cols")
        shift_rows = sem("shift_rows")
        shift_ready = sem("shift_ready")
        scores_done = sem("scores_done")
        exp_done = sem("exp_done")
        av_done = sem("av_done")
        acc_copied = sem("acc_copied")
        o_ready = sem("o_ready")
        dve_step = sem("dve_step")
        act_step = sem("act_step")
        out_stored = sem("out_stored")
        once = {}

        def ev(name):
            if name not in once:
                once[name] = sem(name)
            return once[name]

        block = ctx.enter_context(nc.Block())

        @block.sync
        def _(sp):
            def load(pack):
                t, at = base[pack]
                rmax = max(r for _, r, _ in PACKS[pack])
                sp.dma_start(t[0:rmax, at:at + words(pack)], packs[pack][0:rmax, :]).then_inc(in_pack[pack], 16)

            def stack(l, g, k):
                G = NG * l + g
                b0, b1 = KC[k]
                a, b = b0 * CW, min(b1 * CW, S)
                sp.wait_ge(k_split, l * NB + min(b1, NB))
                if G >= 2:
                    sp.wait_ge(scores_done, NB * (G - 2) + b1)
                for r, src in ((0, khi), (1, khi), (2, klo)):
                    sp.dma_start(kst[r * GC:(r + 1) * GC, G % 2, a:b].bitcast(F32),
                                 src[g * GC:(g + 1) * GC, a:b]).then_inc(in_stack[G % 2][k], 16)

            def load_experts(i, e0, e1):
                t, at = (arena, e0 * EW) if e0 < NEAR else (w0, (e0 - NEAR) * EW)
                sp.dma_start(t[:, at:at + (e1 - e0) * EW], experts[:, e0 * EW:e1 * EW]).then_inc(in_exp[i], 16)

            def ctx_piece(i):
                a, b = CTX_PIECES[i], CTX_PIECES[i + 1]
                sp.dma_start(ctx_sb[:, a:b], ctxT[:, a:b]).then_inc(in_ctx[i], 16)

            load("early")
            ctx_piece(0)
            load("rows")
            load("const")
            for i in range(1, len(in_ctx)):
                ctx_piece(i)
            load("raw1")
            load("small1")
            for k in range(len(KC)):
                stack(0, 0, k)
                stack(0, 1, k)
            load("late")
            for g in (2, 3):
                for k in range(len(KC)):
                    stack(0, g, k)
            for k in range(len(KC)):
                stack(1, 0, k)
                stack(1, 1, k)
            sp.wait_ge(ev("ffn0_y"), 1)
            load_experts(1, NEAR, E1)
            sp.wait_ge(v_set, 2 * NB)
            first = S // EW
            load_experts(0, 0, first)
            for g in (2, 3):
                for k in range(len(KC)):
                    stack(1, g, k)
            for s in range(2):
                for k in range(len(KC)):
                    sp.wait_ge(in_stack[s][k], 48 * 4)
            load("tail1")
            load_experts(2, first, NEAR)
            sp.wait_ge(ev("out_ready"), 1)
            sp.dma_start(out, x).then_inc(out_stored, 16)
            sp.wait_ge(out_stored, 16)

        @block.gpsimd
        def _(pool):
            nc.gpsimd.memset(vaug[:, :, :, DH], 1.0).then_inc(v_ones, 1)
            pool.wait_ge(v_ones, 1)

            def split(l):
                for c in range(NB):
                    a, b = c * CW, c * CW + width(c)
                    pool.wait_ge(k_full, l * NB + c + 1)
                    nc.gpsimd.tensor_tensor(klo[:, a:b], klo[:, a:b], khi[:, a:b], ALU.subtract).then_inc(k_split, 1)

            split(0)
            pool.wait_ge(av_done, NG * NB)
            nc.gpsimd.memset(flat[:, 0:1024], 0.0).then_inc(ev("qbd_zero"), 1)
            split(1)

        @block.scalar
        def _(act):
            n = [0]

            def link(ins):
                n[0] += 1
                ins.then_inc(act_step, 1)
                act.wait_ge(act_step, n[0])

            nc.scalar.preload_act_table_set("natural_log_exp_and_others")

            def v_out(l, c):
                k = tiles(c)
                act.wait_ge(v_proj, l * NB + c + 1)
                nc.scalar.activation(vaug[:, BT * c:BT * c + k, :, 0:DH],
                                     ps[:, 2 + c % 2, 0:k * D].rearrange("p (t h d) -> p t h d", t=k, h=H),
                                     ACT.Copy).then_inc(v_set, 1)

            def keys0():
                act.wait_ge(in_pack["early"], 16)
                for c in range(NB):
                    a, b = c * CW, c * CW + width(c)
                    act.wait_ge(k_proj, c + 1)
                    nc.scalar.activation(klo[:, a:b], ps[:, c % 2, 0:width(c)], ACT.Identity, bias=view["bk0"])
                    nc.scalar.activation(khi[:, a:b].bitcast(F32R), ps[:, c % 2, 0:width(c)], ACT.Identity,
                                         bias=view["bk0"]).then_inc(k_full, 1)

            def keys1():
                act.wait_ge(ev("l1_weights"), 1)
                for s in range(2):
                    for k in range(len(KC)):
                        act.wait_ge(in_stack[s][k], 48 * 2)

                def centred(c):
                    a, b = c * CW, c * CW + width(c)
                    act.wait_ge(k_proj, NB + c + 1)
                    nc.scalar.activation(klo[:, a:b], ps[:, c % 2, 0:width(c)], ACT.Identity, bias=bk1c[:, 0:1])
                    nc.scalar.activation(khi[:, a:b], ps[:, c % 2, 0:width(c)], ACT.Square,
                                         bias=bk1c[:, 0:1]).then_inc(k_sq, 1)

                def inverse_std(c):
                    a, b = c * CW, c * CW + width(c)
                    act.wait_ge(k_var, c + 1)
                    link(nc.scalar.activation(khi[:, a:b], ps[:, 2 + c % 2, 0:width(c)], ACT.Ln, bias=eps_col[:, 0:1]))
                    nc.scalar.activation(khi[:, a:b], khi[:, a:b], ACT.Exp, scale=-0.5).then_inc(k_rstd, 1)

                for c in range(NB + 1):
                    if c < NB:
                        centred(c)
                    if c >= 1:
                        inverse_std(c - 1)

            def exps(l):
                for g in range(NG):
                    for i in range(NB):
                        B = (NG * l + g) * NB + i
                        act.wait_ge(scores_done, B + 1)
                        if B >= 2:
                            act.wait_ge(av_done, B - 1)
                        w = tiles(i) * GQ
                        b0 = 2 * (B % 2)
                        nc.scalar.activation(prob[:, B % 2, 0:w],
                                             ps[:, b0:b0 + 2, :].rearrange("p a b -> p (a b)")[:, 0:w],
                                             ACT.Exp, scale=XSCALE).then_inc(exp_done, 1)

            def norm_std(tag):
                act.wait_ge(ev(f"{tag}_var"), 1)
                link(nc.scalar.activation(lnv[:, 0:1], mv[:, 1:2], ACT.Ln, bias=eps_col[0:T, 0:1]))
                nc.scalar.activation(rstd[:, 0:1], lnv[:, 0:1], ACT.Exp, scale=-0.5).then_inc(ev(f"{tag}_std"), 1)

            act.wait_ge(ev("eps_set"), 1)
            norm_std("ln0")
            keys0()
            for c in range(NB):
                v_out(0, c)
            exps(0)

            keys1()
            for c in range(NB):
                v_out(1, c)

            norm_std("ln1")
            act.wait_ge(ev("sa0_shifted"), 1)
            nc.scalar.activation(sa_s[:], sa_s[:], ACT.Exp, scale=SD ** -0.5).then_inc(ev("sa0_exp"), 1)

            norm_std("ln2")
            act.wait_ge(ev("ffn0_hidden"), 1)
            nc.scalar.activation(f0_sig[:], ps[:, 4:6, :].rearrange("p a b -> p (a b)")[:, 0:(E0 + 1) * T],
                                 ACT.Exp, scale=-1.0).then_inc(ev("ffn0_sig"), 1)
            act.wait_ge(ev("ffn0_negmax"), 1)
            nc.scalar.activation(stat[0:T, 0:E0], ps[0:T, 6, 0:E0], ACT.Exp, bias=stat[0:T, 8:9],
                                 accum_out=stat[0:T, 9:10])
            nc.scalar.activation(stat[0:T, 10:11], ps[0:T, 6, E0:E0 + 1], ACT.Exp, scale=-1.0).then_inc(ev("ffn0_exp"), 1)

            norm_std("ln3")
            act.wait_ge(ev("q1_var"), 1)
            link(nc.scalar.activation(q_b[0:QROWS, :], ps[0:QROWS, 6, 256:256 + NG * T], ACT.Ln, bias=eps_col[0:QROWS, 0:1]))
            nc.scalar.activation(q_b[0:QROWS, :], q_b[0:QROWS, :], ACT.Exp, scale=-0.5).then_inc(ev("q1_std"), 1)
            exps(1)

            norm_std("ln4")
            act.wait_ge(ev("sa1_shifted"), 1)
            nc.scalar.activation(sa_s[:], sa_s[:], ACT.Exp, scale=DH ** -0.5).then_inc(ev("sa1_exp"), 1)

            norm_std("ln5")
            act.wait_ge(ev("top1"), 1)
            nc.scalar.activation(stat[0:T, 8:9], stat[0:T, 0:1], ACT.Exp, scale=-1.0).then_inc(ev("top1_exp"), 1)
            act.wait_ge(ev("gu_folded"), 1)
            nc.scalar.activation(f1_sig, ps[:, 5, 0:F1], ACT.Exp, scale=-1.0).then_inc(ev("ffn1_sig"), 1)

        @block.vector
        def _(dve):
            n = [0]

            def link(ins):
                n[0] += 1
                ins.then_inc(dve_step, 1)
                dve.wait_ge(dve_step, n[0])

            V = nc.vector

            def norm(tag):
                link(V.bn_stats(st6[:, :], x))
                V.bn_aggr(mv[:, :], st6[:, :]).then_inc(ev(f"{tag}_var"), 1)
                dve.wait_ge(ev(f"{tag}_var"), 1)
                dve.wait_ge(ev(f"{tag}_std"), 1)
                V.tensor_scalar(y[:, :], x, mv[:, 0:1], rstd[:, 0:1], ALU.subtract, ALU.mult).then_inc(ev(f"{tag}_y"), 1)
                dve.wait_ge(ev(f"{tag}_ps"), 1)
                V.tensor_copy(yT[:, :], ps[:, 7, 0:T]).then_inc(ev(f"{tag}_yT"), 1)

            def stack_queries():
                link(V.tensor_copy(q_b[0:QROWS, :].bitcast(F32R), q_a[0:QROWS, :]))
                link(V.tensor_tensor(q_b[GC:2 * GC, :].bitcast(F32R), q_a[GC:2 * GC, :], q_b[GC:2 * GC, :], ALU.subtract))
                qv = q_b[0:QROWS, :].rearrange("p (g q) -> p g q", g=NG)
                for h in range(HG):
                    last = V.tensor_scalar(qst[0:QROWS, :, h * T:(h + 1) * T], qv, view["hmask"][:, h:h + 1], None, ALU.mult)
                last.then_inc(q_ready, 1)

            def max_chunk(G, m):
                N = MAXN * G + m
                k, p = m // 2, m % 2
                dve.wait_ge(max_made, N + 1)
                V.reduce_max(mx[:, p, k:k + 1], ps[:, 4 + N % 2, 0:width(k)], AX).then_inc(max_read, 1)

            def shift(G):
                dve.wait_ge(max_read, MAXN * (G + 1))
                link(V.tensor_reduce(mneg[:, :], mx[:, :, :], AX, ALU.max))
                link(V.tensor_scalar(mneg[:, :], mneg[:, :], -1.0, None, ALU.mult))
                link(V.tensor_copy(mhl[:, :, 0].bitcast(F32R), mneg[:, :]))
                V.tensor_tensor(mhl[:, :, 1].bitcast(F32R), mneg[:, :], mhl[:, :, 0], ALU.subtract).then_inc(shift_cols, 1)

            def shift_in(G):
                dve.wait_ge(shift_rows, G + 1)
                V.tensor_copy(qst[QROWS:KROWS, G % NG, :], ps[QROWS:KROWS, 7, 256:512]).then_inc(shift_ready, 1)

            def copy_acc(G):
                dve.wait_ge(av_done, NB * (G + 1))
                if G >= 1:
                    dve.wait_ge(o_ready, G)
                V.tensor_copy(avsb[:, :], ps[:, 6, 0:GQ]).then_inc(acc_copied, 1)

            def cross(l):
                G0 = NG * l
                for m in range(MAXN):
                    max_chunk(G0, m)
                shift(G0)
                shift_in(G0)
                for g in range(NG):
                    G = G0 + g
                    for i in range(NB):
                        if g + 1 < NG:
                            for m in max_schedule(i):
                                max_chunk(G + 1, m)
                            if i == MAX_LAST:
                                shift(G + 1)
                                shift_in(G + 1)
                        if i == 0 and g >= 1:
                            copy_acc(G - 1)
                copy_acc(G0 + NG - 1)

            def cross_out(l, bv, bo, tag):
                dve.wait_ge(o_ready, NG * (l + 1))
                o = ps[0:T, 7, 0:H * AUG].rearrange("p (h a) -> p h a", a=AUG)
                link(V.reciprocal(stat[0:T, 0:H], o[:, :, DH]))
                att = y[:, :].rearrange("p (h a) -> p h a", a=DH)
                link(V.tensor_tensor(att, o[:, :, 0:DH], stat[0:T, 0:H].unsqueeze(2).to_broadcast([T, H, DH]), ALU.mult))
                V.tensor_tensor(y[:, :], y[:, :], bv, ALU.add).then_inc(ev(f"{tag}_att"), 1)
                link(V.tensor_tensor(x, x, bo, ALU.add))
                dve.wait_ge(ev(f"{tag}_attps"), 1)
                V.tensor_copy(attT[:, :], ps[:, 6, 0:T]).then_inc(ev(f"{tag}_attT"), 1)
                dve.wait_ge(ev(f"{tag}_proj"), 1)
                link(V.tensor_tensor(x, ps[0:T, 6, 128:256], x, ALU.add))

            def softmax(tag, bnk):
                s3 = sa_s[:].rearrange("p (j k) -> p j k", k=T)
                mask = view["causal"].unsqueeze(1).to_broadcast([P, 8, T])
                dve.wait_ge(ev(f"{tag}_scores"), 1)
                link(V.tensor_tensor(s3, ps[:, bnk, :].rearrange("p (j k) -> p j k", k=T), mask, ALU.add))
                link(V.tensor_reduce(stat[:, 0:8], s3, AX, ALU.max))
                V.tensor_tensor(s3, s3, stat[:, 0:8].unsqueeze(2).to_broadcast([P, 8, T]),
                                ALU.subtract).then_inc(ev(f"{tag}_shifted"), 1)
                dve.wait_ge(ev(f"{tag}_exp"), 1)
                link(V.tensor_reduce(stat[:, 8:16], s3, AX, ALU.add))
                link(V.reciprocal(stat[:, 8:16], stat[:, 8:16]))
                V.tensor_tensor(s3, s3, stat[:, 8:16].unsqueeze(2).to_broadcast([P, 8, T]),
                                ALU.mult).then_inc(ev(f"{tag}_probs"), 1)
                dve.wait_ge(ev(f"{tag}_pT"), 1)
                V.tensor_copy(sa_pT[0:T, :], ps[0:T, 4:6, :].rearrange("p a b -> p (a b)")).then_inc(ev(f"{tag}_pTs"), 1)

            V.memset(eps_col[:, :], EPS).then_inc(ev("eps_set"), 1)
            V.memset(ps[:, 6, :], 0.0).then_inc(zeroed, 1)
            V.memset(kst[QROWS:KROWS, 0, :].bitcast(F32), 1.0).then_inc(ones_set, 1)
            dve.wait_ge(in_pack["rows"], 16)
            norm("ln0")
            dve.wait_ge(in_pack["const"], 16)
            dve.wait_ge(ev("q0_ps"), 1)
            link(V.tensor_tensor(q_a[0:QROWS, :].rearrange("p (g q) -> p g q", g=NG),
                                 ps[0:QROWS, 6, 256:256 + NG * T].rearrange("p (g q) -> p g q", g=NG),
                                 view["bq0x3"].unsqueeze(2).to_broadcast([QROWS, NG, T]), ALU.add))
            stack_queries()
            V.memset(kst[QROWS:KROWS, 1, :].bitcast(F32), 1.0).then_inc(ones_set, 1)
            dve.wait_ge(ev("l1_wps"), 1)
            V.tensor_copy(wk1c[:, :], ps[:, 7, 0:D])
            V.tensor_copy(bk1c[:, :], ps[:, 7, D:D + 1])
            V.tensor_copy(bq1c[0:QROWS, :], ps[0:QROWS, 7, D + 1:D + 1 + NG])
            V.tensor_copy(wq1c[:, :], ps[:, 5, 0:NG * QROWS]).then_inc(ev("l1_weights"), 1)
            cross(0)
            cross_out(0, view["bv0"], view["bo0"], "x0")

            dve.wait_ge(ev("l1_weights"), 1)
            m = 0
            for c in range(NB):
                a, b = c * CW, c * CW + width(c)
                dve.wait_ge(k_rstd, c + 1)
                for ins in (lambda: V.tensor_tensor(klo[:, a:b], klo[:, a:b], khi[:, a:b], ALU.mult),
                            lambda: V.tensor_scalar(klo[:, a:b], klo[:, a:b], view["kgb"][:, 0:1], view["kgb"][:, 1:2],
                                                    ALU.mult, ALU.add)):
                    ins().then_inc(k_aff, 1)
                    m += 1
                    dve.wait_ge(k_aff, m)
                V.tensor_copy(khi[:, a:b].bitcast(F32R), klo[:, a:b]).then_inc(k_full, 1)

            norm("ln1")
            dve.wait_ge(ev("qbd_zero"), 1)
            dve.wait_ge(ev("sa0_q"), 1)
            q3 = sa_q[:].rearrange("p (j c) -> p j c", j=NP_)
            for hh in range(2):
                r = slice(64 * hh, 64 * hh + 64)
                V.tensor_tensor(q3[r, :, r], ps[r, 4, :].rearrange("p (j q) -> p j q", q=T),
                                view["bqa"][r].unsqueeze(2).to_broadcast([64, NP_, T]), ALU.add)
            V.tensor_tensor(sa_k[:].rearrange("p (j q) -> p j q", q=T), ps[:, 5, :].rearrange("p (j q) -> p j q", q=T),
                            view["bka"].unsqueeze(2).to_broadcast([P, NP_, T]), ALU.add).then_inc(ev("sa0_qk"), 1)
            dve.wait_ge(ev("sa0_v"), 1)
            V.tensor_copy(sa_v[0:T, :], ps[0:T, 2:4, :].rearrange("p a b -> p (a b)")).then_inc(ev("sa0_vs"), 1)
            softmax("sa0", 6)
            dve.wait_ge(ev("sa0_z"), 1)
            V.tensor_tensor(sa_k[:].rearrange("p (h q) -> p h q", h=SH), ps[:, 6, :].rearrange("p (h q) -> p h q", h=SH),
                            view["bva"].unsqueeze(2).to_broadcast([P, SH, T // 2]), ALU.add).then_inc(ev("sa0_zT"), 1)
            dve.wait_ge(ev("sa0_proj"), 1)
            link(V.scalar_tensor_tensor(x, ps[0:T, 7, 0:D], SD ** -0.5, x, ALU.mult, ALU.add))

            norm("ln2")
            dve.wait_ge(ev("ffn0_hidden"), 1)
            lg = stat[0:T, 16:16 + E0]
            link(V.tensor_copy(lg, ps[0:T, 6, 0:E0]))
            link(V.max(stat[0:T, 24:32], lg))
            V.tensor_scalar(stat[0:T, 8:9], stat[0:T, 24:25], -1.0, None, ALU.mult).then_inc(ev("ffn0_negmax"), 1)
            link(V.max_index(idx8[:, :], stat[0:T, 24:32], lg))
            link(V.tensor_copy(stat[0:T, 32:40], idx8[:, :]))
            link(V.tensor_scalar(stat[0:T, 40:48], view["iota"][0:T, 0:E0], stat[0:T, 32:33], None, ALU.is_equal))
            link(V.scalar_tensor_tensor(stat[0:T, 40:48], view["iota"][0:T, 0:E0], stat[0:T, 33:34], stat[0:T, 40:48],
                                        ALU.is_equal, ALU.add))
            dve.wait_ge(ev("ffn0_exp"), 1)
            link(V.reciprocal(stat[0:T, 9:10], stat[0:T, 9:10]))
            link(V.scalar_tensor_tensor(stat[0:T, 48:56], stat[0:T, 0:E0], stat[0:T, 9:10], stat[0:T, 40:48],
                                        ALU.mult, ALU.mult))
            link(V.tensor_scalar(stat[0:T, 10:11], stat[0:T, 10:11], 1.0, None, ALU.add))
            link(V.reciprocal(stat[0:T, 10:11], stat[0:T, 10:11]))
            dve.wait_ge(ev("ffn0_sig"), 1)
            link(V.tensor_scalar(f0_sig[:], f0_sig[:], 1.0, None, ALU.add))
            link(V.reciprocal(f0_sig[:], f0_sig[:]))
            hid = ps[:, 4:6, :].rearrange("p a b -> p (a b)")
            link(V.tensor_tensor(f0_h[:], hid[:, 0:(E0 + 1) * T], f0_sig[:], ALU.mult))
            V.tensor_tensor(f0_h[:, E0 * T:(E0 + 1) * T], hid[:, (E0 + 1) * T:(E0 + 2) * T], f0_h[:, E0 * T:(E0 + 1) * T],
                            ALU.mult).then_inc(ev("ffn0_h"), 1)
            dve.wait_ge(ev("ffn0_y"), 1)
            ye = ps[0:T, 2:4, :].rearrange("p a (e d) -> p (a e) d", d=D)
            for e in range(E0):
                link(V.scalar_tensor_tensor(x, ye[:, e, :], stat[0:T, 48 + e:49 + e], x, ALU.mult, ALU.add))
            link(V.scalar_tensor_tensor(x, ps[0:T, 7, 0:D], stat[0:T, 10:11], x, ALU.mult, ALU.add))

            norm("ln3")
            dve.wait_ge(ev("q1_ps"), 1)
            qa3 = q_a[0:QROWS, :].rearrange("p (g q) -> p g q", g=NG)
            link(V.tensor_tensor(qa3, ps[0:QROWS, 6, 0:NG * T].rearrange("p (g q) -> p g q", g=NG),
                                 bq1c[0:QROWS, :].unsqueeze(2).to_broadcast([QROWS, NG, T]), ALU.add))
            V.tensor_tensor(q_b[0:QROWS, :], q_a[0:QROWS, :], q_a[0:QROWS, :], ALU.mult).then_inc(ev("q1_sq"), 1)
            dve.wait_ge(ev("q1_std"), 1)
            link(V.tensor_tensor(q_a[0:QROWS, :], q_a[0:QROWS, :], q_b[0:QROWS, :], ALU.mult))
            link(V.tensor_scalar(q_a[0:QROWS, :], q_a[0:QROWS, :], view["qgb"][:, 0:1], view["qgb"][:, 1:2],
                                 ALU.mult, ALU.add))
            stack_queries()
            cross(1)
            cross_out(1, view["bv1"], view["bp1"], "x1")

            norm("ln4")
            dve.wait_ge(ev("sa1_qkv"), 1)
            link(V.tensor_tensor(s1_qkv, ps[0:T, 4, 0:3 * D], view["bqkv1"], ALU.add))
            qk = s1_qkv[:, 0:2 * D].rearrange("p (h a) -> p h a", a=DH)
            r1 = s1_r[:, 0:2 * D].rearrange("p (h a) -> p h a", a=DH)
            r2 = s1_r[:, 2 * D:4 * D].rearrange("p (h a) -> p h a", a=DH)
            half = DH // 2
            V.tensor_tensor(r1, qk, view["cos"].unsqueeze(1).to_broadcast([T, 2 * H, DH]), ALU.mult)
            V.tensor_tensor(r2[:, :, 0:half], qk[:, :, half:DH],
                            view["sin"][:, 0:half].unsqueeze(1).to_broadcast([T, 2 * H, half]), ALU.mult)
            link(V.tensor_tensor(r2[:, :, half:DH], qk[:, :, 0:half],
                                 view["sin"][:, half:DH].unsqueeze(1).to_broadcast([T, 2 * H, half]), ALU.mult))
            V.tensor_tensor(s1_r[:, 0:2 * D], s1_r[:, 0:2 * D], s1_r[:, 2 * D:4 * D], ALU.add).then_inc(ev("sa1_rope"), 1)
            link(V.tensor_tensor(x, x, view["bproj1"], ALU.add))
            dve.wait_ge(ev("sa1_qkT"), 1)
            V.tensor_copy(attT[:, :], ps[:, 7, 0:T])
            V.tensor_tensor(sa_q[:].rearrange("p (h k) -> p h k", k=T),
                            ps[:, 7, T:2 * T].unsqueeze(1).to_broadcast([P, H, T]),
                            view["headmask"].unsqueeze(2).to_broadcast([P, H, T]), ALU.mult).then_inc(ev("sa1_qk"), 1)
            softmax("sa1", 6)
            dve.wait_ge(ev("sa1_av"), 1)
            V.tensor_copy(y[:, :], ps[0:T, 7, 0:D]).then_inc(ev("sa1_o"), 1)
            dve.wait_ge(ev("sa1_oT"), 1)
            V.tensor_copy(attT[:, :], ps[:, 6, 0:T]).then_inc(ev("sa1_oTs"), 1)
            dve.wait_ge(ev("sa1_proj"), 1)
            link(V.tensor_tensor(x, ps[0:T, 6, 128:256], x, ALU.add))

            norm("ln5")
            dve.wait_ge(ev("ffn1_logits"), 1)
            lg = stat[0:T, 16:16 + E1]
            link(V.tensor_copy(lg, ps[0:T, 6, 0:E1]))
            V.max(stat[0:T, 0:8], lg).then_inc(ev("top1"), 1)
            dve.wait_ge(ev("top1"), 1)
            link(V.max_index(idx8[:, :], stat[0:T, 0:8], lg))
            link(V.tensor_copy(stat[0:T, 9:10], idx8[:, 0:1]))
            dve.wait_ge(ev("top1_exp"), 1)
            link(V.tensor_scalar(stat[0:T, 10:11], stat[0:T, 8:9], 1.0, None, ALU.add))
            link(V.reciprocal(stat[0:T, 10:11], stat[0:T, 10:11]))
            link(V.memset(f1_bc[:, :, :], 0.0))
            V.tensor_scalar(f1_bc[:, 0, :], f1_bc[:, 0, :], stat[0:T, 9:10], None, ALU.add)
            V.tensor_scalar(f1_bc[:, 1, :], f1_bc[:, 1, :], stat[0:T, 10:11], None, ALU.add).then_inc(ev("ffn1_bc"), 1)
            dve.wait_ge(ev("ffn1_bcps"), 1)
            link(V.tensor_tensor(attT[:, :], ps[:, 7, T:2 * T], yT[:, :], ALU.mult))
            EC = 8
            for c in range(E1 // EC):
                es = slice(c * EC, (c + 1) * EC)
                link(V.tensor_tensor(f1_mask[:, es, :], ps[:, 7, 0:T].unsqueeze(1).to_broadcast([P, EC, T]),
                                     view["iota"][:, es].unsqueeze(2).to_broadcast([P, EC, T]), ALU.is_equal))
                V.tensor_tensor(f1_x[:, es, :], f1_mask[:, es, :], attT[:, :].unsqueeze(1).to_broadcast([P, EC, T]),
                                ALU.mult).then_inc(ev("ffn1_x"), 1)
            dve.wait_ge(ev("ffn1_gu"), 1)
            V.tensor_copy(f1_gu, ps[:, 4, :]).then_inc(ev("ffn1_gus"), 1)
            dve.wait_ge(ev("ffn1_sig"), 1)
            link(V.tensor_scalar(f1_sig, f1_sig, 1.0, None, ALU.add))
            link(V.reciprocal(f1_sig, f1_sig))
            link(V.tensor_tensor(f1_sig, ps[:, 5, 0:F1], f1_sig, ALU.mult))
            V.tensor_tensor(f1_h, ps[:, 5, F1:2 * F1], f1_sig, ALU.mult).then_inc(ev("ffn1_h"), 1)
            dve.wait_ge(ev("ffn1_hT"), 1)
            link(V.tensor_copy(f1_hT, ps[:, 6, 0:2 * P]))
            for c in range(E1 // EC):
                es = slice(c * EC, (c + 1) * EC)
                for k in range(2):
                    last = V.tensor_tensor(f1_he[k][:, es, :], f1_mask[:, es, :],
                                           f1_hT[:, k * P + T:(k + 1) * P].unsqueeze(1).to_broadcast([P, EC, T]), ALU.mult)
                last.then_inc(ev("ffn1_he"), 1)
            dve.wait_ge(ev("ffn1_d"), 1)
            V.tensor_copy(y2, ps[:, 4, 0:D]).then_inc(ev("ffn1_ds"), 1)
            dve.wait_ge(ev("ffn1_out"), 1)
            V.tensor_tensor(x, ps[0:T, 5, 0:D], x, ALU.add).then_inc(ev("out_ready"), 1)

        @block.tensor
        def _(pe):
            mm = nc.tensor.matmul

            def one(out_, lhsT, rhs, start=True, stop=True):
                return mm(out_, lhsT, rhs, start=start, stop=stop, skip_group_check=True)

            def yT_of(tag):
                pe.wait_ge(ev(f"{tag}_y"), 1)
                nc.tensor.transpose(ps[:, 7, 0:T], y[:, :], ident[0:T, 0:T]).then_inc(ev(f"{tag}_ps"), 1)
                pe.wait_ge(ev(f"{tag}_yT"), 1)

            def key_chunk(l, c, w):
                a, b = c * CW, c * CW + width(c)
                if l == 0:
                    for i in range(len(in_ctx)):
                        if CTX_PIECES[i] <= a < CTX_PIECES[i + 1]:
                            pe.wait_ge(in_ctx[i], 16)
                if c >= 2:
                    pe.wait_ge(k_full if l == 0 else k_sq, c - 1)
                one(ps[:, c % 2, 0:width(c)], w, ctx_sb[:, a:b]).then_inc(k_proj, 1)

            def var_chunk(c):
                a, b = c * CW, c * CW + width(c)
                pe.wait_ge(k_sq, c + 1)
                if c >= 2:
                    pe.wait_ge(k_rstd, c - 1)
                one(ps[:, 2 + c % 2, 0:width(c)], view["avg"], khi[:, a:b]).then_inc(k_var, 1)

            def v_chunk(l, c, w):
                if c >= 2:
                    pe.wait_ge(v_set, l * NB + c - 1)
                for t in range(tiles(c)):
                    for hh in range(2):
                        a = (BT * c + t) * P + 64 * hh
                        last = one(ps[64 * hh:64 * hh + 64, 2 + c % 2, t * D:(t + 1) * D], ctx_sb[:, a:a + 64], w)
                last.then_inc(v_proj, 1)

            def max_chunk(G, m):
                N = MAXN * G + m
                k, p = m // 2, m % 2
                for j, (b0, b1) in enumerate(KC):
                    if b0 == k and p == 0:
                        pe.wait_ge(in_stack[G % 2][j], 48 * (G // 2 + 1))
                if N >= 2:
                    pe.wait_ge(max_read, N - 1)
                a, b = k * CW, k * CW + width(k)
                one(ps[:, 4 + N % 2, 0:width(k)], qst[0:QROWS, G % NG, p * P:(p + 1) * P],
                    kst[0:QROWS, G % 2, a:b]).then_inc(max_made, 1)

            def shift(G):
                pe.wait_ge(shift_cols, G + 1)
                for p in range(2):
                    last = one(ps[QROWS:KROWS, 7, 256 + p * P:256 + (p + 1) * P], mhl[:, p, :], ident)
                last.then_inc(shift_rows, 1)

            def scores(G, i):
                B = NB * G + i
                if i == 0:
                    pe.wait_ge(shift_ready, G + 1)
                if B % (NG * NB) >= 2:
                    pe.wait_ge(exp_done, B - 1)
                dst = ps[:, 2 * (B % 2):2 * (B % 2) + 2, :].rearrange("p a b -> p (a b)")
                for t in range(tiles(i)):
                    a = (BT * i + t) * P
                    last = one(dst[:, t * GQ:(t + 1) * GQ], kst[0:KROWS, G % 2, a:a + P], qst[0:KROWS, G % NG, :])
                last.then_inc(scores_done, 1)

            def weighted(G, i):
                B = NB * G + i
                g = G % NG
                pe.wait_ge(exp_done, B + 1)
                if i == 0 and G >= 1:
                    pe.wait_ge(acc_copied, G)
                for t in range(tiles(i)):
                    for p in range(2):
                        h = HG * g + 2 * p
                        last = one(ps[32 * t:32 * t + 2 * AUG, 6, p * P:(p + 1) * P],
                                   vaug[:, BT * i + t, h:h + 2, :].rearrange("p h a -> p (h a)"),
                                   prob[:, B % 2, t * GQ + p * P:t * GQ + (p + 1) * P],
                                   start=(i == 0 and p == 0), stop=(i == NB - 1))
                last.then_inc(av_done, 1)

            def gather(G):
                g = G % NG
                pe.wait_ge(acc_copied, G + 1)
                for h in range(HG):
                    c = (HG * g + h) * AUG
                    last = one(ps[0:T, 7, c:c + AUG], avsb[:, h * T:(h + 1) * T],
                               view["sel"][:, (h % 2) * AUG:(h % 2 + 1) * AUG])
                last.then_inc(o_ready, 1)

            def cross(l):
                G0 = NG * l
                shift(G0)
                for g in range(NG):
                    G = G0 + g
                    for i in range(NB):
                        scores(G, i)
                        if g + 1 < NG:
                            for m in max_schedule(i):
                                max_chunk(G + 1, m)
                        if i >= 1:
                            weighted(G, i - 1)
                        elif g >= 1:
                            weighted(G - 1, NB - 1)
                        if i == MAX_LAST + 1 and g + 1 < NG:
                            shift(G + 1)
                        if i == 3 and g >= 1:
                            gather(G - 1)
                weighted(G0 + NG - 1, NB - 1)
                gather(G0 + NG - 1)

            def cross_out(w, tag):
                pe.wait_ge(ev(f"{tag}_att"), 1)
                nc.tensor.transpose(ps[:, 6, 0:T], y[:, :], ident[0:T, 0:T]).then_inc(ev(f"{tag}_attps"), 1)
                pe.wait_ge(ev(f"{tag}_attT"), 1)
                one(ps[0:T, 6, 128:256], attT[:, :], w).then_inc(ev(f"{tag}_proj"), 1)

            def turn_probs(tag):
                pe.wait_ge(ev(f"{tag}_probs"), 1)
                pt = ps[0:T, 4:6, :].rearrange("p a b -> p (a b)")
                for j in range(8):
                    last = nc.tensor.transpose(pt[:, j * P:(j + 1) * P], sa_s[:, j * T:(j + 1) * T], ident)
                last.then_inc(ev(f"{tag}_pT"), 1)
                pe.wait_ge(ev(f"{tag}_pTs"), 1)

            pe.wait_ge(in_pack["early"], 16)
            key_chunk(0, 0, view["wk0"])
            key_chunk(0, 1, view["wk0"])
            pe.wait_ge(in_pack["const"], 16)
            yT_of("ln0")
            pe.wait_ge(zeroed, 1)
            for g in range(NG):
                last = one(ps[0:QROWS, 6, 256 + g * T:256 + (g + 1) * T], view["wq0x3"][:, g * QROWS:(g + 1) * QROWS], yT[:, :])
            last.then_inc(ev("q0_ps"), 1)
            for c in range(2, NB):
                key_chunk(0, c, view["wk0"])
            pe.wait_ge(in_pack["raw1"], 16)
            one(ps[:, 7, 0:D], view["wk1"], view["cen"])
            one(ps[:, 7, D:D + 1], view["cen"], view["bk1"])
            one(ps[0:QROWS, 7, D + 1:D + 1 + NG], view["cen"][0:QROWS, 0:QROWS], view["bq1x3"])
            one(ps[:, 5, 0:NG * QROWS], view["wq1"], view["cen3"]).then_inc(ev("l1_wps"), 1)
            pe.wait_ge(ev("l1_weights"), 1)
            pe.wait_ge(q_ready, 1)
            for c in range(NB):
                v_chunk(0, c, view["wv0"])
                max_chunk(0, 2 * c)
                max_chunk(0, 2 * c + 1)
            pe.wait_ge(v_set, NB)
            pe.wait_ge(v_ones, 1)
            pe.wait_ge(ones_set, 2)
            cross(0)
            cross_out(view["wo0"], "x0")

            pe.wait_ge(in_pack["small1"], 16)
            for c in range(NB + 1):
                if c < NB:
                    key_chunk(1, c, wk1c[:, :])
                if c >= 1:
                    var_chunk(c - 1)
            pe.wait_ge(k_rstd, NB)
            for c in range(NB):
                v_chunk(1, c, view["wv1"])
            pe.wait_ge(v_set, 2 * NB)

            yT_of("ln1")
            pe.wait_ge(in_pack["late"], 16)
            for w, bnk in (("wqa", 4), ("wka", 5)):
                for h in range(SH):
                    last = one(ps[64 * (h % 2):64 * (h % 2) + 64, bnk, (h // 2) * T:(h // 2 + 1) * T],
                               view[w][:, h * SD:(h + 1) * SD], yT[:, :])
            last.then_inc(ev("sa0_q"), 1)
            for k in range(2):
                last = one(ps[0:T, 2 + k, :], yT[:, :], view["wva"][:, k * 512:(k + 1) * 512])
            last.then_inc(ev("sa0_v"), 1)
            pe.wait_ge(ev("sa0_qk"), 1)
            for j in range(NP_):
                last = one(ps[:, 6, j * T:(j + 1) * T], sa_q[:, j * P:(j + 1) * P], sa_k[:, j * T:(j + 1) * T])
            last.then_inc(ev("sa0_scores"), 1)
            turn_probs("sa0")
            pe.wait_ge(ev("sa0_vs"), 1)
            for h in range(SH):
                for u in range(2):
                    q0 = (h // 2) * P + (h % 2) * T
                    last = one(ps[64 * u:64 * u + 64, 6, h * (T // 2):(h + 1) * (T // 2)],
                               sa_v[0:T, h * SD:(h + 1) * SD], sa_pT[0:T, q0 + u:q0 + T:2])
            last.then_inc(ev("sa0_z"), 1)
            pe.wait_ge(ev("sa0_zT"), 1)
            zT = sa_k[:].rearrange("p (s r) -> p r s", r=NP_)
            for r in range(NP_):
                last = one(ps[0:T, 7, 0:D], zT[:, r, :], view["proja"][:, r * D:(r + 1) * D],
                           start=(r == 0), stop=(r == NP_ - 1))
            last.then_inc(ev("sa0_proj"), 1)

            yT_of("ln2")
            one(ps[0:T, 6, 0:E0 + 1], yT[:, :], view["router0"])
            hid = ps[:, 4:6, :].rearrange("p a b -> p (a b)")
            for e in range(E0 + 2):
                last = one(hid[:, e * T:(e + 1) * T], view["w1"][:, e * F0:(e + 1) * F0], yT[:, :])
            last.then_inc(ev("ffn0_hidden"), 1)
            pe.wait_ge(ev("ffn0_h"), 1)
            for e in range(E0):
                one(ps[0:T, 2 + e // 4, (e % 4) * D:(e % 4 + 1) * D], f0_h[:, e * T:(e + 1) * T],
                    view["w2"][:, e * D:(e + 1) * D])
            one(ps[0:T, 7, 0:D], f0_h[:, E0 * T:(E0 + 1) * T], view["sdown0"]).then_inc(ev("ffn0_y"), 1)

            yT_of("ln3")
            for g in range(NG):
                last = one(ps[0:QROWS, 6, g * T:(g + 1) * T], wq1c[:, g * QROWS:(g + 1) * QROWS], yT[:, :])
            last.then_inc(ev("q1_ps"), 1)
            pe.wait_ge(ev("q1_sq"), 1)
            one(ps[0:QROWS, 6, 256:256 + NG * T], view["avg"][0:QROWS, 0:QROWS], q_b[0:QROWS, :]).then_inc(ev("q1_var"), 1)
            pe.wait_ge(q_ready, 2)
            for m in range(MAXN):
                max_chunk(NG, m)
            cross(1)
            cross_out(view["wp1"], "x1")

            yT_of("ln4")
            pe.wait_ge(in_pack["tail1"], 16)
            one(ps[0:T, 4, 0:3 * D], yT[:, :], view["wqkv1"]).then_inc(ev("sa1_qkv"), 1)
            pe.wait_ge(ev("sa1_rope"), 1)
            for k in range(2):
                last = nc.tensor.transpose(ps[:, 7, k * T:(k + 1) * T], s1_r[:, k * D:(k + 1) * D], ident[0:T, 0:T])
            last.then_inc(ev("sa1_qkT"), 1)
            pe.wait_ge(ev("sa1_qk"), 1)
            for hh in range(2):
                last = one(ps[64 * hh:64 * hh + 64, 6, :], attT[:, :], sa_q[:, hh * 512:(hh + 1) * 512])
            last.then_inc(ev("sa1_scores"), 1)
            turn_probs("sa1")
            for h in range(H):
                hh, j = h // 8, h % 8
                last = one(ps[0:T, 7, h * DH:(h + 1) * DH], sa_pT[0:T, j * P + hh * T:j * P + hh * T + T],
                           s1_qkv[:, 2 * D + h * DH:2 * D + (h + 1) * DH])
            last.then_inc(ev("sa1_av"), 1)
            pe.wait_ge(ev("sa1_o"), 1)
            nc.tensor.transpose(ps[:, 6, 0:T], y[:, :], ident[0:T, 0:T]).then_inc(ev("sa1_oT"), 1)
            pe.wait_ge(ev("sa1_oTs"), 1)
            one(ps[0:T, 6, 128:256], attT[:, :], view["wproj1"]).then_inc(ev("sa1_proj"), 1)

            yT_of("ln5")
            one(ps[0:T, 6, 0:E1], yT[:, :], view["gate1"]).then_inc(ev("ffn1_logits"), 1)
            one(ps[0:T, 5, :], yT[:, :], view["sgu1"])
            pe.wait_ge(ev("ffn1_bc"), 1)
            for k in range(2):
                last = one(ps[:, 7, k * T:(k + 1) * T], f1_bc[:, k, :], ident[0:T, 0:T])
            last.then_inc(ev("ffn1_bcps"), 1)
            for s in in_exp:
                pe.wait_ge(s, 16)
            for e in range(E1):
                if e % 8 == 0:
                    pe.wait_ge(ev("ffn1_x"), e // 8 + 1)
                o = 64 * (e % 2)
                last = one(ps[o:o + 64, 4, :], f1_x[:, e, :], expert(e)[:, 0:2 * F1], start=(e < 2), stop=(e >= E1 - 2))
            last.then_inc(ev("ffn1_gu"), 1)
            pe.wait_ge(ev("ffn1_gus"), 1)
            one(ps[64:128, 5, :], view["fold"], f1_gu).then_inc(ev("gu_folded"), 1)
            pe.wait_ge(ev("ffn1_h"), 1)
            for k in range(2):
                last = nc.tensor.transpose(ps[:, 6, k * P:(k + 1) * P], f1_h[:, k * P:(k + 1) * P], ident)
            last.then_inc(ev("ffn1_hT"), 1)
            pe.wait_ge(ev("ffn1_he"), 1)
            for k in range(2):
                one(ps[64 * k:64 * k + 64, 4, 0:D], f1_hT[:, k * P:k * P + T], view["sdown1"][:, k * D:(k + 1) * D],
                    start=True, stop=False)
            for e in range(E1):
                if e % 8 == 0:
                    pe.wait_ge(ev("ffn1_he"), e // 8 + 1)
                for k in range(2):
                    last = one(ps[64 * k:64 * k + 64, 4, 0:D], f1_he[k][:, e, :],
                               expert(e)[:, 2 * F1 + k * D:2 * F1 + (k + 1) * D], start=False, stop=(e == E1 - 1))
            last.then_inc(ev("ffn1_d"), 1)
            pe.wait_ge(ev("ffn1_ds"), 1)
            one(ps[0:T, 5, 0:D], view["fold"], y2).then_inc(ev("ffn1_out"), 1)


def _constants():
    c = {}
    head = np.arange(P) // DH
    same = (head[:, None] == head[None, :]).astype(np.float32) / DH
    cen = np.eye(P, dtype=np.float32) - same
    c["ident"] = np.eye(P, dtype=np.float32)
    c["avg"] = same
    c["cen"] = cen
    c["cen3"] = np.concatenate([np.tile(cen[:, g * GC:(g + 1) * GC], (1, 3)) for g in range(NG)], axis=1)
    r = np.arange(P) % 32
    c["sel"] = (r[:, None] == np.arange(2 * AUG)[None, :]).astype(np.float32)
    c["fold"] = (np.arange(P)[:, None] % T == np.arange(T)[None, :]).astype(np.float32)
    c["hmask"] = ((np.arange(QROWS)[:, None] % GC) // DH == np.arange(HG)[None, :]).astype(np.float32)
    c["headmask"] = (head[:, None] == np.arange(H)[None, :]).astype(np.float32)
    q, k = np.arange(P)[:, None] % T, np.arange(T)[None, :]
    c["causal"] = np.where(k > q, np.float32(-1e30), np.float32(0)).astype(np.float32)
    c["iota"] = np.tile(np.arange(E1, dtype=np.float32), (P, 1))
    half = DH // 2
    freqs = np.float32(1.0) / np.float32(10000.0) ** (np.arange(half, dtype=np.float32) / np.float32(half))
    angle = np.arange(T, dtype=np.float32)[:, None] * freqs[None, :].astype(np.float32)
    cos, sin = np.cos(angle).astype(np.float32), np.sin(angle).astype(np.float32)
    c["cos"] = np.concatenate([cos, cos], axis=1)
    c["sin"] = np.concatenate([-sin, sin], axis=1)
    return c


def _blocks(w, n):
    return w.reshape(n, P, -1).transpose(1, 0, 2).reshape(P, -1)


def _layout(i):
    a = dict(_constants())
    rep = lambda v: np.broadcast_to(v[None, :], (T, v.shape[0]))
    g3 = lambda w: np.concatenate([np.tile(w[:, g * GC:(g + 1) * GC], (1, 3)) for g in range(NG)], axis=1)
    b3 = lambda b: np.tile(b.reshape(NG, GC).T, (3, 1))
    a["wk0"], a["wv0"], a["wo0"] = i["L0_xattn_Wk"], i["L0_xattn_Wv"], i["L0_xattn_Wo"]
    a["wq0x3"], a["bq0x3"] = g3(i["L0_xattn_Wq"]), b3(i["L0_xattn_bq"])
    a["bk0"] = i["L0_xattn_bk"].reshape(P, 1)
    for n, m in (("wqa", "Wq"), ("wka", "Wk"), ("wva", "Wv")):
        a[n] = i["L0_attn_" + m].reshape(SH * SD, D).T
    for n, m in (("bqa", "bq"), ("bka", "bk")):
        a[n] = i["L0_attn_" + m].reshape(NP_, P).T
    a["bva"] = np.tile(i["L0_attn_bv"].T, (2, 1))
    a["proja"] = _blocks(i["L0_attn_proj"], NP_)
    a["w1"] = np.concatenate([i["L0_ffn_w1"].transpose(1, 0, 2).reshape(P, -1), i["L0_ffn_shared_gate_up"]], axis=1)
    a["w2"] = i["L0_ffn_w2"].transpose(1, 0, 2).reshape(P, -1)
    a["sdown0"] = i["L0_ffn_shared_down"]
    a["router0"] = np.concatenate([i["L0_ffn_router_w"], i["L0_ffn_shared_gate_w"]], axis=1)
    a["x"] = i["x"][0]
    for n, m in (("bv0", "L0_xattn_bv"), ("bo0", "L0_xattn_bo"), ("bv1", "L1_xattn_bv"), ("bp1", "L1_xattn_bp"),
                 ("bproj1", "L1_attn_proj_b"), ("bqkv1", "L1_attn_qkv_b")):
        a[n] = rep(i[m])
    a["wv1"], a["wp1"] = i["L1_xattn_Wv"].T, i["L1_xattn_Wp"].T
    a["wk1"], a["wq1"] = i["L1_xattn_Wk"], i["L1_xattn_Wq"]
    a["bk1"], a["bq1x3"] = i["L1_xattn_bk"].reshape(P, 1), b3(i["L1_xattn_bq"])
    gb = np.stack([np.tile(i["L1_xattn_q_gamma"], H), np.tile(i["L1_xattn_q_beta"], H)], axis=1)
    a["qgb"] = gb[:QROWS]
    a["kgb"] = np.stack([np.tile(i["L1_xattn_k_gamma"], H), np.tile(i["L1_xattn_k_beta"], H)], axis=1)
    a["wproj1"], a["wqkv1"] = i["L1_attn_proj_w"].T, i["L1_attn_qkv_w"].T
    a["gate1"] = i["L1_ffn_gate_w"]
    a["sgu1"] = np.concatenate([i["L1_ffn_shared_gate_w"], i["L1_ffn_shared_up_w"]], axis=1)
    a["sdown1"] = _blocks(i["L1_ffn_shared_down_w"], 2)
    packs = {}
    for pack, items in PACKS.items():
        out = np.zeros((P, words(pack)), np.float32)
        at = 0
        for name, r, w in items:
            out[0:r, at:at + w] = a[name]
            at += w
        packs[pack] = out
    gate = i["L1_ffn_routed_gate_w"].transpose(1, 0, 2)
    up = i["L1_ffn_routed_up_w"].transpose(1, 0, 2)
    down = i["L1_ffn_routed_down_w"].reshape(E1, 2, P, D).transpose(2, 0, 1, 3).reshape(P, E1, 2 * D)
    experts = np.concatenate([gate, up, down], axis=2).reshape(P, E1 * EW)
    return np.ascontiguousarray(i["ctx_1024"][0].T), packs, np.ascontiguousarray(experts)


def kernel(**inputs):
    import concourse.bacc as _bacc
    from concourse.bass_utils import run_bass_kernel_spmd as _run

    i = {k: np.asarray(v) for k, v in inputs.items()}
    ctxT, packs, experts = _layout(i)
    arrays = {"in_ctxT": ctxT, "in_experts": experts, **{"in_" + n: a for n, a in packs.items()}}
    nc = _bacc.Bacc("TRN2", target_bir_lowering=False, num_devices=1)
    aps = {n: nc.dram_tensor(n, a.shape, mybir.dt.from_np(a.dtype), kind="ExternalInput").ap() for n, a in arrays.items()}
    out = nc.dram_tensor("out", (T, D), F32, kind="ExternalOutput").ap()
    perceiver(nc, aps["in_ctxT"], {n: aps["in_" + n] for n in packs}, aps["in_experts"], out)
    r = _run(nc, [arrays], core_ids=[0])
    return r.results[0]["out"].reshape(1, T, D)
```

```python
from contextlib import ExitStack

import numpy as np

import concourse.bass as bass
from concourse import mybir

F32 = mybir.dt.float32
F32R = mybir.dt.float32r
U32 = mybir.dt.uint32
ALU = mybir.AluOpType
ACT = mybir.ActivationFunctionType
AX = mybir.AxisListType.X

P = 128
T = 64
D = 128
S = 6272
H = 16
DH = D // H
NG = 4
HG = H // NG
GC = HG * DH
GQ = HG * T
NT = S // P
BT = 4
NB = -(-NT // BT)
CW = BT * P
AUG = DH + 1
SH = 16
SD = 64
NP_ = SH // 2
E0, E1 = 8, 32
F0, F1 = 128, 256
EW = 3 * F1
EPS = 1e-5
XSCALE = DH ** -0.5
QROWS = 3 * GC
KROWS = QROWS + 2
KC = [(0, 2), (2, 4), (4, 7), (7, 10), (10, NB)]
CTX_PIECES = [0, 512, 1536, 3072, 4608, S]
MAXN = 2 * NB
LEAD = 4

KEYS_AHEAD = 6

SHIFT_AT = NB - LEAD // 2


def v_schedule(c):
    return range(min(NB, max(0, c - 2) + max(0, c - 11)), min(NB, max(0, c - 1) + max(0, c - 10)))


def max_count(G):
    l, g = divmod(G, NG)
    return l * (NB + (NG - 1) * MAXN) + (NB + (g - 1) * MAXN if g else 0)


def width(c):
    return min(CW, S - c * CW)


def tiles(i):
    return min(BT, NT - i * BT)


def max_stream(G0, a, b):
    return [(G0 + 1 + n // MAXN, n % MAXN) for n in range(a, min(b, (NG - 1) * MAXN))]


EARLY = [("wk0", P, D), ("wv0", P, D), ("bk0", P, 1), ("wq0x3", P, NG * QROWS), ("bq0x3", QROWS, NG), ("wo0", P, D)]
LATE = [("wqa", P, SH * SD), ("wka", P, SH * SD), ("wva", P, SH * SD), ("proja", P, NP_ * D),
        ("bqa", P, NP_), ("bka", P, NP_), ("bva", P, SH),
        ("w1", P, (E0 + 2) * F0), ("w2", P, E0 * D), ("sdown0", P, D), ("router0", P, E0 + 1)]
CONST = [("ident", P, P), ("avg", P, P), ("sel", P, 2 * AUG), ("fold", P, T), ("hmask", QROWS, HG),
         ("headmask", P, H), ("causal", P, T), ("iota", P, E1), ("cos", T, DH), ("sin", T, DH),
         ("qgb", QROWS, 2), ("kgb", P, 2), ("x", T, D)]
ROWS = [("bv0", T, D), ("bo0", T, D), ("bv1", T, D), ("bp1", T, D), ("bproj1", T, D), ("bqkv1", T, 3 * D)]
SMALL1 = [("wv1", P, D), ("wp1", P, D), ("wproj1", P, D), ("gate1", P, E1)]
RAW1 = [("wk1", P, D), ("wq1", P, D), ("cen", P, P), ("cen3", P, NG * QROWS), ("bk1", P, 1), ("bq1x3", QROWS, NG)]
TAIL1 = [("wqkv1", P, 3 * D), ("sgu1", P, 2 * F1), ("sdown1", P, 2 * D)]
PACKS = {"early": EARLY, "late": LATE, "const": CONST, "rows": ROWS, "small1": SMALL1, "raw1": RAW1, "tail1": TAIL1}


def words(pack):
    return sum(w for _, _, w in PACKS[pack])


NEAR = (3 * S - words("tail1")) // EW
assert (E1 - NEAR) * EW <= words("early") + words("late")


def perceiver(nc, ctxT, packs, experts, out):
    with ExitStack() as ctx:
        def sb(name, shape, dt=F32):
            return ctx.enter_context(nc.sbuf_tensor(name, shape, dt))

        def sem(name):
            return ctx.enter_context(nc.semaphore(name))

        ps = ctx.enter_context(nc.psum_tensor("ps", [P, 8, 512], F32))

        arena = sb("arena", [P, 3 * S])
        ctx_sb, khi, klo = arena[:, 0:S], arena[:, S:2 * S], arena[:, 2 * S:3 * S]
        kst = sb("kst", [P, 2, S], F32R)
        qst = sb("qst", [P, NG, GQ], F32R)
        vaug = sb("vaug", [P, NT, H, AUG])
        prob = sb("prob", [P, 2, BT * GQ])
        w0 = sb("w0", [P, words("early") + words("late")])
        consts = sb("consts", [P, words("const")])
        rows = sb("rows", [T, words("rows")])
        small1 = sb("small1", [P, words("small1")])
        wk1c = sb("wk1c", [P, D])
        wq1c = sb("wq1c", [P, NG * QROWS])
        bk1c = sb("bk1c", [P, 1])
        bq1c = sb("bq1c", [P, NG])
        scratch = sb("scratch", [P, 1024])
        y = sb("y", [T, D])
        yT = sb("yT", [P, T])
        attT = sb("attT", [P, T])
        avsb = sb("avsb", [P, GQ])
        eps_col = sb("eps_col", [P, 1])
        mx = sb("mx", [P, 2, NB])
        mneg = sb("mneg", [P, 2])
        mhl = sb("mhl", [P, 2, 2])
        st6 = sb("st6", [T, 6])
        mv = sb("mv", [T, 2])
        lnv = sb("lnv", [T, 1])
        rstd = sb("rstd", [T, 1])
        stat = sb("stat", [P, 4 * 16])
        idx8 = sb("idx8", [T, 8], U32)

        view = {}
        base = {"early": (w0, 0), "late": (w0, words("early")), "const": (consts, 0), "rows": (rows, 0),
                "small1": (small1, 0), "raw1": (w0, words("early")),
                "tail1": (arena, NEAR * EW)}
        for pack, items in PACKS.items():
            t, at = base[pack]
            for name, r, w in items:
                view[name] = t[0:r, at:at + w]
                at += w
        ident = view["ident"]
        x = view["x"]
        flat = prob.rearrange("p a b -> p (a b)")

        q_a, q_b = scratch[:, 0:256], scratch[:, 256:512]
        sa_q, sa_k, sa_s = flat[:, 0:1024], flat[:, 1024:1536], flat[:, 1536:2048]
        sa_pT, sa_v = flat[:, 0:1024], scratch[:, 0:1024]
        s1_qkv, s1_r = scratch[0:T, 0:3 * D], scratch[0:T, 3 * D:7 * D]
        f0_sig, f0_h = flat[:, 0:(E0 + 1) * T], flat[:, (E0 + 1) * T:2 * (E0 + 1) * T]
        vflat = vaug.rearrange("p t h a -> p (t h a)")
        f1_mask, f1_x, f1_h1 = (vflat[:, k * E1 * T:(k + 1) * E1 * T].rearrange("p (e q) -> p e q", e=E1) for k in range(3))
        f1_he = (f1_x, f1_h1)
        f1_gu, f1_sig, f1_h, f1_hT = flat[:, 0:512], flat[:, 512:768], flat[:, 768:1024], flat[:, 1024:1280]
        y2 = flat[:, 1280:1408]
        f1_bc = flat[0:T, 1408:1664].rearrange("p (k c) -> p k c", k=2)

        def expert(e):
            return arena[:, e * EW:(e + 1) * EW] if e < NEAR else w0[:, (e - NEAR) * EW:(e - NEAR + 1) * EW]

        in_pack = {n: sem("in_" + n) for n in PACKS}
        in_ctx = [sem(f"in_ctx{i}") for i in range(len(CTX_PIECES) - 1)]
        in_stack = [[sem(f"in_stack{s}{k}") for k in range(len(KC))] for s in range(2)]
        in_exp = [sem(f"in_exp{i}") for i in range(3)]
        zeroed = sem("zeroed")
        v_ones = sem("v_ones")
        ones_set = sem("ones_set")
        k_proj = sem("k_proj")
        k_full = sem("k_full")
        k_split = sem("k_split")
        k_sq = sem("k_sq")
        k_var = sem("k_var")
        k_rstd = sem("k_rstd")
        k_scaled = sem("k_scaled")
        k_aff = sem("k_aff")
        v_proj = sem("v_proj")
        v_set = sem("v_set")
        q_ready = sem("q_ready")
        max_made = sem("max_made")
        max_read = sem("max_read")
        shift_cols = sem("shift_cols")
        shift_rows = sem("shift_rows")
        shift_ready = sem("shift_ready")
        scores_done = sem("scores_done")
        exp_done = sem("exp_done")
        av_done = sem("av_done")
        acc_copied = sem("acc_copied")
        o_ready = sem("o_ready")
        dve_step = sem("dve_step")
        act_step = sem("act_step")
        out_stored = sem("out_stored")
        once = {}

        def ev(name):
            if name not in once:
                once[name] = sem(name)
            return once[name]

        block = ctx.enter_context(nc.Block())

        @block.sync
        def _(sp):
            def load(pack):
                t, at = base[pack]
                rmax = max(r for _, r, _ in PACKS[pack])
                sp.dma_start(t[0:rmax, at:at + words(pack)], packs[pack][0:rmax, :]).then_inc(in_pack[pack], 16)

            def stack(l, g, k):
                G = NG * l + g
                b0, b1 = KC[k]
                a, b = b0 * CW, min(b1 * CW, S)
                sp.wait_ge(k_split, l * NB + min(b1, NB))
                if G >= 2:
                    sp.wait_ge(scores_done, NB * (G - 2) + b1)
                for r, src in ((0, khi), (1, khi), (2, klo)):
                    sp.dma_start(kst[r * GC:(r + 1) * GC, G % 2, a:b].bitcast(F32),
                                 src[g * GC:(g + 1) * GC, a:b]).then_inc(in_stack[G % 2][k], 16)

            def load_experts(i, e0, e1):
                t, at = (arena, e0 * EW) if e0 < NEAR else (w0, (e0 - NEAR) * EW)
                sp.dma_start(t[:, at:at + (e1 - e0) * EW], experts[:, e0 * EW:e1 * EW]).then_inc(in_exp[i], 16)

            def ctx_piece(i):
                a, b = CTX_PIECES[i], CTX_PIECES[i + 1]
                sp.dma_start(ctx_sb[:, a:b], ctxT[:, a:b]).then_inc(in_ctx[i], 16)

            load("const")
            load("early")
            for i in range(len(in_ctx)):
                ctx_piece(i)
            for g in range(2):
                for k in range(len(KC)):
                    stack(0, g, k)
                if g == 0:
                    load("rows")
                    load("raw1")
                    load("small1")
            for g in (2, 3):
                for k in range(len(KC)):
                    stack(0, g, k)
            sp.wait_ge(ev("l1_weights"), 1)
            load("late")
            for k in range(len(KC)):
                stack(1, 0, k)
                stack(1, 1, k)
            sp.wait_ge(ev("ffn0_y"), 1)
            load_experts(1, NEAR, E1)
            sp.wait_ge(v_set, 2 * NB)
            first = S // EW
            load_experts(0, 0, first)
            for g in (2, 3):
                for k in range(len(KC)):
                    stack(1, g, k)
            for s in range(2):
                for k in range(len(KC)):
                    sp.wait_ge(in_stack[s][k], 48 * 4)
            load("tail1")
            load_experts(2, first, NEAR)
            sp.wait_ge(ev("out_ready"), 1)
            sp.dma_start(out, x).then_inc(out_stored, 16)
            sp.wait_ge(out_stored, 16)

        @block.gpsimd
        def _(pool):
            nc.gpsimd.memset(vaug[:, :, :, DH], 1.0).then_inc(v_ones, 1)
            pool.wait_ge(v_ones, 1)
            for s in range(2):
                nc.gpsimd.memset(kst[QROWS:P, s, :].bitcast(F32), 1.0).then_inc(ones_set, 1)
                pool.wait_ge(ones_set, s + 1)

            def split(c):
                a, b = c * CW, c * CW + width(c)
                pool.wait_ge(k_full, NB + c + 1)
                nc.gpsimd.tensor_tensor(klo[:, a:b], klo[:, a:b], khi[:, a:b], ALU.subtract).then_inc(k_split, 1)

            pool.wait_ge(av_done, NG * NB)
            nc.gpsimd.memset(flat[:, 0:1024], 0.0).then_inc(ev("qbd_zero"), 1)
            for c in range(NB + 1):
                if c < NB:
                    a, b = c * CW, c * CW + width(c)
                    pool.wait_ge(k_rstd, c + 1)
                    nc.gpsimd.tensor_tensor(klo[:, a:b], klo[:, a:b], khi[:, a:b], ALU.mult).then_inc(k_scaled, 1)
                if c >= 1:
                    split(c - 1)

        @block.scalar
        def _(act):
            n = [0]

            def link(ins):
                n[0] += 1
                ins.then_inc(act_step, 1)
                act.wait_ge(act_step, n[0])

            nc.scalar.preload_act_table_set("natural_log_exp_and_others")

            def v_out(l, c):
                k = tiles(c)
                act.wait_ge(v_proj, l * NB + c + 1)
                nc.scalar.activation(vaug[:, BT * c:BT * c + k, :, 0:DH],
                                     ps[:, 2 + c % 2, 0:k * D].rearrange("p (t h d) -> p t h d", t=k, h=H),
                                     ACT.Copy).then_inc(v_set, 1)

            def keys0(c):
                a, b = c * CW, c * CW + width(c)
                act.wait_ge(k_proj, c + 1)
                nc.scalar.activation(khi[:, a:b].bitcast(F32R), ps[:, c % 2, 0:width(c)], ACT.Identity,
                                     bias=view["bk0"]).then_inc(k_full, 1)

            key_step = [0]

            def key_steps(n):
                for c in range(key_step[0], min(key_step[0] + n, NB + 1)):
                    if c < NB:
                        a, b = c * CW, c * CW + width(c)
                        act.wait_ge(k_proj, NB + c + 1)
                        nc.scalar.activation(klo[:, a:b], ps[:, c % 2, 0:width(c)], ACT.Identity, bias=bk1c[:, 0:1])
                        nc.scalar.activation(khi[:, a:b], ps[:, c % 2, 0:width(c)], ACT.Square,
                                             bias=bk1c[:, 0:1]).then_inc(k_sq, 1)
                    if c >= 1:
                        v = (c - 1) % 2
                        a, b = (c - 1) * CW, (c - 1) * CW + width(c - 1)
                        act.wait_ge(k_var, c)
                        link(nc.scalar.activation(khi[:, a:b], ps[:, 2 + v, 0:b - a], ACT.Ln, bias=eps_col[:, 0:1]))
                        nc.scalar.activation(khi[:, a:b], khi[:, a:b], ACT.Exp, scale=-0.5).then_inc(k_rstd, 1)
                    key_step[0] = c + 1

            def exps(l):
                for g in range(NG):
                    for i in range(NB):
                        B = (NG * l + g) * NB + i
                        act.wait_ge(scores_done, B + 1)
                        if B >= 2:
                            act.wait_ge(av_done, B - 1)
                        w = tiles(i) * GQ
                        b0 = 2 * (B % 2)
                        nc.scalar.activation(prob[:, B % 2, 0:w],
                                             ps[:, b0:b0 + 2, :].rearrange("p a b -> p (a b)")[:, 0:w],
                                             ACT.Exp, scale=XSCALE).then_inc(exp_done, 1)

            def norm_std(tag):
                act.wait_ge(ev(f"{tag}_var"), 1)
                link(nc.scalar.activation(lnv[:, 0:1], mv[:, 1:2], ACT.Ln, bias=eps_col[0:T, 0:1]))
                nc.scalar.activation(rstd[:, 0:1], lnv[:, 0:1], ACT.Exp, scale=-0.5).then_inc(ev(f"{tag}_std"), 1)

            act.wait_ge(ev("eps_set"), 1)
            norm_std("ln0")
            act.wait_ge(in_pack["early"], 16)
            for c in range(-KEYS_AHEAD, NB):
                if c + KEYS_AHEAD < NB:
                    keys0(c + KEYS_AHEAD)
                for v in v_schedule(c):
                    v_out(0, v)
            exps(0)

            act.wait_ge(ev("l1_weights"), 1)
            for s in range(2):
                for k in range(len(KC)):
                    act.wait_ge(in_stack[s][k], 48 * 2)
            key_steps(1)
            norm_std("ln1")
            key_steps(3)
            act.wait_ge(ev("sa0_v"), 1)
            nc.scalar.activation(sa_v[0:T, :], ps[0:T, 4:6, :].rearrange("p a b -> p (a b)"),
                                 ACT.Copy).then_inc(ev("sa0_vs"), 1)
            act.wait_ge(ev("sa0_shifted"), 1)
            nc.scalar.activation(sa_s[:], sa_s[:], ACT.Exp, scale=SD ** -0.5).then_inc(ev("sa0_exp"), 1)
            key_steps(4)

            norm_std("ln2")
            act.wait_ge(ev("ffn0_hidden"), 1)
            nc.scalar.activation(f0_sig[:], ps[:, 4:6, :].rearrange("p a b -> p (a b)")[:, 0:(E0 + 1) * T],
                                 ACT.Exp, scale=-1.0).then_inc(ev("ffn0_sig"), 1)
            act.wait_ge(ev("ffn0_negmax"), 1)
            nc.scalar.activation(stat[0:T, 0:E0], ps[0:T, 6, 0:E0], ACT.Exp, bias=stat[0:T, 8:9],
                                 accum_out=stat[0:T, 9:10])
            nc.scalar.activation(stat[0:T, 10:11], ps[0:T, 6, E0:E0 + 1], ACT.Exp, scale=-1.0).then_inc(ev("ffn0_exp"), 1)

            key_steps(4)
            norm_std("ln3")
            key_steps(NB + 1)
            act.wait_ge(ev("q1_var"), 1)
            link(nc.scalar.activation(q_b[0:QROWS, :], ps[0:QROWS, 6, 256:256 + NG * T], ACT.Ln, bias=eps_col[0:QROWS, 0:1]))
            nc.scalar.activation(q_b[0:QROWS, :], q_b[0:QROWS, :], ACT.Exp, scale=-0.5).then_inc(ev("q1_std"), 1)
            for c in range(NB):
                v_out(1, c)
            exps(1)

            norm_std("ln4")
            act.wait_ge(ev("sa1_shifted"), 1)
            nc.scalar.activation(sa_s[:], sa_s[:], ACT.Exp, scale=DH ** -0.5).then_inc(ev("sa1_exp"), 1)

            norm_std("ln5")
            act.wait_ge(ev("top1"), 1)
            nc.scalar.activation(stat[0:T, 8:9], stat[0:T, 0:1], ACT.Exp, scale=-1.0).then_inc(ev("top1_exp"), 1)
            act.wait_ge(ev("gu_folded"), 1)
            nc.scalar.activation(f1_sig, ps[:, 5, 0:F1], ACT.Exp, scale=-1.0).then_inc(ev("ffn1_sig"), 1)

        @block.vector
        def _(dve):
            n = [0]

            def link(ins):
                n[0] += 1
                ins.then_inc(dve_step, 1)
                dve.wait_ge(dve_step, n[0])

            V = nc.vector

            def norm(tag):
                link(V.bn_stats(st6[:, :], x))
                V.bn_aggr(mv[:, :], st6[:, :]).then_inc(ev(f"{tag}_var"), 1)
                dve.wait_ge(ev(f"{tag}_var"), 1)
                dve.wait_ge(ev(f"{tag}_std"), 1)
                V.tensor_scalar(y[:, :], x, mv[:, 0:1], rstd[:, 0:1], ALU.subtract, ALU.mult).then_inc(ev(f"{tag}_y"), 1)
                dve.wait_ge(ev(f"{tag}_ps"), 1)
                V.tensor_copy(yT[:, :], ps[:, 7, 0:T]).then_inc(ev(f"{tag}_yT"), 1)

            def stack_queries():
                link(V.tensor_copy(q_b[0:QROWS, :].bitcast(F32R), q_a[0:QROWS, :]))
                link(V.tensor_tensor(q_b[GC:2 * GC, :].bitcast(F32R), q_a[GC:2 * GC, :], q_b[GC:2 * GC, :], ALU.subtract))
                qv = q_b[0:QROWS, :].rearrange("p (g q) -> p g q", g=NG)
                for h in range(HG):
                    last = V.tensor_scalar(qst[0:QROWS, :, h * T:(h + 1) * T], qv, view["hmask"][:, h:h + 1], None, ALU.mult)
                last.then_inc(q_ready, 1)

            def max_chunk(G, m):
                k, p = m // 2, m % 2
                dve.wait_ge(max_made, max_count(G) + m + 1)
                V.reduce_max(mx[:, p, k:k + 1], ps[:, 4 + m % 2, 0:width(k)], AX).then_inc(max_read, 1)

            def max_pair(G, k):
                dve.wait_ge(max_made, max_count(G) + k + 1)
                b0 = 4 + 2 * (k % 2)
                V.tensor_reduce(mx[:, :, k], ps[:, b0:b0 + 2, 0:width(k)], AX, ALU.max).then_inc(max_read, 1)

            def shift(G):
                dve.wait_ge(max_read, max_count(G + 1))
                link(V.tensor_reduce(mneg[:, :], mx[:, :, :], AX, ALU.max))
                link(V.tensor_scalar(mneg[:, :], mneg[:, :], -1.0, None, ALU.mult))
                link(V.tensor_copy(mhl[:, :, 0].bitcast(F32R), mneg[:, :]))
                V.tensor_tensor(mhl[:, :, 1].bitcast(F32R), mneg[:, :], mhl[:, :, 0], ALU.subtract).then_inc(shift_cols, 1)

            def shift_in(G):
                dve.wait_ge(shift_rows, G + 1)
                V.tensor_copy(qst[QROWS:KROWS, G % NG, :], ps[QROWS:KROWS, 7, 256:512]).then_inc(shift_ready, 1)

            def copy_acc(G):
                dve.wait_ge(av_done, NB * (G + 1))
                if G >= 1:
                    dve.wait_ge(o_ready, G)
                V.tensor_copy(avsb[:, :], ps[:, 6, 0:GQ]).then_inc(acc_copied, 1)

            key_step = [0]

            def key_steps(n):
                for c in range(key_step[0], min(key_step[0] + n, NB)):
                    a, b = c * CW, c * CW + width(c)
                    dve.wait_ge(k_scaled, c + 1)
                    V.tensor_scalar(klo[:, a:b], klo[:, a:b], view["kgb"][:, 0:1], view["kgb"][:, 1:2],
                                    ALU.mult, ALU.add).then_inc(k_aff, 1)
                    dve.wait_ge(k_aff, c + 1)
                    V.tensor_copy(khi[:, a:b].bitcast(F32R), klo[:, a:b]).then_inc(k_full, 1)
                    key_step[0] = c + 1

            def split(c):
                a, b = c * CW, c * CW + width(c)
                dve.wait_ge(k_full, c + 1)
                V.scalar_tensor_tensor(klo[:, a:b], ps[:, c % 2, 0:width(c)], view["bk0"], khi[:, a:b],
                                       ALU.add, ALU.subtract).then_inc(k_split, 1)

            def cross(l):
                G0 = NG * l
                for k in range(NB):
                    if l == 0 and k + KEYS_AHEAD < NB:
                        split(k + KEYS_AHEAD)
                    max_pair(G0, k)
                shift(G0)
                shift_in(G0)
                for G, m in max_stream(G0, 0, LEAD):
                    max_chunk(G, m)
                for g in range(NG):
                    for i in range(NB):
                        n = LEAD + 2 * (g * NB + i)
                        for j in range(2):
                            for G, m in max_stream(G0, n + j, n + j + 1):
                                max_chunk(G, m)
                                if m == MAXN - 1:
                                    shift(G)
                                    shift_in(G)
                            if i == 0 and g >= 1 and j == 0:
                                copy_acc(G0 + g - 1)
                        G = G0 + g
                        if G == 0 and i == 1:
                            dve.wait_ge(ev("l1_wkps"), 1)
                            V.tensor_copy(wk1c[:, :], ps[:, 7, 0:D])
                            V.tensor_copy(bk1c[:, :], ps[:, 7, D:D + 1])
                            V.tensor_copy(bq1c[0:QROWS, :], ps[0:QROWS, 7, D + 1:D + 1 + NG]).then_inc(ev("l1_wk"), 1)
                        if G == 0 and i == 4:
                            dve.wait_ge(ev("l1_wqps"), 1)
                            V.tensor_copy(wq1c[:, :], ps[:, 7, 0:NG * QROWS]).then_inc(ev("l1_weights"), 1)
                copy_acc(G0 + NG - 1)

            def cross_out(l, bv, bo, tag):
                dve.wait_ge(o_ready, NG * (l + 1))
                o = ps[0:T, 7, 0:H * AUG].rearrange("p (h a) -> p h a", a=AUG)
                link(V.reciprocal(stat[0:T, 0:H], o[:, :, DH]))
                att = y[:, :].rearrange("p (h a) -> p h a", a=DH)
                link(V.tensor_tensor(att, o[:, :, 0:DH], stat[0:T, 0:H].unsqueeze(2).to_broadcast([T, H, DH]), ALU.mult))
                V.tensor_tensor(y[:, :], y[:, :], bv, ALU.add).then_inc(ev(f"{tag}_att"), 1)
                link(V.tensor_tensor(x, x, bo, ALU.add))
                dve.wait_ge(ev(f"{tag}_attps"), 1)
                V.tensor_copy(attT[:, :], ps[:, 6, 0:T]).then_inc(ev(f"{tag}_attT"), 1)
                dve.wait_ge(ev(f"{tag}_proj"), 1)
                link(V.tensor_tensor(x, ps[0:T, 6, 128:256], x, ALU.add))

            def softmax(tag, bnk):
                s3 = sa_s[:].rearrange("p (j k) -> p j k", k=T)
                mask = view["causal"].unsqueeze(1).to_broadcast([P, 8, T])
                dve.wait_ge(ev(f"{tag}_scores"), 1)
                link(V.tensor_tensor(s3, ps[:, bnk, :].rearrange("p (j k) -> p j k", k=T), mask, ALU.add))
                link(V.tensor_reduce(stat[:, 0:8], s3, AX, ALU.max))
                V.tensor_tensor(s3, s3, stat[:, 0:8].unsqueeze(2).to_broadcast([P, 8, T]),
                                ALU.subtract).then_inc(ev(f"{tag}_shifted"), 1)
                dve.wait_ge(ev(f"{tag}_exp"), 1)
                link(V.tensor_reduce(stat[:, 8:16], s3, AX, ALU.add))
                link(V.reciprocal(stat[:, 8:16], stat[:, 8:16]))
                V.tensor_tensor(s3, s3, stat[:, 8:16].unsqueeze(2).to_broadcast([P, 8, T]),
                                ALU.mult).then_inc(ev(f"{tag}_probs"), 1)
                dve.wait_ge(ev(f"{tag}_pT"), 1)
                V.tensor_copy(sa_pT[0:T, :], ps[0:T, 4:6, :].rearrange("p a b -> p (a b)")).then_inc(ev(f"{tag}_pTs"), 1)

            V.memset(eps_col[:, :], EPS).then_inc(ev("eps_set"), 1)
            V.memset(ps[:, 6, :], 0.0).then_inc(zeroed, 1)
            V.memset(qst[QROWS:P, :, :].bitcast(F32), 0.0)
            dve.wait_ge(in_pack["const"], 16)
            norm("ln0")
            dve.wait_ge(in_pack["early"], 16)
            split(0)
            split(1)
            dve.wait_ge(ev("q0_ps"), 1)
            link(V.tensor_tensor(q_a[0:QROWS, :].rearrange("p (g q) -> p g q", g=NG),
                                 ps[0:QROWS, 6, 256:256 + NG * T].rearrange("p (g q) -> p g q", g=NG),
                                 view["bq0x3"].unsqueeze(2).to_broadcast([QROWS, NG, T]), ALU.add))
            stack_queries()
            for c in range(2, KEYS_AHEAD):
                split(c)
            cross(0)
            dve.wait_ge(in_pack["rows"], 16)
            cross_out(0, view["bv0"], view["bo0"], "x0")

            norm("ln1")
            dve.wait_ge(ev("qbd_zero"), 1)
            dve.wait_ge(ev("sa0_q"), 1)
            q3 = sa_q[:].rearrange("p (j c) -> p j c", j=NP_)
            for hh in range(2):
                r = slice(64 * hh, 64 * hh + 64)
                V.tensor_tensor(q3[r, :, r], ps[r, 4, :].rearrange("p (j q) -> p j q", q=T),
                                view["bqa"][r].unsqueeze(2).to_broadcast([64, NP_, T]), ALU.add)
            V.tensor_tensor(sa_k[:].rearrange("p (j q) -> p j q", q=T), ps[:, 5, :].rearrange("p (j q) -> p j q", q=T),
                            view["bka"].unsqueeze(2).to_broadcast([P, NP_, T]), ALU.add).then_inc(ev("sa0_qk"), 1)
            key_steps(2)
            softmax("sa0", 6)
            key_steps(3)
            dve.wait_ge(ev("sa0_z"), 1)
            V.tensor_tensor(sa_k[:].rearrange("p (h q) -> p h q", h=SH), ps[:, 6, :].rearrange("p (h q) -> p h q", h=SH),
                            view["bva"].unsqueeze(2).to_broadcast([P, SH, T // 2]), ALU.add).then_inc(ev("sa0_zT"), 1)
            dve.wait_ge(ev("sa0_proj"), 1)
            link(V.scalar_tensor_tensor(x, ps[0:T, 7, 0:D], SD ** -0.5, x, ALU.mult, ALU.add))

            norm("ln2")
            key_steps(2)
            dve.wait_ge(ev("ffn0_hidden"), 1)
            lg = stat[0:T, 16:16 + E0]
            link(V.tensor_copy(lg, ps[0:T, 6, 0:E0]))
            link(V.max(stat[0:T, 24:32], lg))
            V.tensor_scalar(stat[0:T, 8:9], stat[0:T, 24:25], -1.0, None, ALU.mult).then_inc(ev("ffn0_negmax"), 1)
            link(V.max_index(idx8[:, :], stat[0:T, 24:32], lg))
            link(V.tensor_copy(stat[0:T, 32:40], idx8[:, :]))
            link(V.tensor_scalar(stat[0:T, 40:48], view["iota"][0:T, 0:E0], stat[0:T, 32:33], None, ALU.is_equal))
            link(V.scalar_tensor_tensor(stat[0:T, 40:48], view["iota"][0:T, 0:E0], stat[0:T, 33:34], stat[0:T, 40:48],
                                        ALU.is_equal, ALU.add))
            dve.wait_ge(ev("ffn0_exp"), 1)
            link(V.reciprocal(stat[0:T, 9:10], stat[0:T, 9:10]))
            link(V.scalar_tensor_tensor(stat[0:T, 48:56], stat[0:T, 0:E0], stat[0:T, 9:10], stat[0:T, 40:48],
                                        ALU.mult, ALU.mult))
            link(V.tensor_scalar(stat[0:T, 10:11], stat[0:T, 10:11], 1.0, None, ALU.add))
            link(V.reciprocal(stat[0:T, 10:11], stat[0:T, 10:11]))
            dve.wait_ge(ev("ffn0_sig"), 1)
            link(V.tensor_scalar(f0_sig[:], f0_sig[:], 1.0, None, ALU.add))
            link(V.reciprocal(f0_sig[:], f0_sig[:]))
            hid = ps[:, 4:6, :].rearrange("p a b -> p (a b)")
            link(V.tensor_tensor(f0_h[:], hid[:, 0:(E0 + 1) * T], f0_sig[:], ALU.mult))
            V.tensor_tensor(f0_h[:, E0 * T:(E0 + 1) * T], hid[:, (E0 + 1) * T:(E0 + 2) * T], f0_h[:, E0 * T:(E0 + 1) * T],
                            ALU.mult).then_inc(ev("ffn0_h"), 1)
            key_steps(2)
            dve.wait_ge(ev("ffn0_y"), 1)
            ye = ps[0:T, 4:6, :].rearrange("p a (e d) -> p (a e) d", d=D)
            for e in range(E0):
                link(V.scalar_tensor_tensor(x, ye[:, e, :], stat[0:T, 48 + e:49 + e], x, ALU.mult, ALU.add))
            link(V.scalar_tensor_tensor(x, ps[0:T, 7, 0:D], stat[0:T, 10:11], x, ALU.mult, ALU.add))

            norm("ln3")
            V.memset(qst[QROWS:P, :, :].bitcast(F32), 0.0)
            dve.wait_ge(ev("q1_ps"), 1)
            qa3 = q_a[0:QROWS, :].rearrange("p (g q) -> p g q", g=NG)
            link(V.tensor_tensor(qa3, ps[0:QROWS, 6, 0:NG * T].rearrange("p (g q) -> p g q", g=NG),
                                 bq1c[0:QROWS, :].unsqueeze(2).to_broadcast([QROWS, NG, T]), ALU.add))
            V.tensor_tensor(q_b[0:QROWS, :], q_a[0:QROWS, :], q_a[0:QROWS, :], ALU.mult).then_inc(ev("q1_sq"), 1)
            dve.wait_ge(ev("q1_std"), 1)
            link(V.tensor_tensor(q_a[0:QROWS, :], q_a[0:QROWS, :], q_b[0:QROWS, :], ALU.mult))
            link(V.tensor_scalar(q_a[0:QROWS, :], q_a[0:QROWS, :], view["qgb"][:, 0:1], view["qgb"][:, 1:2],
                                 ALU.mult, ALU.add))
            stack_queries()
            key_steps(NB)
            cross(1)
            cross_out(1, view["bv1"], view["bp1"], "x1")

            norm("ln4")
            dve.wait_ge(ev("sa1_qkv"), 1)
            link(V.tensor_tensor(s1_qkv, ps[0:T, 4, 0:3 * D], view["bqkv1"], ALU.add))
            qk = s1_qkv[:, 0:2 * D].rearrange("p (h a) -> p h a", a=DH)
            r1 = s1_r[:, 0:2 * D].rearrange("p (h a) -> p h a", a=DH)
            r2 = s1_r[:, 2 * D:4 * D].rearrange("p (h a) -> p h a", a=DH)
            half = DH // 2
            V.tensor_tensor(r1, qk, view["cos"].unsqueeze(1).to_broadcast([T, 2 * H, DH]), ALU.mult)
            V.tensor_tensor(r2[:, :, 0:half], qk[:, :, half:DH],
                            view["sin"][:, 0:half].unsqueeze(1).to_broadcast([T, 2 * H, half]), ALU.mult)
            link(V.tensor_tensor(r2[:, :, half:DH], qk[:, :, 0:half],
                                 view["sin"][:, half:DH].unsqueeze(1).to_broadcast([T, 2 * H, half]), ALU.mult))
            V.tensor_tensor(s1_r[:, 0:2 * D], s1_r[:, 0:2 * D], s1_r[:, 2 * D:4 * D], ALU.add).then_inc(ev("sa1_rope"), 1)
            link(V.tensor_tensor(x, x, view["bproj1"], ALU.add))
            dve.wait_ge(ev("sa1_qkT"), 1)
            V.tensor_copy(attT[:, :], ps[:, 7, 0:T])
            V.tensor_tensor(sa_q[:].rearrange("p (h k) -> p h k", k=T),
                            ps[:, 7, T:2 * T].unsqueeze(1).to_broadcast([P, H, T]),
                            view["headmask"].unsqueeze(2).to_broadcast([P, H, T]), ALU.mult).then_inc(ev("sa1_qk"), 1)
            softmax("sa1", 6)
            dve.wait_ge(ev("sa1_av"), 1)
            V.tensor_copy(y[:, :], ps[0:T, 7, 0:D]).then_inc(ev("sa1_o"), 1)
            dve.wait_ge(ev("sa1_oT"), 1)
            V.tensor_copy(attT[:, :], ps[:, 6, 0:T]).then_inc(ev("sa1_oTs"), 1)
            dve.wait_ge(ev("sa1_proj"), 1)
            link(V.tensor_tensor(x, ps[0:T, 6, 128:256], x, ALU.add))

            norm("ln5")
            dve.wait_ge(ev("ffn1_logits"), 1)
            lg = stat[0:T, 16:16 + E1]
            link(V.tensor_copy(lg, ps[0:T, 6, 0:E1]))
            V.max(stat[0:T, 0:8], lg).then_inc(ev("top1"), 1)
            dve.wait_ge(ev("top1"), 1)
            link(V.max_index(idx8[:, :], stat[0:T, 0:8], lg))
            link(V.tensor_copy(stat[0:T, 9:10], idx8[:, 0:1]))
            dve.wait_ge(ev("top1_exp"), 1)
            link(V.tensor_scalar(stat[0:T, 10:11], stat[0:T, 8:9], 1.0, None, ALU.add))
            link(V.reciprocal(stat[0:T, 10:11], stat[0:T, 10:11]))
            link(V.memset(f1_bc[:, :, :], 0.0))
            V.tensor_scalar(f1_bc[:, 0, :], f1_bc[:, 0, :], stat[0:T, 9:10], None, ALU.add)
            V.tensor_scalar(f1_bc[:, 1, :], f1_bc[:, 1, :], stat[0:T, 10:11], None, ALU.add).then_inc(ev("ffn1_bc"), 1)
            dve.wait_ge(ev("ffn1_bcps"), 1)
            link(V.tensor_tensor(attT[:, :], ps[:, 7, T:2 * T], yT[:, :], ALU.mult))
            EC = 8
            for c in range(E1 // EC):
                es = slice(c * EC, (c + 1) * EC)
                link(V.tensor_tensor(f1_mask[:, es, :], ps[:, 7, 0:T].unsqueeze(1).to_broadcast([P, EC, T]),
                                     view["iota"][:, es].unsqueeze(2).to_broadcast([P, EC, T]), ALU.is_equal))
                V.tensor_tensor(f1_x[:, es, :], f1_mask[:, es, :], attT[:, :].unsqueeze(1).to_broadcast([P, EC, T]),
                                ALU.mult).then_inc(ev("ffn1_x"), 1)
            dve.wait_ge(ev("ffn1_gu"), 1)
            V.tensor_copy(f1_gu, ps[:, 4, :]).then_inc(ev("ffn1_gus"), 1)
            dve.wait_ge(ev("ffn1_sig"), 1)
            link(V.tensor_scalar(f1_sig, f1_sig, 1.0, None, ALU.add))
            link(V.reciprocal(f1_sig, f1_sig))
            link(V.tensor_tensor(f1_sig, ps[:, 5, 0:F1], f1_sig, ALU.mult))
            V.tensor_tensor(f1_h, ps[:, 5, F1:2 * F1], f1_sig, ALU.mult).then_inc(ev("ffn1_h"), 1)
            dve.wait_ge(ev("ffn1_hT"), 1)
            link(V.tensor_copy(f1_hT, ps[:, 6, 0:2 * P]))
            for c in range(E1 // EC):
                es = slice(c * EC, (c + 1) * EC)
                for k in range(2):
                    last = V.tensor_tensor(f1_he[k][:, es, :], f1_mask[:, es, :],
                                           f1_hT[:, k * P + T:(k + 1) * P].unsqueeze(1).to_broadcast([P, EC, T]), ALU.mult)
                last.then_inc(ev("ffn1_he"), 1)
            dve.wait_ge(ev("ffn1_d"), 1)
            V.tensor_copy(y2, ps[:, 4, 0:D]).then_inc(ev("ffn1_ds"), 1)
            dve.wait_ge(ev("ffn1_out"), 1)
            V.tensor_tensor(x, ps[0:T, 5, 0:D], x, ALU.add).then_inc(ev("out_ready"), 1)

        @block.tensor
        def _(pe):
            mm = nc.tensor.matmul

            def one(out_, lhsT, rhs, start=True, stop=True):
                return mm(out_, lhsT, rhs, start=start, stop=stop, skip_group_check=True)

            key_step = [0]

            def key_steps(n):
                for c in range(key_step[0], min(key_step[0] + n, NB + 1)):
                    if c < NB:
                        key_chunk(1, c, wk1c[:, :])
                    if c >= 1:
                        var_chunk(c - 1)
                    key_step[0] = c + 1

            def yT_of(tag, steps=0):
                key_steps(steps)
                pe.wait_ge(ev(f"{tag}_y"), 1)
                nc.tensor.transpose(ps[:, 7, 0:T], y[:, :], ident[0:T, 0:T]).then_inc(ev(f"{tag}_ps"), 1)
                pe.wait_ge(ev(f"{tag}_yT"), 1)

            def key_chunk(l, c, w):
                a, b = c * CW, c * CW + width(c)
                if l == 0:
                    for i in range(len(in_ctx)):
                        if CTX_PIECES[i] <= a < CTX_PIECES[i + 1]:
                            pe.wait_ge(in_ctx[i], 16)
                if c >= 2:
                    pe.wait_ge(k_split if l == 0 else k_sq, c - 1)
                one(ps[:, c % 2, 0:width(c)], w, ctx_sb[:, a:b]).then_inc(k_proj, 1)

            def var_chunk(c):
                a, b = c * CW, c * CW + width(c)
                pe.wait_ge(k_sq, c + 1)
                if c >= 2:
                    pe.wait_ge(k_rstd, c - 1)
                one(ps[:, 2 + c % 2, 0:width(c)], view["avg"], khi[:, a:b]).then_inc(k_var, 1)

            def v_chunk(l, c, w):
                if c >= 2:
                    pe.wait_ge(v_set, l * NB + c - 1)
                for t in range(tiles(c)):
                    for hh in range(2):
                        a = (BT * c + t) * P + 64 * hh
                        last = one(ps[64 * hh:64 * hh + 64, 2 + c % 2, t * D:(t + 1) * D], ctx_sb[:, a:a + 64], w)
                last.then_inc(v_proj, 1)

            def stack_there(G, k):
                for j, (b0, b1) in enumerate(KC):
                    if b0 == k:
                        pe.wait_ge(in_stack[G % 2][j], 48 * (G // 2 + 1))

            def max_scores(G, k, p, bnk):
                a, b = k * CW, k * CW + width(k)
                return one(ps[:, bnk, 0:width(k)], qst[:, G % NG, p * P:(p + 1) * P], kst[:, G % 2, a:b])

            def max_chunk(G, m):
                k, p = m // 2, m % 2
                if p == 0:
                    stack_there(G, k)
                first = G % NG == 1 and m < 2
                pe.wait_ge(max_read, max_count(G) + (0 if first else m - 1))
                max_scores(G, k, p, 4 + m % 2).then_inc(max_made, 1)

            def max_pair(G, k):
                stack_there(G, k)
                if k >= 2:
                    pe.wait_ge(max_read, max_count(G) + k - 1)
                for p in range(2):
                    last = max_scores(G, k, p, 4 + 2 * (k % 2) + p)
                last.then_inc(max_made, 1)

            def shift(G):
                pe.wait_ge(shift_cols, G + 1)
                for p in range(2):
                    last = one(ps[QROWS:KROWS, 7, 256 + p * P:256 + (p + 1) * P], mhl[:, p, :], ident)
                last.then_inc(shift_rows, 1)

            def scores(G, i):
                B = NB * G + i
                if i == 0:
                    pe.wait_ge(shift_ready, G + 1)
                if B % (NG * NB) >= 2:
                    pe.wait_ge(exp_done, B - 1)
                dst = ps[:, 2 * (B % 2):2 * (B % 2) + 2, :].rearrange("p a b -> p (a b)")
                for t in range(tiles(i)):
                    a = (BT * i + t) * P
                    last = one(dst[:, t * GQ:(t + 1) * GQ], kst[:, G % 2, a:a + P], qst[:, G % NG, :])
                last.then_inc(scores_done, 1)

            def weighted(G, i):
                B = NB * G + i
                g = G % NG
                pe.wait_ge(exp_done, B + 1)
                if i == 0 and G >= 1:
                    pe.wait_ge(acc_copied, G)
                for t in range(tiles(i)):
                    for p in range(2):
                        h = HG * g + 2 * p
                        last = one(ps[32 * t:32 * t + 2 * AUG, 6, p * P:(p + 1) * P],
                                   vaug[:, BT * i + t, h:h + 2, :].rearrange("p h a -> p (h a)"),
                                   prob[:, B % 2, t * GQ + p * P:t * GQ + (p + 1) * P],
                                   start=(i == 0 and p == 0), stop=(i == NB - 1))
                last.then_inc(av_done, 1)

            def gather(G):
                g = G % NG
                pe.wait_ge(acc_copied, G + 1)
                for h in range(HG):
                    c = (HG * g + h) * AUG
                    last = one(ps[0:T, 7, c:c + AUG], avsb[:, h * T:(h + 1) * T],
                               view["sel"][:, (h % 2) * AUG:(h % 2 + 1) * AUG])
                last.then_inc(o_ready, 1)

            def cross(l):
                G0 = NG * l
                shift(G0)
                for Gm, m in max_stream(G0, 0, LEAD):
                    max_chunk(Gm, m)
                for g in range(NG):
                    G = G0 + g
                    for i in range(NB):
                        n = LEAD + 2 * (g * NB + i)
                        scores(G, i)
                        for Gm, m in max_stream(G0, n, n + 1):
                            max_chunk(Gm, m)
                        if i >= 1:
                            weighted(G, i - 1)
                        elif g >= 1:
                            weighted(G - 1, NB - 1)
                        for Gm, m in max_stream(G0, n + 1, n + 2):
                            max_chunk(Gm, m)
                        if i == SHIFT_AT and g + 1 < NG:
                            shift(G + 1)
                        if i == 3 and g >= 1:
                            gather(G - 1)
                        if G == 0 and i == 0:
                            pe.wait_ge(in_pack["raw1"], 16)
                            one(ps[:, 7, 0:D], view["wk1"], view["cen"])
                            one(ps[:, 7, D:D + 1], view["cen"], view["bk1"])
                            one(ps[0:QROWS, 7, D + 1:D + 1 + NG], view["cen"][0:QROWS, 0:QROWS],
                                view["bq1x3"]).then_inc(ev("l1_wkps"), 1)
                        if G == 0 and i == 3:
                            pe.wait_ge(ev("l1_wk"), 1)
                            one(ps[:, 7, 0:NG * QROWS], view["wq1"], view["cen3"]).then_inc(ev("l1_wqps"), 1)
                weighted(G0 + NG - 1, NB - 1)
                gather(G0 + NG - 1)

            def cross_out(w, tag):
                pe.wait_ge(ev(f"{tag}_att"), 1)
                nc.tensor.transpose(ps[:, 6, 0:T], y[:, :], ident[0:T, 0:T]).then_inc(ev(f"{tag}_attps"), 1)
                pe.wait_ge(ev(f"{tag}_attT"), 1)
                one(ps[0:T, 6, 128:256], attT[:, :], w).then_inc(ev(f"{tag}_proj"), 1)

            def turn_probs(tag, steps=0):
                pe.wait_ge(ev(f"{tag}_probs"), 1)
                pt = ps[0:T, 4:6, :].rearrange("p a b -> p (a b)")
                for j in range(8):
                    last = nc.tensor.transpose(pt[:, j * P:(j + 1) * P], sa_s[:, j * T:(j + 1) * T], ident)
                last.then_inc(ev(f"{tag}_pT"), 1)
                key_steps(steps)
                pe.wait_ge(ev(f"{tag}_pTs"), 1)

            pe.wait_ge(in_pack["const"], 16)
            yT_of("ln0")
            pe.wait_ge(in_pack["early"], 16)
            key_chunk(0, 0, view["wk0"])
            key_chunk(0, 1, view["wk0"])
            pe.wait_ge(zeroed, 1)
            for g in range(NG):
                last = one(ps[0:QROWS, 6, 256 + g * T:256 + (g + 1) * T], view["wq0x3"][:, g * QROWS:(g + 1) * QROWS], yT[:, :])
            last.then_inc(ev("q0_ps"), 1)
            for c in range(2, KEYS_AHEAD):
                key_chunk(0, c, view["wk0"])
            for c in range(NB):
                if c + KEYS_AHEAD < NB:
                    key_chunk(0, c + KEYS_AHEAD, view["wk0"])
                if c == 0:
                    pe.wait_ge(q_ready, 1)
                    pe.wait_ge(ones_set, 1)
                max_pair(0, c)
                for v in v_schedule(c):
                    v_chunk(0, v, view["wv0"])
            pe.wait_ge(v_set, NB)
            pe.wait_ge(v_ones, 1)
            pe.wait_ge(ones_set, 2)
            cross(0)
            key_steps(2)
            cross_out(view["wo0"], "x0")

            yT_of("ln1", 1)
            pe.wait_ge(in_pack["late"], 16)
            for w, bnk in (("wqa", 4), ("wka", 5)):
                for h in range(SH):
                    last = one(ps[64 * (h % 2):64 * (h % 2) + 64, bnk, (h // 2) * T:(h // 2 + 1) * T],
                               view[w][:, h * SD:(h + 1) * SD], yT[:, :])
            last.then_inc(ev("sa0_q"), 1)
            key_steps(1)
            pe.wait_ge(ev("sa0_qk"), 1)
            for j in range(NP_):
                last = one(ps[:, 6, j * T:(j + 1) * T], sa_q[:, j * P:(j + 1) * P], sa_k[:, j * T:(j + 1) * T])
            last.then_inc(ev("sa0_scores"), 1)
            for k in range(2):
                last = one(ps[0:T, 4 + k, :], yT[:, :], view["wva"][:, k * 512:(k + 1) * 512])
            last.then_inc(ev("sa0_v"), 1)
            key_steps(2)
            pe.wait_ge(ev("sa0_vs"), 1)
            turn_probs("sa0", 1)
            for h in range(SH):
                for u in range(2):
                    q0 = (h // 2) * P + (h % 2) * T
                    last = one(ps[64 * u:64 * u + 64, 6, h * (T // 2):(h + 1) * (T // 2)],
                               sa_v[0:T, h * SD:(h + 1) * SD], sa_pT[0:T, q0 + u:q0 + T:2])
            last.then_inc(ev("sa0_z"), 1)
            key_steps(1)
            pe.wait_ge(ev("sa0_zT"), 1)
            zT = sa_k[:].rearrange("p (s r) -> p r s", r=NP_)
            for r in range(NP_):
                last = one(ps[0:T, 7, 0:D], zT[:, r, :], view["proja"][:, r * D:(r + 1) * D],
                           start=(r == 0), stop=(r == NP_ - 1))
            last.then_inc(ev("sa0_proj"), 1)

            yT_of("ln2", 1)
            one(ps[0:T, 6, 0:E0 + 1], yT[:, :], view["router0"])
            hid = ps[:, 4:6, :].rearrange("p a b -> p (a b)")
            for e in range(E0 + 2):
                last = one(hid[:, e * T:(e + 1) * T], view["w1"][:, e * F0:(e + 1) * F0], yT[:, :])
            last.then_inc(ev("ffn0_hidden"), 1)
            key_steps(3)
            pe.wait_ge(ev("ffn0_h"), 1)
            for e in range(E0):
                one(ps[0:T, 4 + e // 4, (e % 4) * D:(e % 4 + 1) * D], f0_h[:, e * T:(e + 1) * T],
                    view["w2"][:, e * D:(e + 1) * D])
            one(ps[0:T, 7, 0:D], f0_h[:, E0 * T:(E0 + 1) * T], view["sdown0"]).then_inc(ev("ffn0_y"), 1)

            yT_of("ln3", 3)
            for g in range(NG):
                last = one(ps[0:QROWS, 6, g * T:(g + 1) * T], wq1c[:, g * QROWS:(g + 1) * QROWS], yT[:, :])
            last.then_inc(ev("q1_ps"), 1)
            pe.wait_ge(ev("q1_sq"), 1)
            one(ps[0:QROWS, 6, 256:256 + NG * T], view["avg"][0:QROWS, 0:QROWS], q_b[0:QROWS, :]).then_inc(ev("q1_var"), 1)
            pe.wait_ge(k_rstd, NB)
            pe.wait_ge(in_pack["small1"], 16)
            v_chunk(1, 0, view["wv1"])
            v_chunk(1, 1, view["wv1"])
            pe.wait_ge(q_ready, 2)
            for c in range(NB):
                max_pair(NG, c)
                if c + 2 < NB:
                    v_chunk(1, c + 2, view["wv1"])
            pe.wait_ge(v_set, 2 * NB)
            cross(1)
            cross_out(view["wp1"], "x1")

            yT_of("ln4")
            pe.wait_ge(in_pack["tail1"], 16)
            one(ps[0:T, 4, 0:3 * D], yT[:, :], view["wqkv1"]).then_inc(ev("sa1_qkv"), 1)
            pe.wait_ge(ev("sa1_rope"), 1)
            for k in range(2):
                last = nc.tensor.transpose(ps[:, 7, k * T:(k + 1) * T], s1_r[:, k * D:(k + 1) * D], ident[0:T, 0:T])
            last.then_inc(ev("sa1_qkT"), 1)
            pe.wait_ge(ev("sa1_qk"), 1)
            for hh in range(2):
                last = one(ps[64 * hh:64 * hh + 64, 6, :], attT[:, :], sa_q[:, hh * 512:(hh + 1) * 512])
            last.then_inc(ev("sa1_scores"), 1)
            turn_probs("sa1")
            for h in range(H):
                hh, j = h // 8, h % 8
                last = one(ps[0:T, 7, h * DH:(h + 1) * DH], sa_pT[0:T, j * P + hh * T:j * P + hh * T + T],
                           s1_qkv[:, 2 * D + h * DH:2 * D + (h + 1) * DH])
            last.then_inc(ev("sa1_av"), 1)
            pe.wait_ge(ev("sa1_o"), 1)
            nc.tensor.transpose(ps[:, 6, 0:T], y[:, :], ident[0:T, 0:T]).then_inc(ev("sa1_oT"), 1)
            pe.wait_ge(ev("sa1_oTs"), 1)
            one(ps[0:T, 6, 128:256], attT[:, :], view["wproj1"]).then_inc(ev("sa1_proj"), 1)

            yT_of("ln5")
            one(ps[0:T, 6, 0:E1], yT[:, :], view["gate1"]).then_inc(ev("ffn1_logits"), 1)
            one(ps[0:T, 5, :], yT[:, :], view["sgu1"])
            pe.wait_ge(ev("ffn1_bc"), 1)
            for k in range(2):
                last = one(ps[:, 7, k * T:(k + 1) * T], f1_bc[:, k, :], ident[0:T, 0:T])
            last.then_inc(ev("ffn1_bcps"), 1)
            for s in in_exp:
                pe.wait_ge(s, 16)
            for e in range(E1):
                if e % 8 == 0:
                    pe.wait_ge(ev("ffn1_x"), e // 8 + 1)
                o = 64 * (e % 2)
                last = one(ps[o:o + 64, 4, :], f1_x[:, e, :], expert(e)[:, 0:2 * F1], start=(e < 2), stop=(e >= E1 - 2))
            last.then_inc(ev("ffn1_gu"), 1)
            pe.wait_ge(ev("ffn1_gus"), 1)
            one(ps[64:128, 5, :], view["fold"], f1_gu).then_inc(ev("gu_folded"), 1)
            pe.wait_ge(ev("ffn1_h"), 1)
            for k in range(2):
                last = nc.tensor.transpose(ps[:, 6, k * P:(k + 1) * P], f1_h[:, k * P:(k + 1) * P], ident)
            last.then_inc(ev("ffn1_hT"), 1)
            pe.wait_ge(ev("ffn1_he"), 1)
            for k in range(2):
                one(ps[64 * k:64 * k + 64, 4, 0:D], f1_hT[:, k * P:k * P + T], view["sdown1"][:, k * D:(k + 1) * D],
                    start=True, stop=False)
            for e in range(E1):
                if e % 8 == 0:
                    pe.wait_ge(ev("ffn1_he"), e // 8 + 1)
                for k in range(2):
                    last = one(ps[64 * k:64 * k + 64, 4, 0:D], f1_he[k][:, e, :],
                               expert(e)[:, 2 * F1 + k * D:2 * F1 + (k + 1) * D], start=False, stop=(e == E1 - 1))
            last.then_inc(ev("ffn1_d"), 1)
            pe.wait_ge(ev("ffn1_ds"), 1)
            one(ps[0:T, 5, 0:D], view["fold"], y2).then_inc(ev("ffn1_out"), 1)


def _constants():
    c = {}
    head = np.arange(P) // DH
    same = (head[:, None] == head[None, :]).astype(np.float32) / DH
    cen = np.eye(P, dtype=np.float32) - same
    c["ident"] = np.eye(P, dtype=np.float32)
    c["avg"] = same
    c["cen"] = cen
    c["cen3"] = np.concatenate([np.tile(cen[:, g * GC:(g + 1) * GC], (1, 3)) for g in range(NG)], axis=1)
    r = np.arange(P) % 32
    c["sel"] = (r[:, None] == np.arange(2 * AUG)[None, :]).astype(np.float32)
    c["fold"] = (np.arange(P)[:, None] % T == np.arange(T)[None, :]).astype(np.float32)
    c["hmask"] = ((np.arange(QROWS)[:, None] % GC) // DH == np.arange(HG)[None, :]).astype(np.float32)
    c["headmask"] = (head[:, None] == np.arange(H)[None, :]).astype(np.float32)
    q, k = np.arange(P)[:, None] % T, np.arange(T)[None, :]
    c["causal"] = np.where(k > q, np.float32(-1e30), np.float32(0)).astype(np.float32)
    c["iota"] = np.tile(np.arange(E1, dtype=np.float32), (P, 1))
    half = DH // 2
    freqs = np.float32(1.0) / np.float32(10000.0) ** (np.arange(half, dtype=np.float32) / np.float32(half))
    angle = np.arange(T, dtype=np.float32)[:, None] * freqs[None, :].astype(np.float32)
    cos, sin = np.cos(angle).astype(np.float32), np.sin(angle).astype(np.float32)
    c["cos"] = np.concatenate([cos, cos], axis=1)
    c["sin"] = np.concatenate([-sin, sin], axis=1)
    return c


def _blocks(w, n):
    return w.reshape(n, P, -1).transpose(1, 0, 2).reshape(P, -1)


def _layout(i):
    a = dict(_constants())
    rep = lambda v: np.broadcast_to(v[None, :], (T, v.shape[0]))
    g3 = lambda w: np.concatenate([np.tile(w[:, g * GC:(g + 1) * GC], (1, 3)) for g in range(NG)], axis=1)
    b3 = lambda b: np.tile(b.reshape(NG, GC).T, (3, 1))
    a["wk0"], a["wv0"], a["wo0"] = i["L0_xattn_Wk"], i["L0_xattn_Wv"], i["L0_xattn_Wo"]
    a["wq0x3"], a["bq0x3"] = g3(i["L0_xattn_Wq"]), b3(i["L0_xattn_bq"])
    a["bk0"] = i["L0_xattn_bk"].reshape(P, 1)
    for n, m in (("wqa", "Wq"), ("wka", "Wk"), ("wva", "Wv")):
        a[n] = i["L0_attn_" + m].reshape(SH * SD, D).T
    for n, m in (("bqa", "bq"), ("bka", "bk")):
        a[n] = i["L0_attn_" + m].reshape(NP_, P).T
    a["bva"] = np.tile(i["L0_attn_bv"].T, (2, 1))
    a["proja"] = _blocks(i["L0_attn_proj"], NP_)
    a["w1"] = np.concatenate([i["L0_ffn_w1"].transpose(1, 0, 2).reshape(P, -1), i["L0_ffn_shared_gate_up"]], axis=1)
    a["w2"] = i["L0_ffn_w2"].transpose(1, 0, 2).reshape(P, -1)
    a["sdown0"] = i["L0_ffn_shared_down"]
    a["router0"] = np.concatenate([i["L0_ffn_router_w"], i["L0_ffn_shared_gate_w"]], axis=1)
    a["x"] = i["x"][0]
    for n, m in (("bv0", "L0_xattn_bv"), ("bo0", "L0_xattn_bo"), ("bv1", "L1_xattn_bv"), ("bp1", "L1_xattn_bp"),
                 ("bproj1", "L1_attn_proj_b"), ("bqkv1", "L1_attn_qkv_b")):
        a[n] = rep(i[m])
    a["wv1"], a["wp1"] = i["L1_xattn_Wv"].T, i["L1_xattn_Wp"].T
    a["wk1"], a["wq1"] = i["L1_xattn_Wk"], i["L1_xattn_Wq"]
    a["bk1"], a["bq1x3"] = i["L1_xattn_bk"].reshape(P, 1), b3(i["L1_xattn_bq"])
    gb = np.stack([np.tile(i["L1_xattn_q_gamma"], H), np.tile(i["L1_xattn_q_beta"], H)], axis=1)
    a["qgb"] = gb[:QROWS]
    a["kgb"] = np.stack([np.tile(i["L1_xattn_k_gamma"], H), np.tile(i["L1_xattn_k_beta"], H)], axis=1)
    a["wproj1"], a["wqkv1"] = i["L1_attn_proj_w"].T, i["L1_attn_qkv_w"].T
    a["gate1"] = i["L1_ffn_gate_w"]
    a["sgu1"] = np.concatenate([i["L1_ffn_shared_gate_w"], i["L1_ffn_shared_up_w"]], axis=1)
    a["sdown1"] = _blocks(i["L1_ffn_shared_down_w"], 2)
    packs = {}
    for pack, items in PACKS.items():
        out = np.zeros((P, words(pack)), np.float32)
        at = 0
        for name, r, w in items:
            out[0:r, at:at + w] = a[name]
            at += w
        packs[pack] = out
    gate = i["L1_ffn_routed_gate_w"].transpose(1, 0, 2)
    up = i["L1_ffn_routed_up_w"].transpose(1, 0, 2)
    down = i["L1_ffn_routed_down_w"].reshape(E1, 2, P, D).transpose(2, 0, 1, 3).reshape(P, E1, 2 * D)
    experts = np.concatenate([gate, up, down], axis=2).reshape(P, E1 * EW)
    return np.ascontiguousarray(i["ctx_1024"][0].T), packs, np.ascontiguousarray(experts)


def kernel(**inputs):
    import concourse.bacc as _bacc
    from concourse.bass_utils import run_bass_kernel_spmd as _run

    i = {k: np.asarray(v) for k, v in inputs.items()}
    ctxT, packs, experts = _layout(i)
    arrays = {"in_ctxT": ctxT, "in_experts": experts, **{"in_" + n: a for n, a in packs.items()}}
    nc = _bacc.Bacc("TRN2", target_bir_lowering=False, num_devices=1)
    aps = {n: nc.dram_tensor(n, a.shape, mybir.dt.from_np(a.dtype), kind="ExternalInput").ap() for n, a in arrays.items()}
    out = nc.dram_tensor("out", (T, D), F32, kind="ExternalOutput").ap()
    perceiver(nc, aps["in_ctxT"], {n: aps["in_" + n] for n in packs}, aps["in_experts"], out)
    r = _run(nc, [arrays], core_ids=[0])
    return r.results[0]["out"].reshape(1, T, D)
```

```python
from contextlib import ExitStack

import numpy as np

import concourse.bass as bass
from concourse import mybir

F32 = mybir.dt.float32
F32R = mybir.dt.float32r
U32 = mybir.dt.uint32
ALU = mybir.AluOpType
ACT = mybir.ActivationFunctionType
AX = mybir.AxisListType.X

P = 128
T = 64
D = 128
S = 6272
H = 16
DH = D // H
NG = 4
HG = H // NG
GC = HG * DH
GQ = HG * T
NT = S // P
BT = 4
NB = -(-NT // BT)
CW = BT * P
AUG = DH + 1
SH = 16
SD = 64
NP_ = SH // 2
E0, E1 = 8, 32
F0, F1 = 128, 256
EW = 3 * F1
EPS = 1e-5
XSCALE = DH ** -0.5
QROWS = 3 * GC
KROWS = QROWS + 2
KC = [(0, 2), (2, 4), (4, 7), (7, 10), (10, NB)]
CTX_PIECES = [0, 512, 1536, 3072, 4608, S]
MAXN = 2 * NB
LEAD = 4
KEYS_AHEAD = 6

SHIFT_AT = NB - LEAD // 2

STEPS = 2 * (NB + 1)
DONE = {"out": 4, "ln1": 6, "qk": 10, "v": 14, "probs": 16, "z": 16, "ln2": 18, "ffn": 24, "h": STEPS, "ln3": STEPS}
ACT_DONE = {"ln1": 4, "v": 10, "exp": 10, "ln2": 16, "ffn": 18, "ln3": STEPS}
HI_DONE = {"scores": 3, "z": 5, "h": 9, "y": 11}


def v_schedule(c):
    return range(min(NB, max(0, c - 2) + max(0, c - 10)), min(NB, max(0, c - 1) + max(0, c - 9)))


def v_bank(l, c):
    return 2 + c % 2 if l == 0 else c % 4


def max_count(G):
    l, g = divmod(G, NG)
    return l * (NB + (NG - 1) * MAXN) + (NB + (g - 1) * MAXN if g else 0)


def width(c):
    return min(CW, S - c * CW)


def tiles(i):
    return min(BT, NT - i * BT)


def max_stream(G0, a, b):
    return [(G0 + 1 + n // MAXN, n % MAXN) for n in range(a, min(b, (NG - 1) * MAXN))]


HE_CHUNKS = [(0, 2), (2, 8), (8, 16), (16, 24), (24, E1)]

FIRST = [("wk0", P, D), ("bk0", P, 1)]
EARLY = [("wv0", P, D), ("wq0x3", P, NG * QROWS), ("bq0x3", QROWS, NG), ("wo0", P, D)]
LATE = [("wqa", P, SH * SD), ("wka", P, SH * SD), ("wva", P, SH * SD), ("proja", P, NP_ * D),
        ("bqa", P, NP_), ("bka", P, NP_), ("bva", P, SH),
        ("w1", P, (E0 + 2) * F0), ("w2", P, E0 * D), ("sdown0", P, D), ("router0", P, E0 + 1)]
CONST = [("ident", P, P), ("avg", P, P), ("sel", P, 2 * AUG), ("fold", P, T), ("hmask", QROWS, HG),
         ("headmask", P, H), ("causal", P, T), ("iota", P, E1), ("cos", T, DH), ("sin", T, DH),
         ("qgb", QROWS, 2), ("kgb", P, 2), ("x", T, D)]
ROWS = [("bv0", T, D), ("bo0", T, D), ("bv1", T, D), ("bp1", T, D), ("bproj1", T, D), ("bqkv1", T, 3 * D)]
SMALL1 = [("wv1", P, D), ("wp1", P, D), ("wproj1", P, D), ("gate1", P, E1)]
RAW1 = [("wk1", P, D), ("wq1", P, D), ("cen", P, P), ("cen3", P, NG * QROWS), ("bk1", P, 1), ("bq1x3", QROWS, NG)]
TAIL1 = [("wqkv1", P, 3 * D), ("sgu1", P, 2 * F1), ("sdown1", P, 2 * D)]
PACKS = {"first": FIRST, "early": EARLY, "late": LATE, "const": CONST, "rows": ROWS, "small1": SMALL1, "raw1": RAW1, "tail1": TAIL1}


def words(pack):
    return sum(w for _, _, w in PACKS[pack])


NEAR = (3 * S - words("tail1")) // EW
assert (E1 - NEAR) * EW <= words("first") + words("early") + words("late")


def perceiver(nc, ctxT, packs, experts, out):
    with ExitStack() as ctx:
        def sb(name, shape, dt=F32):
            return ctx.enter_context(nc.sbuf_tensor(name, shape, dt))

        def sem(name):
            return ctx.enter_context(nc.semaphore(name))

        ps = ctx.enter_context(nc.psum_tensor("ps", [P, 8, 512], F32))

        arena = sb("arena", [P, 3 * S])
        ctx_sb, khi, klo = arena[:, 0:S], arena[:, S:2 * S], arena[:, 2 * S:3 * S]
        kst = sb("kst", [P, 2, S], F32R)
        qst = sb("qst", [P, NG, GQ], F32R)
        vaug = sb("vaug", [P, NT, H, AUG])
        prob = sb("prob", [P, 2, BT * GQ])
        w0 = sb("w0", [P, words("first") + words("early") + words("late")])
        consts = sb("consts", [P, words("const")])
        rows = sb("rows", [T, words("rows")])
        small1 = sb("small1", [P, words("small1")])
        wk1c = sb("wk1c", [P, D])
        wq1c = sb("wq1c", [P, NG * QROWS])
        bk1c = sb("bk1c", [P, 1])
        bk1g = sb("bk1g", [P, 1])
        bq1c = sb("bq1c", [P, NG])
        scratch = sb("scratch", [P, 1024])
        y = sb("y", [T, D])
        yT2 = sb("yT2", [P, 2 * T])
        attT = sb("attT", [P, T])
        avsb = sb("avsb", [P, GQ])
        eps_col = sb("eps_col", [P, 1])
        mx = sb("mx", [P, 2, NB])
        mneg = sb("mneg", [P, 2])
        mhl = sb("mhl", [P, 2, 2])
        st6 = sb("st6", [T, 6])
        mv = sb("mv", [T, 2])
        lnv = sb("lnv", [T, 1])
        rstd = sb("rstd", [T, 1])
        stat = sb("stat", [P, 4 * 16])
        idx8 = sb("idx8", [P, 8], U32)

        view = {}
        late_at = words("first") + words("early")
        base = {"first": (w0, 0), "early": (w0, words("first")), "late": (w0, late_at), "const": (consts, 0), "rows": (rows, 0),
                "small1": (small1, 0), "raw1": (w0, late_at),
                "tail1": (arena, NEAR * EW)}
        for pack, items in PACKS.items():
            t, at = base[pack]
            for name, r, w in items:
                view[name] = t[0:r, at:at + w]
                at += w
        ident = view["ident"]
        yT = yT2[:, 0:T]
        x = view["x"]
        flat = prob.rearrange("p a b -> p (a b)")

        q_a, q_b = scratch[:, 0:256], scratch[:, 256:512]
        sa_q, sa_k, sa_s = flat[:, 0:1024], flat[:, 1024:1536], flat[:, 1536:2048]
        sa_pT, sa_v = flat[:, 0:1024], scratch[:, 0:1024]
        s1_qk, s1_r = scratch[0:T, 0:2 * D], scratch[0:T, 2 * D:6 * D]
        s1_v = sa_k[0:T, 0:H * AUG].rearrange("p (h a) -> p h a", a=AUG)
        SL = (E0 + 2) // 2
        f0_sig, f0_h, f0_hT = (flat[:, k * SL * F0:(k + 1) * SL * F0] for k in range(3))
        vflat = vaug.rearrange("p t h a -> p (t h a)")
        f1_mask, f1_x, f1_h1 = (vflat[:, k * E1 * T:(k + 1) * E1 * T].rearrange("p (e q) -> p e q", e=E1) for k in range(3))
        f1_he = (f1_x, f1_h1)
        f1_u, f1_sig, f1_h = (flat[0:T, k * 2 * F1:(k + 1) * 2 * F1].rearrange("p (w f) -> p w f", w=2) for k in range(3))
        f1_hT, y2, f1_row = flat[:, 1536:1792], flat[:, 1792:1920], flat[:, 1920:1984]

        def expert(e):
            return arena[:, e * EW:(e + 1) * EW] if e < NEAR else w0[:, (e - NEAR) * EW:(e - NEAR + 1) * EW]

        in_pack = {n: sem("in_" + n) for n in PACKS}
        in_ctx = [sem(f"in_ctx{i}") for i in range(len(CTX_PIECES) - 1)]
        in_stack = [[sem(f"in_stack{s}{k}") for k in range(len(KC))] for s in range(2)]
        in_exp = [sem(f"in_exp{i}") for i in range(3)]
        zeroed = sem("zeroed")
        v_ones = sem("v_ones")
        ones_set = sem("ones_set")
        k_proj = sem("k_proj")
        k_full = sem("k_full")
        k_split = sem("k_split")
        k_sq = sem("k_sq")
        k_var = sem("k_var")
        k_rstd = sem("k_rstd")
        k_scaled = sem("k_scaled")
        v_proj = sem("v_proj")
        v_set = sem("v_set")
        q_ready = sem("q_ready")
        max_made = sem("max_made")
        max_read = sem("max_read")
        shift_cols = sem("shift_cols")
        shift_rows = sem("shift_rows")
        shift_ready = sem("shift_ready")
        scores_done = sem("scores_done")
        exp_done = sem("exp_done")
        av_done = sem("av_done")
        acc_copied = sem("acc_copied")
        o_ready = sem("o_ready")
        dve_step = sem("dve_step")
        act_step = sem("act_step")
        out_stored = sem("out_stored")
        ln_var = sem("ln_var")
        ln_std = sem("ln_std")
        ln_y = sem("ln_y")
        ln_ps = sem("ln_ps")
        ln_yT = sem("ln_yT")
        once = {}

        def nth(tag):
            return int(tag[2:]) + 1

        def ev(name):
            if name not in once:
                once[name] = sem(name)
            return once[name]

        block = ctx.enter_context(nc.Block())

        @block.sync
        def _(sp):
            def load(pack):
                t, at = base[pack]
                rmax = max(r for _, r, _ in PACKS[pack])
                sp.dma_start(t[0:rmax, at:at + words(pack)], packs[pack][0:rmax, :]).then_inc(in_pack[pack], 16)

            def stack(l, g, k):
                G = NG * l + g
                b0, b1 = KC[k]
                a, b = b0 * CW, min(b1 * CW, S)
                sp.wait_ge(k_split, l * NB + min(b1, NB))
                if G >= 2:
                    sp.wait_ge(scores_done, NB * (G - 2) + b1)
                for r, src in ((0, khi), (1, khi), (2, klo)):
                    sp.dma_start(kst[r * GC:(r + 1) * GC, G % 2, a:b].bitcast(F32),
                                 src[g * GC:(g + 1) * GC, a:b]).then_inc(in_stack[G % 2][k], 16)

            def load_experts(i, e0, e1):
                t, at = (arena, e0 * EW) if e0 < NEAR else (w0, (e0 - NEAR) * EW)
                sp.dma_start(t[:, at:at + (e1 - e0) * EW], experts[:, e0 * EW:e1 * EW]).then_inc(in_exp[i], 16)

            def ctx_piece(i):
                a, b = CTX_PIECES[i], CTX_PIECES[i + 1]
                sp.dma_start(ctx_sb[:, a:b], ctxT[:, a:b]).then_inc(in_ctx[i], 16)

            load("first")
            for i in range(len(in_ctx)):
                ctx_piece(i)
                if i == 0:
                    load("early")
            for g in range(2):
                for k in range(len(KC)):
                    stack(0, g, k)
                if g == 0:
                    load("rows")
                    load("raw1")
                    load("small1")
            for g in (2, 3):
                for k in range(len(KC)):
                    stack(0, g, k)
            sp.wait_ge(ev("l1_weights"), 1)
            load("late")
            for g in range(2):
                for k in range(len(KC)):
                    stack(1, g, k)
            sp.wait_ge(ev("ffn0_y"), 1)
            load_experts(1, NEAR, E1)
            sp.wait_ge(v_set, 2 * NB)
            first = S // EW
            load_experts(0, 0, first)
            for g in (2, 3):
                for k in range(len(KC)):
                    stack(1, g, k)
            for s in range(2):
                for k in range(len(KC)):
                    sp.wait_ge(in_stack[s][k], 48 * 4)
            load("tail1")
            load_experts(2, first, NEAR)
            sp.wait_ge(ev("out_ready"), 1)
            sp.dma_start(out, x).then_inc(out_stored, 16)
            sp.wait_ge(out_stored, 16)

        @block.gpsimd
        def _(pool):
            nc.gpsimd.memset(vaug[:, :, :, DH], 1.0).then_inc(v_ones, 1)
            pool.wait_ge(v_ones, 1)
            for s in range(2):
                nc.gpsimd.memset(kst[QROWS:P, s, :].bitcast(F32), 1.0).then_inc(ones_set, 1)
                pool.wait_ge(ones_set, s + 1)

            pool.wait_ge(av_done, NG * NB)
            nc.gpsimd.memset(flat[:, 0:1024], 0.0).then_inc(ev("qbd_zero"), 1)
            pool.wait_ge(ev("qbd_zero"), 1)
            nc.gpsimd.memset(qst[QROWS:P, :, :].bitcast(F32), 0.0).then_inc(ev("shift_zero"), 1)
            pool.wait_ge(ev("shift_zero"), 1)
            for c in range(NB):
                a, b = c * CW, c * CW + width(c)
                pool.wait_ge(k_rstd, c + 1)
                nc.gpsimd.tensor_tensor(klo[:, a:b], klo[:, a:b], khi[:, a:b], ALU.mult).then_inc(k_scaled, 1)

        @block.scalar
        def _(act):
            n = [0]

            def link(ins):
                n[0] += 1
                ins.then_inc(act_step, 1)
                act.wait_ge(act_step, n[0])

            act.dma_start(consts[:, :], packs["const"]).then_inc(in_pack["const"], 16)
            nc.scalar.preload_act_table_set("natural_log_exp_and_others")

            def v_out(l, c):
                k = tiles(c)
                act.wait_ge(v_proj, l * NB + c + 1)
                nc.scalar.activation(vaug[:, BT * c:BT * c + k, :, 0:DH],
                                     ps[:, v_bank(l, c), 0:k * D].rearrange("p (t h d) -> p t h d", t=k, h=H),
                                     ACT.Copy).then_inc(v_set, 1)

            def keys0(c):
                a, b = c * CW, c * CW + width(c)
                act.wait_ge(k_proj, c + 1)
                nc.scalar.activation(khi[:, a:b].bitcast(F32R), ps[:, c % 2, 0:width(c)], ACT.Identity,
                                     bias=view["bk0"]).then_inc(k_full, 1)

            key_step = [0]

            def keys_until(n):
                for step in range(key_step[0], n):
                    c = step // 2
                    if step % 2 == 0 and c < NB:
                        a, b = c * CW, c * CW + width(c)
                        act.wait_ge(k_proj, NB + c + 1)
                        nc.scalar.activation(klo[:, a:b], ps[:, c % 2, 0:width(c)], ACT.Identity, bias=bk1g[:, 0:1],
                                             scale=view["kgb"][:, 0:1])
                        nc.scalar.activation(khi[:, a:b], ps[:, c % 2, 0:width(c)], ACT.Square,
                                             bias=bk1c[:, 0:1]).then_inc(k_sq, 1)
                    if step % 2 and c >= 1:
                        v = (c - 1) % 2
                        a, b = (c - 1) * CW, (c - 1) * CW + width(c - 1)
                        act.wait_ge(k_var, c)
                        link(nc.scalar.activation(khi[:, a:b], ps[:, 2 + v, 0:b - a], ACT.Ln, bias=eps_col[:, 0:1]))
                        nc.scalar.activation(khi[:, a:b], khi[:, a:b], ACT.Exp, scale=-0.5).then_inc(k_rstd, 1)
                    key_step[0] = step + 1

            def exps(l):
                for g in range(NG):
                    for i in range(NB):
                        B = (NG * l + g) * NB + i
                        act.wait_ge(scores_done, B + 1)
                        if B >= 2:
                            act.wait_ge(av_done, B - 1)
                        w = tiles(i) * GQ
                        b0 = 2 * (B % 2)
                        nc.scalar.activation(prob[:, B % 2, 0:w],
                                             ps[:, b0:b0 + 2, :].rearrange("p a b -> p (a b)")[:, 0:w],
                                             ACT.Exp, scale=XSCALE).then_inc(exp_done, 1)

            def norm_std(tag):
                act.wait_ge(ln_var, nth(tag))
                link(nc.scalar.activation(lnv[:, 0:1], mv[:, 1:2], ACT.Ln, bias=eps_col[0:T, 0:1]))
                nc.scalar.activation(rstd[:, 0:1], lnv[:, 0:1], ACT.Exp, scale=-0.5).then_inc(ln_std, 1)

            act.wait_ge(ev("eps_set"), 1)
            norm_std("ln0")
            act.wait_ge(in_pack["first"], 16)
            for c in range(-KEYS_AHEAD, NB):
                if c + KEYS_AHEAD < NB:
                    keys0(c + KEYS_AHEAD)
                for v in v_schedule(c):
                    v_out(0, v)
            exps(0)

            act.wait_ge(ev("l1_weights"), 1)
            for s in range(2):
                for k in range(len(KC)):
                    act.wait_ge(in_stack[s][k], 48 * 2)
            keys_until(ACT_DONE["ln1"])
            norm_std("ln1")
            keys_until(ACT_DONE["v"])
            act.wait_ge(ev("sa0_shifted"), 1)
            nc.scalar.activation(sa_s[:], sa_s[:], ACT.Exp, scale=SD ** -0.5).then_inc(ev("sa0_exp"), 1)
            keys_until(ACT_DONE["exp"])
            act.wait_ge(ev("sa0_v"), 1)
            nc.scalar.activation(sa_v[0:T, :], ps[0:T, 4:6, :].rearrange("p a b -> p (a b)"),
                                 ACT.Copy).then_inc(ev("sa0_vs"), 1)
            keys_until(ACT_DONE["ln2"])
            norm_std("ln2")
            keys_until(ACT_DONE["ffn"])
            nc.scalar.preload_act_table_set("exp_and_others")
            act.wait_ge(ev("ffn0_negmax"), 1)
            nc.scalar.activation(stat[:, 0:E0], ps[:, 6, 0:E0], ACT.Exp, bias=stat[:, 8:9], accum_out=stat[:, 9:10])
            nc.scalar.activation(stat[:, 10:11], ps[:, 6, E0:E0 + 1], ACT.Tanh, scale=0.5).then_inc(ev("ffn0_exp"), 1)
            act.wait_ge(ev("ffn0_hidden"), 1)
            nc.scalar.activation(f0_sig[:], ps[:, 4:6, :].rearrange("p a b -> p (a b)")[:, 0:SL * F0],
                                 ACT.Tanh, scale=0.5).then_inc(ev("ffn0_sig"), 1)
            nc.scalar.preload_act_table_set("natural_log_exp_and_others")

            keys_until(ACT_DONE["ln3"])
            norm_std("ln3")
            keys_until(STEPS)
            for c in range(3):
                v_out(1, c)
            act.wait_ge(ev("q1_var"), 1)
            link(nc.scalar.activation(q_b[0:QROWS, :], ps[0:QROWS, 6, 256:256 + NG * T], ACT.Ln, bias=eps_col[0:QROWS, 0:1]))
            nc.scalar.activation(q_b[0:QROWS, :], q_b[0:QROWS, :], ACT.Exp, scale=-0.5).then_inc(ev("q1_std"), 1)
            for c in range(3, NB):
                v_out(1, c)
            exps(1)

            norm_std("ln4")
            act.wait_ge(ev("sa1_shifted"), 1)
            nc.scalar.activation(sa_s[:], sa_s[:], ACT.Exp, scale=DH ** -0.5).then_inc(ev("sa1_exp"), 1)
            act.wait_ge(ev("sa1_pT"), 2)
            nc.scalar.activation(sa_pT[0:T, 512:1024], ps[0:T, 5, :], ACT.Copy).then_inc(ev("sa1_pTs"), 1)

            norm_std("ln5")
            nc.scalar.preload_act_table_set("exp_and_others")
            act.wait_ge(ev("top1"), 1)
            nc.scalar.activation(stat[0:T, 8:9], stat[0:T, 0:1], ACT.Tanh, scale=0.5).then_inc(ev("top1_tanh"), 1)
            act.wait_ge(ev("ffn1_shared"), 1)
            nc.scalar.activation(f1_sig[:, 1, :], ps[0:T, 5, 0:F1], ACT.Tanh, scale=0.5).then_inc(ev("shared_tanh"), 1)
            act.wait_ge(ev("top1_score"), 1)
            act.wait_ge(ev("ffn1_gu"), 1)
            nc.scalar.activation(f1_sig[:, 0, :], ps[0:T, 4, 0:F1], ACT.Tanh, scale=stat[0:T, 11:12]).then_inc(ev("ffn1_sig"), 1)

        @block.vector
        def _(dve):
            n = [0]

            def link(ins):
                n[0] += 1
                ins.then_inc(dve_step, 1)
                dve.wait_ge(dve_step, n[0])

            V = nc.vector

            def norm(tag, copies=1):
                link(V.bn_stats(st6[:, :], x))
                V.bn_aggr(mv[:, :], st6[:, :]).then_inc(ln_var, 1)
                dve.wait_ge(ln_var, nth(tag))
                dve.wait_ge(ln_std, nth(tag))
                V.tensor_scalar(y[:, :], x, mv[:, 0:1], rstd[:, 0:1], ALU.subtract, ALU.mult).then_inc(ln_y, 1)
                dve.wait_ge(ln_ps, nth(tag))
                V.tensor_copy(yT2[:, 0:copies * T].rearrange("p (c t) -> p c t", t=T),
                              ps[:, 7, 0:T].unsqueeze(1).to_broadcast([P, copies, T])).then_inc(ln_yT, 1)

            def stack_queries():
                link(V.tensor_copy(q_b[0:QROWS, :].bitcast(F32R), q_a[0:QROWS, :]))
                link(V.tensor_tensor(q_b[GC:2 * GC, :].bitcast(F32R), q_a[GC:2 * GC, :], q_b[GC:2 * GC, :], ALU.subtract))
                qv = q_b[0:QROWS, :].rearrange("p (g q) -> p g q", g=NG)
                for h in range(HG):
                    last = V.tensor_scalar(qst[0:QROWS, :, h * T:(h + 1) * T], qv, view["hmask"][:, h:h + 1], None, ALU.mult)
                last.then_inc(q_ready, 1)

            def max_chunk(G, m):
                k, p = m // 2, m % 2
                dve.wait_ge(max_made, max_count(G) + m + 1)
                V.reduce_max(mx[:, p, k:k + 1], ps[:, 4 + m % 2, 0:width(k)], AX).then_inc(max_read, 1)

            def max_pair(G, k):
                dve.wait_ge(max_made, max_count(G) + k + 1)
                b0 = 4 + 2 * (k % 2)
                V.tensor_reduce(mx[:, :, k], ps[:, b0:b0 + 2, 0:width(k)], AX, ALU.max).then_inc(max_read, 1)

            def shift(G):
                dve.wait_ge(max_read, max_count(G + 1))
                link(V.tensor_reduce(mneg[:, :], mx[:, :, :], AX, ALU.max))
                link(V.tensor_scalar(mneg[:, :], mneg[:, :], -1.0, None, ALU.mult))
                link(V.tensor_copy(mhl[:, :, 0].bitcast(F32R), mneg[:, :]))
                V.tensor_tensor(mhl[:, :, 1].bitcast(F32R), mneg[:, :], mhl[:, :, 0], ALU.subtract).then_inc(shift_cols, 1)

            def shift_in(G):
                dve.wait_ge(shift_rows, G + 1)
                V.tensor_copy(qst[QROWS:KROWS, G % NG, :], ps[QROWS:KROWS, 7, 256:512]).then_inc(shift_ready, 1)

            def copy_acc(G):
                dve.wait_ge(av_done, NB * (G + 1))
                if G >= 1:
                    dve.wait_ge(o_ready, G)
                V.tensor_copy(avsb[:, :], ps[:, 6, 0:GQ]).then_inc(acc_copied, 1)

            key_step = [0]

            def keys_until(n):
                for c in range(key_step[0], min(n, NB)):
                    a, b = c * CW, c * CW + width(c)
                    dve.wait_ge(k_scaled, c + 1)
                    V.tensor_scalar(khi[:, a:b].bitcast(F32R), klo[:, a:b], view["kgb"][:, 1:2], None,
                                    ALU.add).then_inc(k_full, 1)
                    dve.wait_ge(k_full, NB + c + 1)
                    V.scalar_tensor_tensor(klo[:, a:b], klo[:, a:b], view["kgb"][:, 1:2], khi[:, a:b],
                                           ALU.add, ALU.subtract).then_inc(k_split, 1)
                    key_step[0] = c + 1

            def split(c):
                a, b = c * CW, c * CW + width(c)
                dve.wait_ge(k_full, c + 1)
                V.scalar_tensor_tensor(klo[:, a:b], ps[:, c % 2, 0:width(c)], view["bk0"], khi[:, a:b],
                                       ALU.add, ALU.subtract).then_inc(k_split, 1)

            def cross(l):
                G0 = NG * l
                for k in range(NB):
                    if l == 0 and k + KEYS_AHEAD < NB:
                        split(k + KEYS_AHEAD)
                    max_pair(G0, k)
                shift(G0)
                shift_in(G0)
                for G, m in max_stream(G0, 0, LEAD):
                    max_chunk(G, m)
                for g in range(NG):
                    for i in range(NB):
                        n = LEAD + 2 * (g * NB + i)
                        for j in range(2):
                            for G, m in max_stream(G0, n + j, n + j + 1):
                                max_chunk(G, m)
                                if m == MAXN - 1:
                                    shift(G)
                                    shift_in(G)
                            if i == 0 and g >= 1 and j == 0:
                                copy_acc(G0 + g - 1)
                        G = G0 + g
                        if G == 0 and i == 1:
                            dve.wait_ge(ev("l1_wkps"), 1)
                            V.tensor_copy(wk1c[:, :], ps[:, 7, 0:D])
                            V.tensor_copy(bk1c[:, :], ps[:, 7, D:D + 1])
                            V.tensor_tensor(bk1g[:, :], ps[:, 7, D:D + 1], view["kgb"][:, 0:1], ALU.mult)
                            V.tensor_copy(bq1c[0:QROWS, :], ps[0:QROWS, 7, D + 1:D + 1 + NG]).then_inc(ev("l1_wk"), 1)
                        if G == 0 and i == 4:
                            dve.wait_ge(ev("l1_wqps"), 1)
                            V.tensor_copy(wq1c[:, :], ps[:, 7, 0:NG * QROWS]).then_inc(ev("l1_weights"), 1)
                copy_acc(G0 + NG - 1)

            def cross_out(l, bv, bo, tag):
                dve.wait_ge(o_ready, NG * (l + 1))
                o = ps[0:T, 7, 0:H * AUG].rearrange("p (h a) -> p h a", a=AUG)
                link(V.reciprocal(stat[0:T, 0:H], o[:, :, DH]))
                att = y[:, :].rearrange("p (h a) -> p h a", a=DH)
                link(V.tensor_tensor(att, o[:, :, 0:DH], stat[0:T, 0:H].unsqueeze(2).to_broadcast([T, H, DH]), ALU.mult))
                V.tensor_tensor(y[:, :], y[:, :], bv, ALU.add).then_inc(ev(f"{tag}_att"), 1)
                link(V.tensor_tensor(x, x, bo, ALU.add))
                dve.wait_ge(ev(f"{tag}_attps"), 1)
                V.tensor_copy(attT[:, :], ps[:, 6, 0:T]).then_inc(ev(f"{tag}_attT"), 1)
                dve.wait_ge(ev(f"{tag}_proj"), 1)
                link(V.tensor_tensor(x, ps[0:T, 6, 128:256], x, ALU.add))

            def shifted_scores(tag):
                s3 = sa_s[:].rearrange("p (j k) -> p j k", k=T)
                scores3 = ps[:, 6, :].rearrange("p (j k) -> p j k", k=T)
                dve.wait_ge(ev(f"{tag}_scores"), 1)
                link(V.tensor_reduce(stat[:, 0:8], scores3, AX, ALU.max))
                V.tensor_tensor(s3, scores3, stat[:, 0:8].unsqueeze(2).to_broadcast([P, 8, T]),
                                ALU.subtract).then_inc(ev(f"{tag}_shifted"), 1)

            def turned(tag, half):
                dve.wait_ge(ev(f"{tag}_pT"), half + 1)
                V.tensor_copy(sa_pT[0:T, half * 512:(half + 1) * 512], ps[0:T, 4 + half, :]).then_inc(ev(f"{tag}_pTs"), 1)

            V.memset(eps_col[:, :], EPS).then_inc(ev("eps_set"), 1)
            V.memset(ps[:, 6, :], 0.0).then_inc(zeroed, 1)
            V.memset(qst[QROWS:P, :, :].bitcast(F32), 0.0)
            dve.wait_ge(in_pack["const"], 16)
            norm("ln0")
            dve.wait_ge(in_pack["first"], 16)
            split(0)
            split(1)
            dve.wait_ge(in_pack["early"], 16)
            dve.wait_ge(ev("q0_ps"), 1)
            link(V.tensor_tensor(q_a[0:QROWS, :].rearrange("p (g q) -> p g q", g=NG),
                                 ps[0:QROWS, 6, 256:256 + NG * T].rearrange("p (g q) -> p g q", g=NG),
                                 view["bq0x3"].unsqueeze(2).to_broadcast([QROWS, NG, T]), ALU.add))
            stack_queries()
            for c in range(2, KEYS_AHEAD):
                split(c)
            cross(0)
            dve.wait_ge(in_pack["rows"], 16)
            cross_out(0, view["bv0"], view["bo0"], "x0")

            norm("ln1")
            dve.wait_ge(ev("qbd_zero"), 1)
            dve.wait_ge(ev("sa0_q"), 1)
            q3 = sa_q[:].rearrange("p (j c) -> p j c", j=NP_)
            for hh in range(2):
                r = slice(64 * hh, 64 * hh + 64)
                V.tensor_tensor(q3[r, :, r], ps[r, 4, :].rearrange("p (j q) -> p j q", q=T),
                                view["bqa"][r].unsqueeze(2).to_broadcast([64, NP_, T]), ALU.add)
            V.tensor_tensor(sa_k[:].rearrange("p (j q) -> p j q", q=T), ps[:, 5, :].rearrange("p (j q) -> p j q", q=T),
                            view["bka"].unsqueeze(2).to_broadcast([P, NP_, T]), ALU.add).then_inc(ev("sa0_qk"), 1)
            keys_until(HI_DONE["scores"])
            shifted_scores("sa0")
            s3 = sa_s[:].rearrange("p (j k) -> p j k", k=T)
            dve.wait_ge(ev("sa0_exp"), 1)
            link(V.tensor_reduce(stat[:, 8:16], s3, AX, ALU.add))
            link(V.reciprocal(stat[:, 8:16], stat[:, 8:16]))
            V.tensor_tensor(s3, s3, stat[:, 8:16].unsqueeze(2).to_broadcast([P, 8, T]),
                            ALU.mult).then_inc(ev("sa0_probs"), 1)
            turned("sa0", 0)
            turned("sa0", 1)
            keys_until(HI_DONE["z"])
            dve.wait_ge(ev("sa0_z"), 1)
            V.tensor_tensor(sa_k[:].rearrange("p (h q) -> p h q", h=SH), ps[:, 6, :].rearrange("p (h q) -> p h q", h=SH),
                            view["bva"].unsqueeze(2).to_broadcast([P, SH, T // 2]), ALU.add).then_inc(ev("sa0_zT"), 1)
            dve.wait_ge(ev("sa0_proj"), 1)
            link(V.scalar_tensor_tensor(x, ps[0:T, 7, 0:D], SD ** -0.5, x, ALU.mult, ALU.add))

            norm("ln2", 2)
            dve.wait_ge(ev("ffn0_logits"), 1)
            lg = stat[:, 16:16 + E0]
            link(V.tensor_copy(lg, ps[:, 6, 0:E0]))
            link(V.max(stat[:, 24:32], lg))
            V.tensor_scalar(stat[:, 8:9], stat[:, 24:25], -1.0, None, ALU.mult).then_inc(ev("ffn0_negmax"), 1)
            link(V.max_index(idx8[:, :], stat[:, 24:32], lg))
            link(V.tensor_copy(stat[:, 32:34], idx8[:, 0:2]))
            link(V.tensor_scalar(stat[:, 40:48], view["iota"][:, 0:E0], stat[:, 32:33], None, ALU.is_equal))
            link(V.scalar_tensor_tensor(stat[:, 40:48], view["iota"][:, 0:E0], stat[:, 33:34], stat[:, 40:48],
                                        ALU.is_equal, ALU.add))
            dve.wait_ge(ev("ffn0_exp"), 1)
            link(V.reciprocal(stat[:, 9:10], stat[:, 9:10]))
            link(V.tensor_scalar(stat[:, 9:10], stat[:, 9:10], 0.5, None, ALU.mult))
            wt = stat[:, 56:56 + SL]
            V.scalar_tensor_tensor(wt[0:T, :], stat[0:T, 0:SL], stat[0:T, 9:10], stat[0:T, 40:40 + SL],
                                   ALU.mult, ALU.mult)
            V.scalar_tensor_tensor(wt[T:P, 0:E0 - SL], stat[T:P, SL:E0], stat[T:P, 9:10], stat[T:P, 40 + SL:48],
                                   ALU.mult, ALU.mult)
            link(V.tensor_scalar(wt[T:P, SL - 2:SL - 1], stat[T:P, 10:11], 0.25, 0.25, ALU.mult, ALU.add))
            dve.wait_ge(ev("ffn0_sig"), 1)
            for k in range(SL):
                r = slice(0, P if k < SL - 1 else T)
                sl = f0_sig[r, k * F0:(k + 1) * F0]
                last = V.tensor_scalar(sl, sl, wt[r, k:k + 1], wt[r, k:k + 1], ALU.mult, ALU.add)
            link(last)
            hid = ps[:, 4:6, :].rearrange("p a b -> p (a b)")
            up = slice((SL - 1) * F0, SL * F0)
            V.tensor_tensor(f0_h[0:T, up], hid[0:T, up], f0_sig[0:T, up], ALU.mult)
            link(V.tensor_tensor(f0_h[:, 0:(SL - 1) * F0], hid[:, 0:(SL - 1) * F0], f0_sig[:, 0:(SL - 1) * F0], ALU.mult))
            shared = slice((SL - 2) * F0, (SL - 1) * F0)
            V.tensor_tensor(f0_h[T:P, shared], hid[T:P, up], f0_h[T:P, shared], ALU.mult).then_inc(ev("ffn0_h"), 1)
            keys_until(HI_DONE["h"])
            dve.wait_ge(ev("ffn0_hT"), 1)
            V.tensor_copy(f0_hT[:, (SL - 1) * F0:(SL - 1) * F0 + T], ps[:, 6, 64:64 + T])
            V.tensor_copy(f0_hT[:, 0:(SL - 1) * F0], ps[:, 7, :]).then_inc(ev("ffn0_hTs"), 1)
            keys_until(HI_DONE["y"])
            dve.wait_ge(ev("ffn0_y"), 1)
            link(V.tensor_tensor(x, ps[0:T, 4, 0:D], x, ALU.add))

            norm("ln3")
            dve.wait_ge(ev("q1_ps"), 1)
            qa3 = q_a[0:QROWS, :].rearrange("p (g q) -> p g q", g=NG)
            link(V.tensor_tensor(qa3, ps[0:QROWS, 6, 0:NG * T].rearrange("p (g q) -> p g q", g=NG),
                                 bq1c[0:QROWS, :].unsqueeze(2).to_broadcast([QROWS, NG, T]), ALU.add))
            V.tensor_tensor(q_b[0:QROWS, :], q_a[0:QROWS, :], q_a[0:QROWS, :], ALU.mult).then_inc(ev("q1_sq"), 1)
            keys_until(NB)
            dve.wait_ge(ev("q1_std"), 1)
            link(V.tensor_tensor(q_a[0:QROWS, :], q_a[0:QROWS, :], q_b[0:QROWS, :], ALU.mult))
            link(V.tensor_scalar(q_a[0:QROWS, :], q_a[0:QROWS, :], view["qgb"][:, 0:1], view["qgb"][:, 1:2],
                                 ALU.mult, ALU.add))
            stack_queries()
            cross(1)
            cross_out(1, view["bv1"], view["bp1"], "x1")

            norm("ln4")
            dve.wait_ge(ev("sa1_qkps"), 1)
            link(V.tensor_tensor(s1_qk, ps[0:T, 4, 0:2 * D], view["bqkv1"][:, 0:2 * D], ALU.add))
            qk = s1_qk.rearrange("p (h a) -> p h a", a=DH)
            r1 = s1_r[:, 0:2 * D].rearrange("p (h a) -> p h a", a=DH)
            r2 = s1_r[:, 2 * D:4 * D].rearrange("p (h a) -> p h a", a=DH)
            half = DH // 2
            V.tensor_tensor(r1, qk, view["cos"].unsqueeze(1).to_broadcast([T, 2 * H, DH]), ALU.mult)
            V.tensor_tensor(r2[:, :, 0:half], qk[:, :, half:DH],
                            view["sin"][:, 0:half].unsqueeze(1).to_broadcast([T, 2 * H, half]), ALU.mult)
            link(V.tensor_tensor(r2[:, :, half:DH], qk[:, :, 0:half],
                                 view["sin"][:, half:DH].unsqueeze(1).to_broadcast([T, 2 * H, half]), ALU.mult))
            V.tensor_tensor(s1_r[:, 0:2 * D], s1_r[:, 0:2 * D], s1_r[:, 2 * D:4 * D], ALU.add).then_inc(ev("sa1_rope"), 1)
            link(V.tensor_tensor(x, x, view["bproj1"], ALU.add))
            dve.wait_ge(ev("sa1_qkT"), 1)
            V.tensor_copy(attT[:, :], ps[:, 7, 0:T])
            for hh in range(2):
                V.tensor_tensor(sa_q[:, hh * 512:(hh + 1) * 512].rearrange("p (h k) -> p h k", k=T),
                                ps[:, 7, T:2 * T].unsqueeze(1).to_broadcast([P, H // 2, T]),
                                view["headmask"][:, hh * H // 2:(hh + 1) * H // 2].unsqueeze(2).to_broadcast([P, H // 2, T]),
                                ALU.mult).then_inc(ev("sa1_qk"), 1)
            V.memset(s1_v[:, :, DH], 1.0)
            dve.wait_ge(ev("sa1_vps"), 1)
            V.tensor_tensor(s1_v[:, :, 0:DH], ps[0:T, 5, 0:D].rearrange("p (h a) -> p h a", a=DH),
                            view["bqkv1"][:, 2 * D:3 * D].rearrange("p (h a) -> p h a", a=DH),
                            ALU.add).then_inc(ev("sa1_vs"), 1)
            shifted_scores("sa1")
            turned("sa1", 0)
            dve.wait_ge(ev("sa1_av"), 1)
            o = ps[:, 7, 0:H // 2 * AUG].rearrange("p (j a) -> p j a", a=AUG)
            link(V.reciprocal(stat[:, 0:8], o[:, :, DH]))
            y4 = y[:, :].rearrange("p (j u a) -> p j u a", u=2, a=DH)
            for u in range(2):
                r = slice(64 * u, 64 * u + 64)
                last = V.tensor_tensor(y4[:, :, u, :], o[r, :, 0:DH], stat[r, 0:8].unsqueeze(2).to_broadcast([T, 8, DH]), ALU.mult)
            last.then_inc(ev("sa1_o"), 1)
            dve.wait_ge(ev("sa1_oT"), 1)
            V.tensor_copy(attT[:, :], ps[:, 6, 0:T]).then_inc(ev("sa1_oTs"), 1)
            dve.wait_ge(ev("sa1_proj"), 1)
            link(V.tensor_tensor(x, ps[0:T, 6, 128:256], x, ALU.add))

            norm("ln5")
            dve.wait_ge(ev("ffn1_logits"), 1)
            lg = stat[0:T, 16:16 + E1]
            link(V.tensor_copy(lg, ps[0:T, 6, 0:E1]))
            V.max(stat[0:T, 0:8], lg).then_inc(ev("top1"), 1)
            dve.wait_ge(ev("top1"), 1)
            link(V.max_index(idx8[0:T, :], stat[0:T, 0:8], lg))
            V.tensor_copy(stat[0:T, 9:10], idx8[0:T, 0:1]).then_inc(ev("top1_index"), 1)
            dve.wait_ge(ev("index_row"), 1)
            link(V.tensor_copy(f1_row, ps[:, 7, 0:T]))
            for e in range(E1):
                V.scalar_tensor_tensor(f1_x[:, e, :], f1_row, view["iota"][:, e:e + 1], yT[:, :],
                                       ALU.is_equal, ALU.mult).then_inc(ev("ffn1_x"), 1)
            dve.wait_ge(ev("top1_tanh"), 1)
            link(V.tensor_scalar(stat[0:T, 10:11], stat[0:T, 8:9], 0.5, 0.5, ALU.mult, ALU.add))
            V.tensor_scalar(stat[0:T, 11:12], stat[0:T, 10:11], 0.5, None, ALU.mult).then_inc(ev("top1_score"), 1)
            link(V.tensor_tensor(stat[0:T, 12:13], stat[0:T, 10:11], stat[0:T, 10:11], ALU.mult))
            dve.wait_ge(ev("shared_tanh"), 1)
            V.tensor_copy(f1_u[:, 1, :], ps[T:P, 5, 0:F1])
            link(V.tensor_scalar(f1_sig[:, 1, :], f1_sig[:, 1, :], 0.5, 0.5, ALU.mult, ALU.add))
            link(V.tensor_tensor(f1_h[:, 1, :], ps[0:T, 5, 0:F1], f1_sig[:, 1, :], ALU.mult))
            V.tensor_tensor(f1_h[:, 1, :], f1_h[:, 1, :], f1_u[:, 1, :], ALU.mult).then_inc(ev("shared_h"), 1)
            EC = 8
            for c in range(E1 // EC):
                es = slice(c * EC, (c + 1) * EC)
                V.tensor_tensor(f1_mask[:, es, :], f1_row.unsqueeze(1).to_broadcast([P, EC, T]),
                                view["iota"][:, es].unsqueeze(2).to_broadcast([P, EC, T]), ALU.is_equal)
            dve.wait_ge(ev("ffn1_gu"), 1)
            V.tensor_copy(f1_u[:, 0, :], ps[T:P, 4, 0:F1])
            dve.wait_ge(ev("ffn1_sig"), 1)
            link(V.tensor_scalar(f1_sig[:, 0, :], f1_sig[:, 0, :], 0.5, 0.5, ALU.mult, ALU.add))
            link(V.scalar_tensor_tensor(f1_h[:, 0, :], ps[0:T, 4, 0:F1], stat[0:T, 12:13], f1_sig[:, 0, :],
                                        ALU.mult, ALU.mult))
            V.tensor_tensor(f1_h[:, 0, :], f1_h[:, 0, :], f1_u[:, 0, :], ALU.mult).then_inc(ev("ffn1_h"), 1)
            dve.wait_ge(ev("shared_hT"), 1)
            V.tensor_copy(f1_hT[:, P:2 * P], ps[:, 6, P:2 * P]).then_inc(ev("shared_hTs"), 1)
            dve.wait_ge(ev("ffn1_hT"), 1)
            link(V.tensor_copy(f1_hT[:, 0:P], ps[:, 7, P:2 * P]))
            for a, b in HE_CHUNKS:
                for k in range(2):
                    last = V.tensor_tensor(f1_he[k][:, a:b, :], f1_mask[:, a:b, :],
                                           f1_hT[:, k * T:(k + 1) * T].unsqueeze(1).to_broadcast([P, b - a, T]), ALU.mult)
                last.then_inc(ev("ffn1_he"), 1)
            dve.wait_ge(ev("ffn1_d"), 1)
            V.tensor_copy(y2, ps[:, 5, 0:D]).then_inc(ev("ffn1_ds"), 1)
            dve.wait_ge(ev("ffn1_out"), 1)
            V.tensor_tensor(x, ps[0:T, 4, 0:D], x, ALU.add).then_inc(ev("out_ready"), 1)

        @block.tensor
        def _(pe):
            mm = nc.tensor.matmul

            def one(out_, lhsT, rhs, start=True, stop=True):
                return mm(out_, lhsT, rhs, start=start, stop=stop, skip_group_check=True)

            key_step = [0]

            def keys_until(n):
                for step in range(key_step[0], n):
                    c = step // 2
                    if step % 2 == 0 and c < NB:
                        key_chunk(1, c, wk1c[:, :])
                    if step % 2 and c >= 1:
                        var_chunk(c - 1)
                    key_step[0] = step + 1

            def yT_of(tag):
                pe.wait_ge(ln_y, nth(tag))
                nc.tensor.transpose(ps[:, 7, 0:T], y[:, :], ident[0:T, 0:T]).then_inc(ln_ps, 1)
                pe.wait_ge(ln_yT, nth(tag))

            def key_chunk(l, c, w):
                a, b = c * CW, c * CW + width(c)
                if l == 0:
                    for i in range(len(in_ctx)):
                        if CTX_PIECES[i] <= a < CTX_PIECES[i + 1]:
                            pe.wait_ge(in_ctx[i], 16)
                if c >= 2:
                    pe.wait_ge(k_split if l == 0 else k_sq, c - 1)
                one(ps[:, c % 2, 0:width(c)], w, ctx_sb[:, a:b]).then_inc(k_proj, 1)

            def var_chunk(c):
                a, b = c * CW, c * CW + width(c)
                pe.wait_ge(k_sq, c + 1)
                if c >= 2:
                    pe.wait_ge(k_rstd, c - 1)
                one(ps[:, 2 + c % 2, 0:width(c)], view["avg"], khi[:, a:b]).then_inc(k_var, 1)

            def v_chunk(l, c, w):
                ring = 2 if l == 0 else 4
                if c >= ring:
                    pe.wait_ge(v_set, l * NB + c + 1 - ring)
                for t in range(tiles(c)):
                    for hh in range(2):
                        a = (BT * c + t) * P + 64 * hh
                        last = one(ps[64 * hh:64 * hh + 64, v_bank(l, c), t * D:(t + 1) * D], ctx_sb[:, a:a + 64], w)
                last.then_inc(v_proj, 1)

            def stack_there(G, k):
                for j, (b0, b1) in enumerate(KC):
                    if b0 == k:
                        pe.wait_ge(in_stack[G % 2][j], 48 * (G // 2 + 1))

            def max_scores(G, k, p, bnk):
                a, b = k * CW, k * CW + width(k)
                return one(ps[:, bnk, 0:width(k)], qst[:, G % NG, p * P:(p + 1) * P], kst[:, G % 2, a:b])

            def max_chunk(G, m):
                k, p = m // 2, m % 2
                if p == 0:
                    stack_there(G, k)
                first = G % NG == 1 and m < 2
                pe.wait_ge(max_read, max_count(G) + (0 if first else m - 1))
                max_scores(G, k, p, 4 + m % 2).then_inc(max_made, 1)

            def max_pair(G, k):
                stack_there(G, k)
                if k >= 2:
                    pe.wait_ge(max_read, max_count(G) + k - 1)
                for p in range(2):
                    last = max_scores(G, k, p, 4 + 2 * (k % 2) + p)
                last.then_inc(max_made, 1)

            def shift(G):
                pe.wait_ge(shift_cols, G + 1)
                for p in range(2):
                    last = one(ps[QROWS:KROWS, 7, 256 + p * P:256 + (p + 1) * P], mhl[:, p, :], ident)
                last.then_inc(shift_rows, 1)

            def scores(G, i):
                B = NB * G + i
                if i == 0:
                    pe.wait_ge(shift_ready, G + 1)
                if B % (NG * NB) >= 2:
                    pe.wait_ge(exp_done, B - 1)
                dst = ps[:, 2 * (B % 2):2 * (B % 2) + 2, :].rearrange("p a b -> p (a b)")
                for t in range(tiles(i)):
                    a = (BT * i + t) * P
                    last = one(dst[:, t * GQ:(t + 1) * GQ], kst[:, G % 2, a:a + P], qst[:, G % NG, :])
                last.then_inc(scores_done, 1)

            def weighted(G, i):
                B = NB * G + i
                g = G % NG
                pe.wait_ge(exp_done, B + 1)
                if i == 0 and G >= 1:
                    pe.wait_ge(acc_copied, G)
                for p in range(2):
                    for t in range(tiles(i)):
                        h = HG * g + 2 * p
                        last = one(ps[32 * t:32 * t + 2 * AUG, 6, p * P:(p + 1) * P],
                                   vaug[:, BT * i + t, h:h + 2, :].rearrange("p h a -> p (h a)"),
                                   prob[:, B % 2, t * GQ + p * P:t * GQ + (p + 1) * P],
                                   start=(i == 0 and p == 0), stop=(i == NB - 1))
                last.then_inc(av_done, 1)

            def gather(G):
                g = G % NG
                pe.wait_ge(acc_copied, G + 1)
                for h in range(HG):
                    c = (HG * g + h) * AUG
                    last = one(ps[0:T, 7, c:c + AUG], avsb[:, h * T:(h + 1) * T],
                               view["sel"][:, (h % 2) * AUG:(h % 2 + 1) * AUG])
                last.then_inc(o_ready, 1)

            def cross(l):
                G0 = NG * l
                for Gm, m in max_stream(G0, 0, 2):
                    max_chunk(Gm, m)
                shift(G0)
                for g in range(NG):
                    G = G0 + g
                    for i in range(NB):
                        n = LEAD + 2 * (g * NB + i)
                        scores(G, i)
                        if G == G0 and i == 0:
                            for Gm, m in max_stream(G0, 2, LEAD):
                                max_chunk(Gm, m)
                        for Gm, m in max_stream(G0, n, n + 1):
                            max_chunk(Gm, m)
                        if i >= 1:
                            weighted(G, i - 1)
                        elif g >= 1:
                            weighted(G - 1, NB - 1)
                        for Gm, m in max_stream(G0, n + 1, n + 2):
                            max_chunk(Gm, m)
                        if i == SHIFT_AT and g + 1 < NG:
                            shift(G + 1)
                        if i == 3 and g >= 1:
                            gather(G - 1)
                        if G == 0 and i == 0:
                            pe.wait_ge(in_pack["raw1"], 16)
                            one(ps[:, 7, 0:D], view["wk1"], view["cen"])
                            one(ps[:, 7, D:D + 1], view["cen"], view["bk1"])
                            one(ps[0:QROWS, 7, D + 1:D + 1 + NG], view["cen"][0:QROWS, 0:QROWS],
                                view["bq1x3"]).then_inc(ev("l1_wkps"), 1)
                        if G == 0 and i == 3:
                            pe.wait_ge(ev("l1_wk"), 1)
                            one(ps[:, 7, 0:NG * QROWS], view["wq1"], view["cen3"]).then_inc(ev("l1_wqps"), 1)
                weighted(G0 + NG - 1, NB - 1)
                gather(G0 + NG - 1)

            def cross_out(w, tag):
                pe.wait_ge(ev(f"{tag}_att"), 1)
                nc.tensor.transpose(ps[:, 6, 0:T], y[:, :], ident[0:T, 0:T]).then_inc(ev(f"{tag}_attps"), 1)
                pe.wait_ge(ev(f"{tag}_attT"), 1)
                one(ps[0:T, 6, 128:256], attT[:, :], w).then_inc(ev(f"{tag}_proj"), 1)

            def causal_mask():
                one(ps[:, 6, :], ident, view["causal"].unsqueeze(1).to_broadcast([P, 8, T]), stop=False)

            def turn_probs(tag, ready, steps=0):
                pe.wait_ge(ev(ready), 1)
                for j in range(8):
                    last = nc.tensor.transpose(ps[0:T, 4 + j // 4, (j % 4) * P:(j % 4 + 1) * P], sa_s[:, j * T:(j + 1) * T], ident)
                    if j % 4 == 3:
                        last.then_inc(ev(f"{tag}_pT"), 1)
                keys_until(steps)
                pe.wait_ge(ev(f"{tag}_pTs"), 2)

            pe.wait_ge(in_pack["first"], 16)
            key_chunk(0, 0, view["wk0"])
            pe.wait_ge(in_pack["const"], 16)
            yT_of("ln0")
            key_chunk(0, 1, view["wk0"])
            pe.wait_ge(in_pack["early"], 16)
            pe.wait_ge(zeroed, 1)
            for g in range(NG):
                last = one(ps[0:QROWS, 6, 256 + g * T:256 + (g + 1) * T], view["wq0x3"][:, g * QROWS:(g + 1) * QROWS], yT[:, :])
            last.then_inc(ev("q0_ps"), 1)
            for c in range(2, KEYS_AHEAD):
                key_chunk(0, c, view["wk0"])
            for c in range(NB):
                if c + KEYS_AHEAD < NB:
                    key_chunk(0, c + KEYS_AHEAD, view["wk0"])
                if c == 0:
                    pe.wait_ge(q_ready, 1)
                    pe.wait_ge(ones_set, 1)
                max_pair(0, c)
                for v in v_schedule(c):
                    v_chunk(0, v, view["wv0"])
            pe.wait_ge(v_set, NB)
            pe.wait_ge(v_ones, 1)
            pe.wait_ge(ones_set, 2)
            cross(0)
            keys_until(DONE["out"])
            cross_out(view["wo0"], "x0")
            keys_until(DONE["ln1"])

            yT_of("ln1")
            pe.wait_ge(in_pack["late"], 16)
            for w, bnk in (("wqa", 4), ("wka", 5)):
                for h in range(SH):
                    last = one(ps[64 * (h % 2):64 * (h % 2) + 64, bnk, (h // 2) * T:(h // 2 + 1) * T],
                               view[w][:, h * SD:(h + 1) * SD], yT[:, :])
            last.then_inc(ev("sa0_q"), 1)
            causal_mask()
            keys_until(DONE["qk"])
            pe.wait_ge(ev("sa0_qk"), 1)
            for j in range(NP_):
                last = one(ps[:, 6, j * T:(j + 1) * T], sa_q[:, j * P:(j + 1) * P], sa_k[:, j * T:(j + 1) * T],
                           start=False)
            last.then_inc(ev("sa0_scores"), 1)
            for k in range(2):
                last = one(ps[0:T, 4 + k, :], yT[:, :], view["wva"][:, k * 512:(k + 1) * 512])
            last.then_inc(ev("sa0_v"), 1)
            keys_until(DONE["v"])
            turn_probs("sa0", "sa0_probs", DONE["probs"])
            pe.wait_ge(ev("sa0_vs"), 1)
            for h in range(SH):
                for u in range(2):
                    q0 = (h // 2) * P + (h % 2) * T
                    last = one(ps[64 * u:64 * u + 64, 6, h * (T // 2):(h + 1) * (T // 2)],
                               sa_v[0:T, h * SD:(h + 1) * SD], sa_pT[0:T, q0 + u:q0 + T:2])
            last.then_inc(ev("sa0_z"), 1)
            keys_until(DONE["z"])
            pe.wait_ge(ev("sa0_zT"), 1)
            zT = sa_k[:].rearrange("p (s r) -> p r s", r=NP_)
            for r in range(NP_):
                last = one(ps[0:T, 7, 0:D], zT[:, r, :], view["proja"][:, r * D:(r + 1) * D],
                           start=(r == 0), stop=(r == NP_ - 1))
            last.then_inc(ev("sa0_proj"), 1)

            keys_until(DONE["ln2"])
            yT_of("ln2")
            one(ps[:, 6, 0:E0 + 1], yT2[:, :], view["router0"]).then_inc(ev("ffn0_logits"), 1)
            hid = ps[:, 4:6, :].rearrange("p a b -> p (a b)")
            for a, b in ((0, 512), (512, SL * F0)):
                for hh in range(2):
                    last = one(hid[64 * hh:64 * hh + 64, a:b], yT[:, :], view["w1"][:, hh * SL * F0 + a:hh * SL * F0 + b])
            last.then_inc(ev("ffn0_hidden"), 1)
            keys_until(DONE["ffn"])
            pe.wait_ge(ev("ffn0_h"), 1)
            nc.tensor.transpose(ps[:, 6, 64:64 + T], f0_h[0:T, (SL - 1) * F0:SL * F0], ident[0:T, 0:T])
            for k in range(SL - 1):
                last = nc.tensor.transpose(ps[:, 7, k * P:(k + 1) * P], f0_h[:, k * F0:(k + 1) * F0], ident)
            last.then_inc(ev("ffn0_hT"), 1)
            keys_until(DONE["h"])
            pe.wait_ge(ev("ffn0_hTs"), 1)
            for e in range(E0 + 1):
                hh, k = e // SL, e % SL
                last = one(ps[0:T, 4, 0:D], f0_hT[:, k * P + hh * T:k * P + hh * T + T],
                           view["w2"][:, e * D:(e + 1) * D] if e < E0 else view["sdown0"], start=(e == 0), stop=(e == E0))
            last.then_inc(ev("ffn0_y"), 1)

            keys_until(STEPS)
            pe.wait_ge(in_pack["small1"], 16)
            pe.wait_ge(k_sq, NB)
            v_chunk(1, 0, view["wv1"])
            v_chunk(1, 1, view["wv1"])
            yT_of("ln3")
            for g in range(NG):
                last = one(ps[0:QROWS, 6, g * T:(g + 1) * T], wq1c[:, g * QROWS:(g + 1) * QROWS], yT[:, :])
            last.then_inc(ev("q1_ps"), 1)
            pe.wait_ge(k_rstd, NB)
            v_chunk(1, 2, view["wv1"])
            pe.wait_ge(ev("q1_sq"), 1)
            one(ps[0:QROWS, 6, 256:256 + NG * T], view["avg"][0:QROWS, 0:QROWS], q_b[0:QROWS, :]).then_inc(ev("q1_var"), 1)
            v_chunk(1, 3, view["wv1"])
            pe.wait_ge(ev("shift_zero"), 1)
            pe.wait_ge(q_ready, 2)
            for c in range(NB):
                max_pair(NG, c)
                for v in range(4 + (NB - 4) * c // NB, 4 + (NB - 4) * (c + 1) // NB):
                    v_chunk(1, v, view["wv1"])
            pe.wait_ge(v_set, 2 * NB)
            cross(1)
            cross_out(view["wp1"], "x1")

            yT_of("ln4")
            pe.wait_ge(in_pack["tail1"], 16)
            one(ps[0:T, 4, 0:2 * D], yT[:, :], view["wqkv1"][:, 0:2 * D]).then_inc(ev("sa1_qkps"), 1)
            one(ps[0:T, 5, 0:D], yT[:, :], view["wqkv1"][:, 2 * D:3 * D]).then_inc(ev("sa1_vps"), 1)
            causal_mask()
            pe.wait_ge(ev("sa1_rope"), 1)
            for k in range(2):
                last = nc.tensor.transpose(ps[:, 7, k * T:(k + 1) * T], s1_r[:, k * D:(k + 1) * D], ident[0:T, 0:T])
            last.then_inc(ev("sa1_qkT"), 1)
            for hh in range(2):
                pe.wait_ge(ev("sa1_qk"), hh + 1)
                last = one(ps[64 * hh:64 * hh + 64, 6, :], attT[:, :], sa_q[:, hh * 512:(hh + 1) * 512], start=False)
            last.then_inc(ev("sa1_scores"), 1)
            turn_probs("sa1", "sa1_exp")
            pe.wait_ge(ev("sa1_vs"), 1)
            for h in range(H):
                hh, j = h // 8, h % 8
                u = 64 * (h % 2)
                last = one(ps[u:u + 64, 7, (h // 2) * AUG:(h // 2 + 1) * AUG], sa_pT[0:T, j * P + hh * T:j * P + hh * T + T],
                           s1_v[:, h, :])
            last.then_inc(ev("sa1_av"), 1)
            pe.wait_ge(ev("sa1_o"), 1)
            nc.tensor.transpose(ps[:, 6, 0:T], y[:, :], ident[0:T, 0:T]).then_inc(ev("sa1_oT"), 1)
            pe.wait_ge(ev("sa1_oTs"), 1)
            one(ps[0:T, 6, 128:256], attT[:, :], view["wproj1"]).then_inc(ev("sa1_proj"), 1)

            yT_of("ln5")
            one(ps[0:T, 6, 0:E1], yT[:, :], view["gate1"]).then_inc(ev("ffn1_logits"), 1)
            pe.wait_ge(ev("top1_index"), 1)
            one(ps[:, 7, 0:T], stat[0:T, 9:10].to_broadcast([T, P]), ident[0:T, 0:T]).then_inc(ev("index_row"), 1)
            for hh in range(2):
                last = one(ps[64 * hh:64 * hh + 64, 5, 0:F1], yT[:, :], view["sgu1"][:, hh * F1:(hh + 1) * F1])
            last.then_inc(ev("ffn1_shared"), 1)
            for s in in_exp:
                pe.wait_ge(s, 16)
            for e in range(E1):
                pe.wait_ge(ev("ffn1_x"), e + 1)
                for hh in range(2):
                    last = one(ps[64 * hh:64 * hh + 64, 4, 0:F1], f1_x[:, e, :], expert(e)[:, hh * F1:(hh + 1) * F1],
                               start=(e == 0), stop=(e == E1 - 1))
            last.then_inc(ev("ffn1_gu"), 1)
            pe.wait_ge(ev("shared_h"), 1)
            for k in range(2):
                last = nc.tensor.transpose(ps[:, 6, P + k * T:P + (k + 1) * T], f1_h[:, 1, k * P:(k + 1) * P], ident[0:T, 0:T])
            last.then_inc(ev("shared_hT"), 1)
            pe.wait_ge(ev("ffn1_h"), 1)
            for k in range(2):
                last = nc.tensor.transpose(ps[:, 7, P + k * T:P + (k + 1) * T], f1_h[:, 0, k * P:(k + 1) * P], ident[0:T, 0:T])
            last.then_inc(ev("ffn1_hT"), 1)
            pe.wait_ge(ev("shared_hTs"), 1)
            for k in range(2):
                one(ps[64 * k:64 * k + 64, 5, 0:D], f1_hT[:, P + k * T:P + (k + 1) * T], view["sdown1"][:, k * D:(k + 1) * D],
                    start=True, stop=False)
            for e in range(E1):
                for c, (a, b) in enumerate(HE_CHUNKS):
                    if a == e:
                        pe.wait_ge(ev("ffn1_he"), c + 1)
                for k in range(2):
                    last = one(ps[64 * k:64 * k + 64, 5, 0:D], f1_he[k][:, e, :],
                               expert(e)[:, 2 * F1 + k * D:2 * F1 + (k + 1) * D], start=False, stop=(e == E1 - 1))
            last.then_inc(ev("ffn1_d"), 1)
            pe.wait_ge(ev("ffn1_ds"), 1)
            one(ps[0:T, 4, 0:D], view["fold"], y2).then_inc(ev("ffn1_out"), 1)


def _constants():
    c = {}
    head = np.arange(P) // DH
    same = (head[:, None] == head[None, :]).astype(np.float32) / DH
    cen = np.eye(P, dtype=np.float32) - same
    c["ident"] = np.eye(P, dtype=np.float32)
    c["avg"] = same
    c["cen"] = cen
    c["cen3"] = np.concatenate([np.tile(cen[:, g * GC:(g + 1) * GC], (1, 3)) for g in range(NG)], axis=1)
    r = np.arange(P) % 32
    c["sel"] = (r[:, None] == np.arange(2 * AUG)[None, :]).astype(np.float32)
    c["fold"] = (np.arange(P)[:, None] % T == np.arange(T)[None, :]).astype(np.float32)
    c["hmask"] = ((np.arange(QROWS)[:, None] % GC) // DH == np.arange(HG)[None, :]).astype(np.float32)
    c["headmask"] = (head[:, None] == np.arange(H)[None, :]).astype(np.float32)
    q, k = np.arange(P)[:, None] % T, np.arange(T)[None, :]
    c["causal"] = np.where(k > q, np.float32(-1e30), np.float32(0)).astype(np.float32)
    c["iota"] = np.tile(np.arange(E1, dtype=np.float32), (P, 1))
    half = DH // 2
    freqs = np.float32(1.0) / np.float32(10000.0) ** (np.arange(half, dtype=np.float32) / np.float32(half))
    angle = np.arange(T, dtype=np.float32)[:, None] * freqs[None, :].astype(np.float32)
    cos, sin = np.cos(angle).astype(np.float32), np.sin(angle).astype(np.float32)
    c["cos"] = np.concatenate([cos, cos], axis=1)
    c["sin"] = np.concatenate([-sin, sin], axis=1)
    return c


def _blocks(w, n):
    return w.reshape(n, P, -1).transpose(1, 0, 2).reshape(P, -1)


def _layout(i):
    a = dict(_constants())
    rep = lambda v: np.broadcast_to(v[None, :], (T, v.shape[0]))
    g3 = lambda w: np.concatenate([np.tile(w[:, g * GC:(g + 1) * GC], (1, 3)) for g in range(NG)], axis=1)
    b3 = lambda b: np.tile(b.reshape(NG, GC).T, (3, 1))
    a["wk0"], a["wv0"], a["wo0"] = i["L0_xattn_Wk"], i["L0_xattn_Wv"], i["L0_xattn_Wo"]
    a["wq0x3"], a["bq0x3"] = g3(i["L0_xattn_Wq"]), b3(i["L0_xattn_bq"])
    a["bk0"] = i["L0_xattn_bk"].reshape(P, 1)
    for n, m in (("wqa", "Wq"), ("wka", "Wk"), ("wva", "Wv")):
        a[n] = i["L0_attn_" + m].reshape(SH * SD, D).T
    for n, m in (("bqa", "bq"), ("bka", "bk")):
        a[n] = i["L0_attn_" + m].reshape(NP_, P).T
    a["bva"] = np.tile(i["L0_attn_bv"].T, (2, 1))
    a["proja"] = _blocks(i["L0_attn_proj"], NP_)
    a["w1"] = np.concatenate([i["L0_ffn_w1"].transpose(1, 0, 2).reshape(P, -1), i["L0_ffn_shared_gate_up"]], axis=1)
    a["w2"] = i["L0_ffn_w2"].transpose(1, 0, 2).reshape(P, -1)
    a["sdown0"] = i["L0_ffn_shared_down"]
    a["router0"] = np.concatenate([i["L0_ffn_router_w"], i["L0_ffn_shared_gate_w"]], axis=1)
    a["x"] = i["x"][0]
    for n, m in (("bv0", "L0_xattn_bv"), ("bo0", "L0_xattn_bo"), ("bv1", "L1_xattn_bv"), ("bp1", "L1_xattn_bp"),
                 ("bproj1", "L1_attn_proj_b"), ("bqkv1", "L1_attn_qkv_b")):
        a[n] = rep(i[m])
    a["wv1"], a["wp1"] = i["L1_xattn_Wv"].T, i["L1_xattn_Wp"].T
    a["wk1"], a["wq1"] = i["L1_xattn_Wk"], i["L1_xattn_Wq"]
    a["bk1"], a["bq1x3"] = i["L1_xattn_bk"].reshape(P, 1), b3(i["L1_xattn_bq"])
    gb = np.stack([np.tile(i["L1_xattn_q_gamma"], H), np.tile(i["L1_xattn_q_beta"], H)], axis=1)
    a["qgb"] = gb[:QROWS]
    a["kgb"] = np.stack([np.tile(i["L1_xattn_k_gamma"], H), np.tile(i["L1_xattn_k_beta"], H)], axis=1)
    a["wproj1"], a["wqkv1"] = i["L1_attn_proj_w"].T, i["L1_attn_qkv_w"].T
    a["gate1"] = i["L1_ffn_gate_w"]
    a["sgu1"] = np.concatenate([i["L1_ffn_shared_gate_w"], i["L1_ffn_shared_up_w"]], axis=1)
    a["sdown1"] = _blocks(i["L1_ffn_shared_down_w"], 2)
    packs = {}
    for pack, items in PACKS.items():
        out = np.zeros((P, words(pack)), np.float32)
        at = 0
        for name, r, w in items:
            out[0:r, at:at + w] = a[name]
            at += w
        packs[pack] = out
    gate = i["L1_ffn_routed_gate_w"].transpose(1, 0, 2)
    up = i["L1_ffn_routed_up_w"].transpose(1, 0, 2)
    down = i["L1_ffn_routed_down_w"].reshape(E1, 2, P, D).transpose(2, 0, 1, 3).reshape(P, E1, 2 * D)
    experts = np.concatenate([gate, up, down], axis=2).reshape(P, E1 * EW)
    return np.ascontiguousarray(i["ctx_1024"][0].T), packs, np.ascontiguousarray(experts)


def kernel(**inputs):
    import concourse.bacc as _bacc
    from concourse.bass_utils import run_bass_kernel_spmd as _run

    i = {k: np.asarray(v) for k, v in inputs.items()}
    ctxT, packs, experts = _layout(i)
    arrays = {"in_ctxT": ctxT, "in_experts": experts, **{"in_" + n: a for n, a in packs.items()}}
    nc = _bacc.Bacc("TRN2", target_bir_lowering=False, num_devices=1)
    aps = {n: nc.dram_tensor(n, a.shape, mybir.dt.from_np(a.dtype), kind="ExternalInput").ap() for n, a in arrays.items()}
    out = nc.dram_tensor("out", (T, D), F32, kind="ExternalOutput").ap()
    perceiver(nc, aps["in_ctxT"], {n: aps["in_" + n] for n in packs}, aps["in_experts"], out)
    r = _run(nc, [arrays], core_ids=[0])
    return r.results[0]["out"].reshape(1, T, D)
```
